# Optimizing a Trainium2 kernel written in Bass

```python
import numpy as np
import jax
import jax.numpy as jnp

def _softmax(x, axis=-1):
    return jax.nn.softmax(x, axis=axis)

def _gelu(x):
    return jax.nn.gelu(x, approximate=True)

def _silu(x):
    return jax.nn.silu(x)

def _sigmoid(x):
    return jax.nn.sigmoid(x)

def _layernorm(x, axis=-1, eps=1e-05):
    m = jnp.mean(x, axis=axis, keepdims=True)
    v = jnp.var(x, axis=axis, keepdims=True)
    return (x - m) / jnp.sqrt(v + eps)

def _scatter_add(tgt, idx, src, axis=0):
    return tgt.at[idx].add(src)

def _segment_sum(src, seg, n):
    return jax.ops.segment_sum(src, seg, n)
kernel_name = 'mk_macaron_d4_jaxref_r8_b53e3b'

def setup_inputs(seed: int=0):
    np.random.seed(seed)
    _w = jnp.asarray

    def _L0_attn_setup():
        import jax, jax.numpy as jnp
        import numpy as np
        D_MODEL = 128
        N_HEADS = 16
        D_HEAD = D_MODEL // N_HEADS
        B, T = (2, 256)
        EPS = 1e-05
        key = jax.random.key(seed)
        ks = jax.random.split(key, 5)
        s = 1.0 / np.sqrt(D_MODEL)
        return {'x': jax.random.normal(ks[0], (B, T, D_MODEL), dtype=jnp.float32), 'W_q': jax.random.normal(ks[1], (D_MODEL, D_MODEL), dtype=jnp.float32) * s, 'W_k': jax.random.normal(ks[2], (D_MODEL, D_MODEL), dtype=jnp.float32) * s, 'W_v': jax.random.normal(ks[3], (D_MODEL, D_MODEL), dtype=jnp.float32) * s, 'W_o': jax.random.normal(ks[4], (D_MODEL, D_MODEL), dtype=jnp.float32) * s, 'gn_weight': jnp.ones((D_MODEL,), dtype=jnp.float32), 'gn_bias': jnp.zeros((D_MODEL,), dtype=jnp.float32)}
    _L0_attn_in = _L0_attn_setup()

    def _L0_ffn_setup():
        import jax, jax.numpy as jnp
        import numpy as np
        HIDDEN = 128
        INTER = 512
        key = jax.random.key(seed)
        k1, k2, k3, k4, k5 = jax.random.split(key, 5)
        hidden_states = jax.random.normal(k1, (4, 256, HIDDEN), dtype=jnp.float32)
        W1 = jax.random.normal(k2, (HIDDEN, INTER), dtype=jnp.float32) * (1.0 / np.sqrt(HIDDEN))
        b1 = jax.random.normal(k3, (INTER,), dtype=jnp.float32) * 0.02
        W2 = jax.random.normal(k4, (INTER, HIDDEN), dtype=jnp.float32) * (1.0 / np.sqrt(INTER))
        b2 = jax.random.normal(k5, (HIDDEN,), dtype=jnp.float32) * 0.02
        return {'hidden_states': hidden_states, 'W1': W1, 'b1': b1, 'W2': W2, 'b2': b2}
    _L0_ffn_in = _L0_ffn_setup()

    def _L1_attn_setup():
        import math
        import jax, jax.numpy as jnp
        import numpy as np
        D_MODEL = 128
        N_HEADS = 16
        HEAD_DIM = D_MODEL // N_HEADS
        WINDOW = 128
        BATCH = 2
        SEQ = 256

        def _alibi_slopes(n_heads):
            start = 2 ** (-2 ** (-(math.log2(n_heads) - 3)))
            return jnp.asarray([start * start ** i for i in range(n_heads)], dtype=jnp.float32)
        key = jax.random.key(seed)
        ks = jax.random.split(key, 5)
        scale = 0.02
        return {'x': jax.random.normal(ks[0], (BATCH, SEQ, D_MODEL), dtype=jnp.float32), 'wq': jax.random.normal(ks[1], (D_MODEL, D_MODEL), dtype=jnp.float32) * scale, 'bq': jnp.zeros((D_MODEL,), dtype=jnp.float32), 'wk': jax.random.normal(ks[2], (D_MODEL, D_MODEL), dtype=jnp.float32) * scale, 'bk': jnp.zeros((D_MODEL,), dtype=jnp.float32), 'wv': jax.random.normal(ks[3], (D_MODEL, D_MODEL), dtype=jnp.float32) * scale, 'bv': jnp.zeros((D_MODEL,), dtype=jnp.float32), 'wo': jax.random.normal(ks[4], (D_MODEL, D_MODEL), dtype=jnp.float32) * scale, 'bo': jnp.zeros((D_MODEL,), dtype=jnp.float32)}
    _L1_attn_in = _L1_attn_setup()

    def _L1_ffn_setup():
        import jax, jax.numpy as jnp
        import numpy as np
        D_MODEL = 128
        HIDDEN = 512
        N_EXPERTS = 8
        TOP_K = 2
        key = jax.random.key(seed)
        k_x, k_g, k_u, k_d, k_r = jax.random.split(key, 5)
        std = 0.02
        return {'x': jax.random.normal(k_x, (2, 256, D_MODEL), dtype=jnp.float32), 'Wg': jax.random.normal(k_g, (N_EXPERTS, D_MODEL, HIDDEN), dtype=jnp.float32) * std, 'Wu': jax.random.normal(k_u, (N_EXPERTS, D_MODEL, HIDDEN), dtype=jnp.float32) * std, 'Wd': jax.random.normal(k_d, (N_EXPERTS, HIDDEN, D_MODEL), dtype=jnp.float32) * std, 'Wr': jax.random.normal(k_r, (D_MODEL, N_EXPERTS), dtype=jnp.float32) * std}
    _L1_ffn_in = _L1_ffn_setup()

    def _L2_attn_setup():
        import jax, jax.numpy as jnp
        import numpy as np
        B, S, DM, H, DH = (2, 256, 128, 16, 64)
        HID = H * DH

        def _xavier(key, shape):
            fan_out, fan_in = shape
            lim = float(np.sqrt(6.0 / (fan_in + fan_out)))
            return jax.random.uniform(key, shape, jnp.float32, -lim, lim)

        def _gla_scan(q, k, v, g):
            qt = jnp.moveaxis(q, 1, 0)
            kt = jnp.moveaxis(k, 1, 0)
            vt = jnp.moveaxis(v, 1, 0)
            gt = jnp.moveaxis(g, 1, 0)

            def step(s, inp):
                qi, ki, vi, gi = inp
                s = jnp.exp(gi)[:, :, None, None] * s + ki[..., :, None] * vi[..., None, :]
                o = jnp.einsum('bhk,bhkv->bhv', qi, s)
                return (s, o)
            s0 = jnp.zeros(q.shape[0:1] + q.shape[2:] + q.shape[-1:], q.dtype)
            _, o = jax.lax.scan(step, s0, (qt, kt, vt, gt))
            return jnp.moveaxis(o, 0, 1)
        key = jax.random.key(seed)
        ks = jax.random.split(key, 8)
        return {'x': jax.random.normal(ks[0], (B, S, DM), jnp.float32), 'Wq': _xavier(ks[1], (HID, DM)), 'Wk': _xavier(ks[2], (HID, DM)), 'Wv': _xavier(ks[3], (HID, DM)), 'Wo': _xavier(ks[4], (DM, HID)), 'Wg': _xavier(ks[5], (HID, DM)), 'Wog': _xavier(ks[6], (HID, DM)), 'Wd': _xavier(ks[7], (H, DM)), 'bd': jnp.full((H,), -2.0, jnp.float32), 'norm_w': jnp.ones((HID,), jnp.float32)}
    _L2_attn_in = _L2_attn_setup()

    def _L2_ffn_setup():
        import jax, jax.numpy as jnp
        import numpy as np
        TOP_K = 2
        key = jax.random.key(seed)
        k1, k2, k3, k4, k5 = jax.random.split(key, 5)
        B, S, D, F, E = (2, 128, 128, 256, 8)
        return {'x': jax.random.normal(k1, (B, S, D), dtype=jnp.float32), 'router_kernel_DE': jax.random.normal(k2, (D, E), dtype=jnp.float32) * 0.02, 'kernel_gating_EDF': jax.random.normal(k3, (E, D, F), dtype=jnp.float32) * 0.02, 'kernel_up_EDF': jax.random.normal(k4, (E, D, F), dtype=jnp.float32) * 0.02, 'kernel_down_EFD': jax.random.normal(k5, (E, F, D), dtype=jnp.float32) * 0.02}
    _L2_ffn_in = _L2_ffn_setup()

    def _L3_attn_setup():
        import jax, jax.numpy as jnp
        import numpy as np
        import math
        DIM = 128
        H = 16
        D = 64
        M = 64
        B = 1
        N = 256

        def _orf_omega(key):
            blocks = []
            n_blocks = (M + D - 1) // D
            for i in range(n_blocks):
                G = jax.random.normal(jax.random.fold_in(key, i), (D, D), dtype=jnp.float32)
                Q, _ = jnp.linalg.qr(G)
                blocks.append(Q.T)
            return jnp.concatenate(blocks, axis=0)[:M]

        def _phi(x, omega):
            proj = jnp.einsum('bhnd,md->bhnm', x, omega)
            norm = 0.5 * jnp.sum(x * x, axis=-1, keepdims=True)
            return jnp.exp(proj - norm) / math.sqrt(M)

        def _heads(t):
            b, n, _ = t.shape
            return t.reshape(b, n, H, D).transpose(0, 2, 1, 3)
        key = jax.random.key(seed)
        ks = jax.random.split(key, 7)
        inner = H * D
        x = jax.random.normal(ks[0], (B, N, DIM), dtype=jnp.float32)
        omega = _orf_omega(ks[1])
        wq = jax.random.normal(ks[2], (inner, DIM), dtype=jnp.float32) * 0.02
        wk = jax.random.normal(ks[3], (inner, DIM), dtype=jnp.float32) * 0.02
        wv = jax.random.normal(ks[4], (inner, DIM), dtype=jnp.float32) * 0.02
        wo = jax.random.normal(ks[5], (DIM, inner), dtype=jnp.float32) * 0.02
        bo = jnp.zeros((DIM,), dtype=jnp.float32)
        return {'x': x, 'omega': omega, 'wq': wq, 'wk': wk, 'wv': wv, 'wo': wo, 'bo': bo}
    _L3_attn_in = _L3_attn_setup()

    def _L3_ffn_setup():
        import jax, jax.numpy as jnp
        import numpy as np
        NUM_EXPERTS = 8
        EXPERT_CAPACITY = 2.0
        DIM = 128
        HIDDEN_DIM = 512
        key = jax.random.key(seed)
        k_x, k_g, k_w1, k_w2 = jax.random.split(key, 4)
        n, t, d, f, e = (8, 128, DIM, HIDDEN_DIM, NUM_EXPERTS)
        x = jax.random.normal(k_x, (n, t, d), dtype=jnp.float32)
        gate_w = jax.random.normal(k_g, (e, d), dtype=jnp.float32) * 0.02
        w1 = jax.random.normal(k_w1, (e, d, f), dtype=jnp.float32) * 0.02
        w2 = jax.random.normal(k_w2, (e, f, d), dtype=jnp.float32) * 0.02
        return {'x': x, 'gate_w': gate_w, 'w1': w1, 'w2': w2}
    _L3_ffn_in = _L3_ffn_setup()
    _d = {'L0_attn_x': _L0_attn_in['x'], 'L0_attn_W_q': _L0_attn_in['W_q'], 'L0_attn_W_k': _L0_attn_in['W_k'], 'L0_attn_W_v': _L0_attn_in['W_v'], 'L0_attn_W_o': _L0_attn_in['W_o'], 'L0_attn_gn_weight': _L0_attn_in['gn_weight'], 'L0_attn_gn_bias': _L0_attn_in['gn_bias'], 'L0_ffn_W1': _L0_ffn_in['W1'], 'L0_ffn_b1': _L0_ffn_in['b1'], 'L0_ffn_W2': _L0_ffn_in['W2'], 'L0_ffn_b2': _L0_ffn_in['b2'], 'L1_attn_wq': _L1_attn_in['wq'], 'L1_attn_bq': _L1_attn_in['bq'], 'L1_attn_wk': _L1_attn_in['wk'], 'L1_attn_bk': _L1_attn_in['bk'], 'L1_attn_wv': _L1_attn_in['wv'], 'L1_attn_bv': _L1_attn_in['bv'], 'L1_attn_wo': _L1_attn_in['wo'], 'L1_attn_bo': _L1_attn_in['bo'], 'L1_ffn_Wg': _L1_ffn_in['Wg'], 'L1_ffn_Wu': _L1_ffn_in['Wu'], 'L1_ffn_Wd': _L1_ffn_in['Wd'], 'L1_ffn_Wr': _L1_ffn_in['Wr'], 'L2_attn_Wq': _L2_attn_in['Wq'], 'L2_attn_Wk': _L2_attn_in['Wk'], 'L2_attn_Wv': _L2_attn_in['Wv'], 'L2_attn_Wo': _L2_attn_in['Wo'], 'L2_attn_Wg': _L2_attn_in['Wg'], 'L2_attn_Wog': _L2_attn_in['Wog'], 'L2_attn_Wd': _L2_attn_in['Wd'], 'L2_attn_bd': _L2_attn_in['bd'], 'L2_attn_norm_w': _L2_attn_in['norm_w'], 'L2_ffn_router_kernel_DE': _L2_ffn_in['router_kernel_DE'], 'L2_ffn_kernel_gating_EDF': _L2_ffn_in['kernel_gating_EDF'], 'L2_ffn_kernel_up_EDF': _L2_ffn_in['kernel_up_EDF'], 'L2_ffn_kernel_down_EFD': _L2_ffn_in['kernel_down_EFD'], 'L3_attn_omega': _L3_attn_in['omega'], 'L3_attn_wq': _L3_attn_in['wq'], 'L3_attn_wk': _L3_attn_in['wk'], 'L3_attn_wv': _L3_attn_in['wv'], 'L3_attn_wo': _L3_attn_in['wo'], 'L3_attn_bo': _L3_attn_in['bo'], 'L3_ffn_gate_w': _L3_ffn_in['gate_w'], 'L3_ffn_w1': _L3_ffn_in['w1'], 'L3_ffn_w2': _L3_ffn_in['w2']}
    _x0 = _d['L0_attn_x']
    _d['L0_attn_x'] = jax.random.normal(jax.random.fold_in(jax.random.key(seed), 1), (2, 1024, 128), dtype=_x0.dtype)
    del _x0
    return _d

def reference(L0_attn_x, L0_attn_W_q, L0_attn_W_k, L0_attn_W_v, L0_attn_W_o, L0_attn_gn_weight, L0_attn_gn_bias, L0_ffn_W1, L0_ffn_b1, L0_ffn_W2, L0_ffn_b2, L1_attn_wq, L1_attn_bq, L1_attn_wk, L1_attn_bk, L1_attn_wv, L1_attn_bv, L1_attn_wo, L1_attn_bo, L1_ffn_Wg, L1_ffn_Wu, L1_ffn_Wd, L1_ffn_Wr, L2_attn_Wq, L2_attn_Wk, L2_attn_Wv, L2_attn_Wo, L2_attn_Wg, L2_attn_Wog, L2_attn_Wd, L2_attn_bd, L2_attn_norm_w, L2_ffn_router_kernel_DE, L2_ffn_kernel_gating_EDF, L2_ffn_kernel_up_EDF, L2_ffn_kernel_down_EFD, L3_attn_omega, L3_attn_wq, L3_attn_wk, L3_attn_wv, L3_attn_wo, L3_attn_bo, L3_ffn_gate_w, L3_ffn_w1, L3_ffn_w2):

    def _L0_attn_ref(x, W_q, W_k, W_v, W_o, gn_weight, gn_bias):
        import jax, jax.numpy as jnp
        import numpy as np
        D_MODEL = 128
        N_HEADS = 16
        D_HEAD = D_MODEL // N_HEADS
        B, T = (2, 256)
        EPS = 1e-05
        b, t, dm = x.shape
        h, dh = (N_HEADS, D_HEAD)
        gammas = 1.0 - 2.0 ** (-5.0 - jnp.arange(h, dtype=jnp.float32))
        q = (x @ W_q.T).reshape(b, t, h, dh)
        k = (x @ W_k.T).reshape(b, t, h, dh)
        v = (x @ W_v.T).reshape(b, t, h, dh)
        idx = jnp.arange(t)
        diff = idx[:, None] - idx[None, :]
        pow_ = jnp.maximum(diff, 0).astype(jnp.float32)
        decay = jnp.where(diff >= 0, gammas[:, None, None] ** pow_, 0.0)
        scale = jnp.sqrt(jnp.float32(dh))
        attn = jnp.einsum('bihd,bjhd->bhij', q, k) * decay[None] / scale
        y = jnp.einsum('bhij,bjhd->bihd', attn, v)
        mean = y.mean(axis=(1, 3), keepdims=True)
        var = y.var(axis=(1, 3), keepdims=True)
        yn = (y - mean) / jnp.sqrt(var + EPS)
        yn = yn.reshape(b, t, dm) * gn_weight + gn_bias
        return yn @ W_o.T

    def _L0_ffn_ref(hidden_states, W1, b1, W2, b2):
        import jax, jax.numpy as jnp
        import numpy as np
        HIDDEN = 128
        INTER = 512
        h = jax.nn.relu(jnp.einsum('bsh,hi->bsi', hidden_states, W1) + b1)
        return jnp.einsum('bsi,ih->bsh', h, W2) + b2

    def _L1_attn_ref(x, wq, bq, wk, bk, wv, bv, wo, bo):
        import math
        import jax, jax.numpy as jnp
        import numpy as np
        D_MODEL = 128
        N_HEADS = 16
        HEAD_DIM = D_MODEL // N_HEADS
        WINDOW = 128
        BATCH = 2
        SEQ = 256

        def _alibi_slopes(n_heads):
            start = 2 ** (-2 ** (-(math.log2(n_heads) - 3)))
            return jnp.asarray([start * start ** i for i in range(n_heads)], dtype=jnp.float32)
        B, S, _ = x.shape
        q = (x @ wq.T + bq).reshape(B, S, N_HEADS, HEAD_DIM).transpose(0, 2, 1, 3)
        k = (x @ wk.T + bk).reshape(B, S, N_HEADS, HEAD_DIM).transpose(0, 2, 1, 3)
        v = (x @ wv.T + bv).reshape(B, S, N_HEADS, HEAD_DIM).transpose(0, 2, 1, 3)
        scores = jnp.einsum('bhqd,bhkd->bhqk', q, k) / math.sqrt(HEAD_DIM)
        pos = jnp.arange(S)
        slopes = _alibi_slopes(N_HEADS)
        pos_diff = -jnp.abs(pos[None, :] - pos[:, None]).astype(scores.dtype)
        scores = scores + pos_diff[None, None, :, :] * slopes[None, :, None, None]
        row = pos[:, None]
        col = pos[None, :]
        mask = (col > row) | (col <= row - WINDOW)
        neg = jnp.finfo(scores.dtype).min
        scores = jnp.where(mask[None, None, :, :], neg, scores)
        probs = jax.nn.softmax(scores, axis=-1)
        out = jnp.einsum('bhqk,bhkd->bhqd', probs, v)
        out = out.transpose(0, 2, 1, 3).reshape(B, S, D_MODEL)
        return out @ wo.T + bo

    def _L1_ffn_ref(x, Wg, Wu, Wd, Wr):
        import jax, jax.numpy as jnp
        import numpy as np
        D_MODEL = 128
        HIDDEN = 512
        N_EXPERTS = 8
        TOP_K = 2
        bsz, seq_len, dim = x.shape
        flat = x.reshape(bsz * seq_len, dim)
        router_probs = jax.nn.softmax(flat @ Wr, axis=-1)
        topk_vals, topk_idx = jax.lax.top_k(router_probs, TOP_K)
        topk_vals = topk_vals / jnp.sum(topk_vals, axis=-1, keepdims=True)
        combine = jnp.sum(jax.nn.one_hot(topk_idx, N_EXPERTS, dtype=flat.dtype) * topk_vals[..., None], axis=1)
        output = jnp.zeros_like(flat)
        for e in range(N_EXPERTS):
            gated = jax.nn.silu(flat @ Wg[e]) * (flat @ Wu[e])
            output = output + combine[:, e:e + 1] * (gated @ Wd[e])
        return output.reshape(bsz, seq_len, dim)

    def _L2_attn_ref(x, Wq, Wk, Wv, Wo, Wg, Wog, Wd, bd, norm_w):
        import jax, jax.numpy as jnp
        import numpy as np
        B, S, DM, H, DH = (2, 256, 128, 16, 64)
        HID = H * DH

        def _xavier(key, shape):
            fan_out, fan_in = shape
            lim = float(np.sqrt(6.0 / (fan_in + fan_out)))
            return jax.random.uniform(key, shape, jnp.float32, -lim, lim)

        def _gla_scan(q, k, v, g):
            qt = jnp.moveaxis(q, 1, 0)
            kt = jnp.moveaxis(k, 1, 0)
            vt = jnp.moveaxis(v, 1, 0)
            gt = jnp.moveaxis(g, 1, 0)

            def step(s, inp):
                qi, ki, vi, gi = inp
                s = jnp.exp(gi)[:, :, None, None] * s + ki[..., :, None] * vi[..., None, :]
                o = jnp.einsum('bhk,bhkv->bhv', qi, s)
                return (s, o)
            s0 = jnp.zeros(q.shape[0:1] + q.shape[2:] + q.shape[-1:], q.dtype)
            _, o = jax.lax.scan(step, s0, (qt, kt, vt, gt))
            return jnp.moveaxis(o, 0, 1)
        b, s, _ = x.shape
        q = (x @ Wq.T).reshape(b, s, H, DH)
        k = (x @ Wk.T).reshape(b, s, H, DH)
        v = (x @ Wv.T).reshape(b, s, H, DH)
        log_decay = -jax.nn.softplus(x @ Wd.T + bd)
        gate = jax.nn.sigmoid((x @ Wg.T).reshape(b, s, H, DH))
        k_gated = k * gate
        out = _gla_scan(q, k_gated, v, log_decay)
        out = out.reshape(b, s, HID)
        eps = jnp.finfo(out.dtype).eps
        out = out * jax.lax.rsqrt(jnp.mean(out * out, -1, keepdims=True) + eps) * norm_w
        out = out * jax.nn.sigmoid(x @ Wog.T)
        return out @ Wo.T

    def _L2_ffn_ref(x, router_kernel_DE, kernel_gating_EDF, kernel_up_EDF, kernel_down_EFD):
        import jax, jax.numpy as jnp
        import numpy as np
        TOP_K = 2
        E = router_kernel_DE.shape[-1]
        x = x.astype(jnp.float32)
        logits_BSE = jnp.einsum('BSD,DE->BSE', x, router_kernel_DE)
        probs_BSE = jax.nn.softmax(logits_BSE.astype(jnp.float32), axis=-1)
        weights_BSK, indices_BSK = jax.lax.top_k(probs_BSE, TOP_K)
        norm_weights_BSK = jax.nn.softmax(weights_BSK, axis=-1)
        one_hot_BSKE = jax.nn.one_hot(indices_BSK, num_classes=E, dtype=x.dtype)
        full_weights_BSE = jnp.sum(one_hot_BSKE * norm_weights_BSK[..., None], axis=2)
        gating_BSEF = jnp.einsum('BSD,EDF->BSEF', x, kernel_gating_EDF)
        act_BSEF = jax.nn.silu(gating_BSEF)
        up_BSEF = jnp.einsum('BSD,EDF->BSEF', x, kernel_up_EDF)
        fuse_BSEF = act_BSEF * up_BSEF
        down_BSED = jnp.einsum('BSEF,EFD->BSED', fuse_BSEF, kernel_down_EFD)
        out_BSD = jnp.einsum('BSED,BSE->BSD', down_BSED, full_weights_BSE)
        return out_BSD.astype(jnp.float32)

    def _L3_attn_ref(x, omega, wq, wk, wv, wo, bo):
        import jax, jax.numpy as jnp
        import numpy as np
        import math
        DIM = 128
        H = 16
        D = 64
        M = 64
        B = 1
        N = 256

        def _orf_omega(key):
            blocks = []
            n_blocks = (M + D - 1) // D
            for i in range(n_blocks):
                G = jax.random.normal(jax.random.fold_in(key, i), (D, D), dtype=jnp.float32)
                Q, _ = jnp.linalg.qr(G)
                blocks.append(Q.T)
            return jnp.concatenate(blocks, axis=0)[:M]

        def _phi(x, omega):
            proj = jnp.einsum('bhnd,md->bhnm', x, omega)
            norm = 0.5 * jnp.sum(x * x, axis=-1, keepdims=True)
            return jnp.exp(proj - norm) / math.sqrt(M)

        def _heads(t):
            b, n, _ = t.shape
            return t.reshape(b, n, H, D).transpose(0, 2, 1, 3)
        b, n, _ = x.shape
        q = _heads(x @ wq.T)
        k = _heads(x @ wk.T)
        v = _heads(x @ wv.T)
        phi_q = _phi(q, omega)
        phi_k = _phi(k, omega)
        kv = jnp.einsum('bhnm,bhnd->bhnmd', phi_k, v)
        kv_cumsum = jnp.cumsum(kv, axis=2)
        k_cumsum = jnp.cumsum(phi_k, axis=2)
        out = jnp.einsum('bhnm,bhnmd->bhnd', phi_q, kv_cumsum)
        z = 1.0 / (jnp.einsum('bhnm,bhnm->bhn', phi_q, k_cumsum) + 1e-06)
        out = out * z[..., None]
        out = out.transpose(0, 2, 1, 3).reshape(b, n, H * D)
        return out @ wo.T + bo

    def _L3_ffn_ref(x, gate_w, w1, w2):
        import jax, jax.numpy as jnp
        import numpy as np
        NUM_EXPERTS = 8
        EXPERT_CAPACITY = 2.0
        DIM = 128
        HIDDEN_DIM = 512
        n, t, d = x.shape
        e = gate_w.shape[0]
        k = int(EXPERT_CAPACITY * t / e)
        scores = jnp.einsum('ntd,ed->nte', x, gate_w)
        probs = jax.nn.softmax(scores, axis=-1)
        g, m = jax.lax.top_k(probs.transpose(0, 2, 1), k)
        batch_idx = jnp.arange(n)[:, None, None]
        xin = x[batch_idx, m]
        h = jnp.einsum('nekd,edf->nekf', xin, w1)
        h = jax.nn.gelu(h, approximate=False)
        h = jnp.einsum('nekf,efd->nekd', h, w2)
        out_tok = g[..., None] * h
        out = jnp.zeros((n, t, d), dtype=x.dtype).at[batch_idx, m].add(out_tok)
        return out
    x = L0_attn_x
    x = x + 0.5 * _L0_ffn_ref(_layernorm(x, axis=-1), L0_ffn_W1, L0_ffn_b1, L0_ffn_W2, L0_ffn_b2)
    x = x + _L0_attn_ref(_layernorm(x, axis=-1), L0_attn_W_q, L0_attn_W_k, L0_attn_W_v, L0_attn_W_o, L0_attn_gn_weight, L0_attn_gn_bias)
    x = x + 0.5 * _L0_ffn_ref(_layernorm(x, axis=-1), L0_ffn_W1, L0_ffn_b1, L0_ffn_W2, L0_ffn_b2)
    x = x + 0.5 * _L1_ffn_ref(_layernorm(x, axis=-1), L1_ffn_Wg, L1_ffn_Wu, L1_ffn_Wd, L1_ffn_Wr)
    x = x + _L1_attn_ref(_layernorm(x, axis=-1), L1_attn_wq, L1_attn_bq, L1_attn_wk, L1_attn_bk, L1_attn_wv, L1_attn_bv, L1_attn_wo, L1_attn_bo)
    x = x + 0.5 * _L1_ffn_ref(_layernorm(x, axis=-1), L1_ffn_Wg, L1_ffn_Wu, L1_ffn_Wd, L1_ffn_Wr)
    x = x + 0.5 * _L2_ffn_ref(_layernorm(x, axis=-1), L2_ffn_router_kernel_DE, L2_ffn_kernel_gating_EDF, L2_ffn_kernel_up_EDF, L2_ffn_kernel_down_EFD)
    x = x + _L2_attn_ref(_layernorm(x, axis=-1), L2_attn_Wq, L2_attn_Wk, L2_attn_Wv, L2_attn_Wo, L2_attn_Wg, L2_attn_Wog, L2_attn_Wd, L2_attn_bd, L2_attn_norm_w)
    x = x + 0.5 * _L2_ffn_ref(_layernorm(x, axis=-1), L2_ffn_router_kernel_DE, L2_ffn_kernel_gating_EDF, L2_ffn_kernel_up_EDF, L2_ffn_kernel_down_EFD)
    x = x + 0.5 * _L3_ffn_ref(_layernorm(x, axis=-1), L3_ffn_gate_w, L3_ffn_w1, L3_ffn_w2)
    x = x + _L3_attn_ref(_layernorm(x, axis=-1), L3_attn_omega, L3_attn_wq, L3_attn_wk, L3_attn_wv, L3_attn_wo, L3_attn_bo)
    x = x + 0.5 * _L3_ffn_ref(_layernorm(x, axis=-1), L3_ffn_gate_w, L3_ffn_w1, L3_ffn_w2)
    return x

_drawn_inputs = setup_inputs


def setup_inputs(seed=0):
    import zlib

    import numpy as np

    out = dict(_drawn_inputs(seed))
    spreads = {'L0_attn_gn_weight': (1.0, 0.2),
     'L0_attn_gn_bias': (0.0, 0.1),
     'L1_attn_bq': (0.0, 0.8),
     'L1_attn_bk': (0.0, 2.0),
     'L1_attn_bv': (0.0, 0.415),
     'L1_attn_bo': (0.0, 0.1),
     'L2_attn_bd': (-2.0, 0.2),
     'L2_attn_norm_w': (1.0, 0.2),
     'L3_attn_bo': (0.0, 0.487)}
    factors = {'L0_ffn_b1': 3.6,
     'L1_attn_wq': 8.0,
     'L1_attn_wk': 8.0,
     'L1_attn_wv': 3.147,
     'L1_ffn_Wg': 8.0,
     'L1_ffn_Wu': 8.0,
     'L1_ffn_Wd': 8.0,
     'L1_ffn_Wr': 8.0,
     'L2_ffn_router_kernel_DE': 8.0,
     'L2_ffn_kernel_gating_EDF': 8.0,
     'L2_ffn_kernel_up_EDF': 8.0,
     'L2_ffn_kernel_down_EFD': 8.0,
     'L3_attn_omega': 8.0,
     'L3_attn_wq': 8.0,
     'L3_attn_wk': 8.0,
     'L3_ffn_gate_w': 8.0,
     'L3_ffn_w1': 8.0,
     'L3_ffn_w2': 8.0}
    for name, (base, spread) in spreads.items():
        noise = np.random.default_rng([zlib.crc32(name.encode()), seed]).standard_normal(out[name].shape)
        drawn = base * np.exp(spread * noise) if base else spread * noise
        out[name] = jnp.asarray(drawn.astype(out[name].dtype))
    for name, factor in factors.items():
        out[name] = (out[name] * factor).astype(out[name].dtype)
    return out
```

```python
from contextlib import ExitStack

import concourse.bass as bass
from concourse import mybir
from concourse.alu_op_type import AluOpType as ALU

ACT = mybir.ActivationFunctionType
F32 = mybir.dt.float32
I32 = mybir.dt.int32
F32R = mybir.dt.float32r
AX_X = mybir.AxisListType.X

P = 128
B, T, D = 2, 1024, 128
TOK = B * T
TILES = TOK // P
PER_B = T // P
GROUP = 512
GROUPS = TOK // GROUP
E = 8
H = 16
EPS = 1e-5
SEMAPHORES = 150
STAGE_SEMAPHORES = 48


class Chip:

    def __init__(self, nc, dram, out, ctx):
        self.nc, self.dram, self.out, self.ctx = nc, dram, out, ctx
        self.used_semaphores = []
        sb = self.sb
        self.x = sb("x_residual", [P, TILES, D])
        self.xnT = sb("xn_features", [P, TOK])
        self.yT = sb("y_features", [P, TOK])
        self.ident = sb("ident", [P, P])
        self.psum = ctx.enter_context(nc.psum_tensor("banks", [P, 8, GROUP], F32))
        self.weights_by_expert = nc.dram_tensor("weights_by_expert", (B * E, T), F32).ap()

    def sb(self, name, shape, dtype=F32):
        return self.ctx.enter_context(self.nc.sbuf_tensor(name, shape, dtype))


class Stage:

    def __init__(self, chip, name):
        self.chip, self.nc, self.name, self.ctx = chip, chip.nc, name, ExitStack()

    def __enter__(self):
        if len(self.chip.used_semaphores) > SEMAPHORES - STAGE_SEMAPHORES:
            self.nc.clear_and_free_semaphores(self.chip.used_semaphores)
            self.nc.all_engine_barrier()
            self.chip.used_semaphores = []
        return self

    def __exit__(self, *a):
        return self.ctx.__exit__(*a)

    def sb(self, name, shape, dtype=F32):
        return self.ctx.enter_context(self.nc.sbuf_tensor(f"{self.name}_{name}", shape, dtype))

    def sem(self, name, ahead=0):
        semaphore = self.nc.alloc_semaphore(f"{self.name}_{name}")
        self.chip.used_semaphores.append(semaphore)
        if ahead:
            self.nc.sync.sem_inc(semaphore, ahead)
        return semaphore

    def block(self):
        return self.ctx.enter_context(self.nc.Block())


class Chain:

    def __init__(self, engine, sem, start=0):
        self.engine, self.sem, self.n = engine, sem, start

    def done(self, instruction):
        instruction.then_inc(self.sem, 1)
        self.n = self.n + 1
        self.engine.wait_ge(self.sem, self.n)


def load_stage(chip):
    with Stage(chip, "load") as st:
        loaded = st.sem("loaded")
        block = st.block()

        @block.sync
        def _(sp):
            xs = chip.dram["x"].rearrange("b (t p) d -> p (b t) d", p=P)
            for q in range(4):
                tiles = slice(4 * q, 4 * q + 4)
                sp.dma_start(chip.x[:, tiles, :], xs[:, tiles, :]).then_inc(loaded, 16)
            sp.dma_start(chip.ident[:, :], chip.dram["ident"]).then_inc(loaded, 16)
            sp.wait_ge(loaded, 80)


def norm_stage(chip, name, scale):
    with Stage(chip, name) as st:
        xn = st.sb("xn", [P, TILES, D])
        stats = st.sb("stats", [P, TILES, 6])
        moments = st.sb("moments", [P, TILES, 2])
        rstd = st.sb("rstd", [P, TILES])
        var = st.sb("var", [P, TILES])
        y_turned = st.sem("y_turned")
        x_added = st.sem("x_added")
        stats_done = st.sem("stats_done")
        moments_done = st.sem("moments_done")
        var_done = st.sem("var_done")
        std_done = st.sem("std_done")
        rstd_done = st.sem("rstd_done")
        xn_ready = st.sem("xn_ready")
        xn_turned = st.sem("xn_turned")
        block = st.block()
        x, psum = chip.x, chip.psum

        @block.tensor
        def _(pe):
            if scale is not None:
                for t in range(TILES):
                    turn = nc_t(pe, psum[:, t // 4, t % 4 * P:(t % 4 + 1) * P], chip.yT[:, t * P:(t + 1) * P], chip)
                    if t % 4 == 3:
                        turn.then_inc(y_turned, 1)
            for t in range(TILES):
                pe.wait_ge(xn_ready, t + 1)
                turn = nc_t(pe, psum[:, 4 + t // 4, t % 4 * P:(t % 4 + 1) * P], xn[:, t, :], chip)
                if t % 4 == 3:
                    turn.then_inc(xn_turned, 1)

        @block.vector
        def _(dve):
            for q in range(4):
                if scale is not None:
                    dve.wait_ge(y_turned, q + 1)
                    tiles = x[:, 4 * q:4 * q + 4, :].rearrange("p t d -> p (t d)")
                    dve.scalar_tensor_tensor(tiles, psum[:, q, :], scale, tiles, ALU.mult, ALU.add).then_inc(x_added, 1)
                    dve.wait_ge(x_added, q + 1)
                for t in range(4 * q, 4 * q + 4):
                    last = dve.bn_stats(stats[:, t, :], x[:, t, :])
                last.then_inc(stats_done, 1)
            dve.wait_ge(stats_done, 4)
            for t in range(TILES):
                last = dve.bn_aggr(moments[:, t, :], stats[:, t, :])
            last.then_inc(moments_done, 1)
            dve.wait_ge(moments_done, 1)
            dve.tensor_scalar(var[:, :], moments[:, :, 1], EPS, None, ALU.add).then_inc(var_done, 1)
            dve.wait_ge(std_done, 1)
            dve.reciprocal(rstd[:, :], var[:, :]).then_inc(rstd_done, 1)
            dve.wait_ge(rstd_done, 1)
            for t in range(TILES):
                dve.tensor_scalar(xn[:, t, :], x[:, t, :], moments[:, t, 0:1], rstd[:, t:t + 1],
                                  ALU.subtract, ALU.mult).then_inc(xn_ready, 1)
            for q in (1, 3):
                dve.wait_ge(xn_turned, q + 1)
                dve.tensor_copy(chip.xnT[:, q * GROUP:(q + 1) * GROUP], psum[:, 4 + q, :])

        @block.scalar
        def _(act):
            act.wait_ge(var_done, 1)
            act.activation(var[:, :], var[:, :], ACT.Sqrt).then_inc(std_done, 1)
            for q in (0, 2):
                act.wait_ge(xn_turned, q + 1)
                act.copy(chip.xnT[:, q * GROUP:(q + 1) * GROUP], psum[:, 4 + q, :])


def nc_t(pe, out, in_, chip):
    return pe.transpose(out, in_, chip.ident[0:in_.shape[0], 0:in_.shape[0]])


def store_stage(chip, scale):
    with Stage(chip, "store") as st:
        y_turned = st.sem("y_turned")
        x_added = st.sem("x_added")
        stored = st.sem("stored")
        block = st.block()

        @block.tensor
        def _(pe):
            for t in range(TILES):
                turn = nc_t(pe, chip.psum[:, t // 4, t % 4 * P:(t % 4 + 1) * P], chip.yT[:, t * P:(t + 1) * P], chip)
                if t % 4 == 3:
                    turn.then_inc(y_turned, 1)

        @block.vector
        def _(dve):
            for q in range(4):
                dve.wait_ge(y_turned, q + 1)
                tiles = chip.x[:, 4 * q:4 * q + 4, :].rearrange("p t d -> p (t d)")
                dve.scalar_tensor_tensor(tiles, chip.psum[:, q, :], scale, tiles, ALU.mult,
                                         ALU.add).then_inc(x_added, 1)

        @block.sync
        def _(sp):
            out = chip.out.rearrange("b (t p) d -> p (b t) d", p=P)
            for q in range(4):
                sp.wait_ge(x_added, q + 1)
                tiles = slice(4 * q, 4 * q + 4)
                sp.dma_start(out[:, tiles, :], chip.x[:, tiles, :]).then_inc(stored, 16)
            sp.wait_ge(stored, 64)


def ffn_stage(chip, name):
    F = 512
    NC = F // P
    with Stage(chip, name) as st:
        w1 = st.sb("w1", [P, F])
        w2 = st.sb("w2", [P, NC, D])
        b1 = st.sb("b1", [P, NC])
        b2 = st.sb("b2", [P, 1])
        hidden = st.sb("hidden", [P, NC, GROUP])
        loaded = st.sem("loaded")
        up_done = st.sem("up_done")
        relu_done = st.sem("relu_done", ahead=NC)
        down_done = st.sem("down_done", ahead=1)
        y_copied = st.sem("y_copied", ahead=2)
        block = st.block()
        up, down = chip.psum[:, 0:NC, :], chip.psum[:, NC:NC + 2, :]

        @block.sync
        def _(sp):
            sp.dma_start(w1[:, :], chip.dram["ffn_w1"]).then_inc(loaded, 16)
            sp.dma_start(w2[:, :, :], chip.dram["ffn_w2"]).then_inc(loaded, 16)
            sp.dma_start(b1[:, :], chip.dram["ffn_b1"]).then_inc(loaded, 16)
            sp.dma_start(b2[:, :], chip.dram["ffn_b2"]).then_inc(loaded, 16)

        @block.tensor
        def _(pe):
            pe.wait_ge(loaded, 64)
            with pe.Fori(0, GROUPS // 2) as pair:
                for q in range(2):
                    g = pair * 2 + q
                    for c in range(NC):
                        pe.wait_ge(relu_done, g * NC + c + 1)
                        pe.matmul(up[:, c, :], w1[:, c * P:(c + 1) * P], chip.xnT[:, bass.ts(g, GROUP)],
                                  start=True, stop=True).then_inc(up_done, 1)
                    pe.wait_ge(y_copied, g + 1)
                    for c in range(NC):
                        pe.wait_ge(relu_done, NC + g * NC + c + 1)
                        mm = pe.matmul(down[:, q, :], w2[:, c, :], hidden[:, c, :], start=(c == 0), stop=(c == NC - 1))
                    mm.then_inc(down_done, 1)

        @block.scalar
        def _(act):
            act.wait_ge(loaded, 64)
            with act.Fori(0, GROUPS) as g:
                act.wait_ge(down_done, g + 1)
                for c in range(NC):
                    act.wait_ge(up_done, g * NC + c + 1)
                    act.activation(hidden[:, c, :], up[:, c, :], ACT.Relu, bias=b1[:, c:c + 1]).then_inc(relu_done, 1)

        @block.vector
        def _(dve):
            dve.wait_ge(loaded, 64)
            with dve.Fori(0, GROUPS // 2) as pair:
                for q in range(2):
                    g = pair * 2 + q
                    dve.wait_ge(down_done, g + 2)
                    dve.tensor_scalar(chip.yT[:, bass.ts(g, GROUP)], down[:, q, :], b2[:, 0:1], None,
                                      ALU.add).then_inc(y_copied, 1)


TRIAL_COUNT = 8
ROUNDS = 10


def router_stage(chip, name, weights, mode):
    J = PER_B
    with Stage(chip, name) as st:
        wr = st.sb("wr", [P, E])
        prob = st.sb("prob", [P, TILES, E])
        pick = st.sb("pick", [P, TILES, E])
        rank = st.sb("rank", [P, TILES, E])
        first = st.sb("first", [P, TILES, E])
        comb = st.sb("comb", [P, J, TRIAL_COUNT if mode == "choice" else 1, B, E])
        descending = st.sb("descending", [P, E])
        best = st.sb("best", [P, TILES])
        best2 = st.sb("best2", [P, TILES])
        part = st.sb("part", [P, TILES])
        share = st.sb("share", [P, TILES])
        combT = st.sb("combT", [B * E, T])
        loaded = st.sem("loaded")
        logits_done = st.sem("logits_done")
        shifted = st.sem("shifted")
        exp_done = st.sem("exp_done")
        own = st.sem("dve_steps")
        comb_ready = st.sem("comb_ready")
        comb_turned = st.sem("comb_turned")
        comb_copied = st.sem("comb_copied")
        stored = st.sem("stored")
        if mode == "choice":
            place = st.sb("place", [P, ROUNDS])
            trials = st.sb("trials", [P, ROUNDS], I32)
            ones = st.sb("ones", [P, 1])
            same_row = st.sb("same_row", [P, P])
            low = st.sb("low", [P, 1], I32)
            trial = st.sb("trial", [P, 1], I32)
            keep = st.sb("keep", [P, 1], I32)
            count = st.sb("count", [P, 1])
            enough = st.sb("enough", [P, 1])
            all_rows = st.sb("all_rows", [P, T])
            above_all = st.sb("above_all", [P, T])
            above = above_all[0:B * E, :]
            compared, summed = st.sem("compared", ahead=1), st.sem("summed", ahead=1)
            equal = st.sb("equal", [B * E, T])
            order = st.sb("order", [B * E, T])
            room = st.sb("room", [B * E, 1])
        block = st.block()
        logits = chip.psum[:, 0, 0:TILES * E].rearrange("p (t e) -> p t e", e=E)
        TRIALS = TRIAL_COUNT if mode == "choice" else 1
        turned = chip.psum[0:TRIALS * B * E, 1:3, :]

        def each(v):
            return v[:, :].unsqueeze(2).to_broadcast([P, TILES, E])

        @block.sync
        def _(sp):
            sp.dma_start(wr[:, :], chip.dram[weights]).then_inc(loaded, 16)
            sp.dma_start(descending[:, :], chip.dram["descending"]).then_inc(loaded, 16)
            if mode == "choice":
                sp.dma_start(place[:, :], chip.dram["place"]).then_inc(loaded, 16)
                sp.dma_start(trials[:, :], chip.dram["trials"]).then_inc(loaded, 16)
                sp.dma_start(same_row[:, :], chip.dram["same_row"]).then_inc(loaded, 16)
            sp.wait_ge(comb_copied, 3 if mode == "choice" else 2)
            sp.dma_start(chip.weights_by_expert, combT[:, :]).then_inc(stored, 16)
            sp.wait_ge(stored, 16)

        @block.tensor
        def _(pe):
            pe.wait_ge(loaded, 80 if mode == "choice" else 32)
            for t in range(TILES):
                mm = pe.matmul(logits[:, t, :], chip.xnT[:, t * P:(t + 1) * P], wr[:, :], start=True, stop=True)
            mm.then_inc(logits_done, 1)
            pe.wait_ge(comb_ready, 1)
            for j in range(J):
                turn = nc_t(pe, turned[:, j // 4, j % 4 * P:(j % 4 + 1) * P],
                            comb[:, j, :, :, :].rearrange("p r b e -> p (r b e)"), chip)
                if j % 4 == 3:
                    turn.then_inc(comb_turned, 1)
            if mode == "choice":
                with pe.Fori(0, ROUNDS) as i:
                    pe.wait_ge(compared, i + 2)
                    pe.matmul(chip.psum[:, 3, 0:1], same_row[:, :], enough[:, :], start=True, stop=True).then_inc(summed, 1)

        @block.scalar
        def _(act):
            act.wait_ge(shifted, 1)
            act.activation(prob[:, :, :], prob[:, :, :], ACT.Exp).then_inc(exp_done, 1)
            if mode == "softmax":
                act.wait_ge(shifted, 2)
                act.activation(part[:, :], part[:, :], ACT.Exp).then_inc(exp_done, 1)

        def choose(dve, chain):
            CAP = T * 2 // E
            done = chain.done
            dve.wait_ge(loaded, 80)
            done(dve.memset(ones[:, :], 1.0))
            done(dve.memset(low[:, :], 0))
            start = chain.n
            with dve.Fori(0, ROUNDS) as i:
                step = Chain(dve, own, i * 4 + start)
                step.done(dve.tensor_tensor(trial[:, :], low[:, :], trials[:, bass.ds(i, 1)], ALU.bitwise_or))
                step.done(dve.tensor_scalar(above_all[:, :], all_rows[:, :], trial[:, :].bitcast(F32), None, ALU.is_ge,
                                            ALU.add, accum_out=count[:, :]))
                dve.tensor_scalar(enough[:, :], count[:, :], float(CAP), None, ALU.is_ge).then_inc(compared, 1)
                dve.wait_ge(summed, i + 2)
                step.done(dve.tensor_scalar(keep[:, :], chip.psum[:, 3, 0:1], place[:, bass.ds(i, 1)], None, ALU.mult))
                step.done(dve.tensor_tensor(low[:, :], low[:, :], keep[:, :], ALU.bitwise_or))
            chain.n = start + 4 * ROUNDS
            least = low[0:B * E, :].bitcast(F32)
            count_own = count[0:B * E, :]
            own_rows = all_rows[0:B * E, :]
            done(dve.tensor_scalar(above, own_rows, least, None, ALU.is_gt, ALU.add, accum_out=count_own))
            done(dve.tensor_scalar(equal[:, :], own_rows, least, None, ALU.is_equal))
            done(dve.tensor_scalar(room[:, :], count_own, -1.0, float(CAP), ALU.mult, ALU.add))
            done(dve.tensor_tensor_scan(order[:, :], ones[0:B * E, :].to_broadcast([B * E, T]), equal[:, :], 0.0,
                                        ALU.mult, ALU.add))
            done(dve.scalar_tensor_tensor(equal[:, :], order[:, :], room[:, 0:1], equal[:, :], ALU.is_le, ALU.mult))
            done(dve.tensor_tensor(above, above, equal[:, :], ALU.add))
            dve.tensor_tensor(combT[:, :], own_rows, above, ALU.mult).then_inc(comb_copied, 1)

        @block.vector
        def _(dve):
            chain = Chain(dve, own)
            done = chain.done
            dve.wait_ge(logits_done, 1)
            done(dve.tensor_reduce(best[:, :], logits, AX_X, ALU.max))
            dve.tensor_tensor(prob[:, :, :], logits, each(best), ALU.subtract).then_inc(shifted, 1)
            dve.wait_ge(exp_done, 1)
            done(dve.tensor_reduce(best[:, :], prob[:, :, :], AX_X, ALU.add))
            done(dve.reciprocal(share[:, :], best[:, :]))
            if mode == "choice":
                done(dve.tensor_tensor(prob[:, :, :], prob[:, :, :], each(share), ALU.mult))
                for b in range(B):
                    copy = dve.tensor_copy(comb[:, :, :, b, :], prob[:, b * J:(b + 1) * J, :].unsqueeze(2).to_broadcast(
                        [P, J, TRIAL_COUNT, E]))
                copy.then_inc(comb_ready, 1)
                for h in range(2):
                    dve.wait_ge(comb_turned, h + 1)
                    copy = dve.tensor_copy(all_rows[:, h * GROUP:(h + 1) * GROUP], turned[:, h, :])
                    copy.then_inc(comb_copied, 1)
                dve.wait_ge(comb_copied, 2)
                choose(dve, chain)
                return
            done(dve.tensor_tensor(prob[:, :, :], prob[:, :, :], each(share), ALU.mult))

            def take_best(value, selected):
                done(dve.tensor_reduce(value[:, :], prob[:, :, :], AX_X, ALU.max))
                done(dve.tensor_tensor(rank[:, :, :], prob[:, :, :], each(value), ALU.is_ge))
                done(dve.tensor_tensor(rank[:, :, :], rank[:, :, :],
                                       descending[:, :].unsqueeze(1).to_broadcast([P, TILES, E]), ALU.mult))
                done(dve.tensor_reduce(part[:, :], rank[:, :, :], AX_X, ALU.max))
                done(dve.tensor_tensor(selected[:, :, :], rank[:, :, :], each(part), ALU.is_ge))

            dve.wait_ge(loaded, 32)
            take_best(best, first)
            if mode == "sum":
                done(dve.tensor_copy(pick[:, :, :], prob[:, :, :]))
            done(dve.scalar_tensor_tensor(prob[:, :, :], first[:, :, :], -2.0, prob[:, :, :], ALU.mult, ALU.add))
            second = rank
            take_best(best2, second)
            by_row = comb[:, :, 0, :, :].rearrange("p j b e -> p b j e")
            if mode == "sum":
                done(dve.tensor_tensor(share[:, :], best[:, :], best2[:, :], ALU.add))
                done(dve.reciprocal(share[:, :], share[:, :]))
                done(dve.tensor_tensor(first[:, :, :], first[:, :, :], second[:, :, :], ALU.add))
                done(dve.tensor_tensor(pick[:, :, :], pick[:, :, :], each(share), ALU.mult))
                final, other, op = pick, first, ALU.mult
            else:
                dve.tensor_tensor(part[:, :], best2[:, :], best[:, :], ALU.subtract).then_inc(shifted, 1)
                dve.wait_ge(exp_done, 2)
                done(dve.tensor_scalar(share[:, :], part[:, :], 1.0, None, ALU.add))
                done(dve.reciprocal(share[:, :], share[:, :]))
                done(dve.tensor_tensor(part[:, :], part[:, :], share[:, :], ALU.mult))
                done(dve.tensor_tensor(first[:, :, :], first[:, :, :], each(share), ALU.mult))
                done(dve.tensor_tensor(second[:, :, :], second[:, :, :], each(part), ALU.mult))
                final, other, op = first, second, ALU.add
            for b in range(B):
                tiles = slice(b * J, (b + 1) * J)
                mul = dve.tensor_tensor(by_row[:, b], final[:, tiles, :], other[:, tiles, :], op)
            mul.then_inc(comb_ready, 1)
            for h in range(2):
                dve.wait_ge(comb_turned, h + 1)
                dve.tensor_copy(combT[:, h * GROUP:(h + 1) * GROUP], turned[:, h, :]).then_inc(comb_copied, 1)


def experts_stage(chip, name, hidden_dim, gated, up_names, down_name):
    NC = hidden_dim // P
    NU = len(up_names)
    STEPS = E * GROUPS
    with Stage(chip, name) as st:
        raw_up = [st.sb(f"raw_up{u}", [P, hidden_dim]) for u in range(NU)]
        raw_down = st.sb("raw_down", [P, NC, D])
        w_up = [[[st.sb(f"w_up{p}{u}_{part}", [P, hidden_dim], F32R) for part in PARTS] for u in range(NU)] for p in range(2)]
        w_down = [[st.sb(f"w_down{p}_{part}", [P, NC, D], F32R) for part in PARTS] for p in range(2)]
        xn = [st.sb(f"xn_{part}", [P, TOK], F32R) for part in PARTS]
        weight = [st.sb(f"weight{p}", [P, TOK]) for p in range(2)]
        ones = st.sb("ones", [P, 1])
        HB = 4
        full = st.sb("full", [P, 2, GROUP])
        hidden = [st.sb(f"hidden_{part}", [P, HB, GROUP], F32R) for part in PARTS]
        silu = st.sb("silu", [P, 2, GROUP])
        scaled = st.sb("scaled", [P, 2, GROUP])
        loaded = st.sem("loaded")
        weight_loaded = [st.sem(f"weight_loaded{p}") for p in range(2)]
        x_high, x_split = st.sem("x_high"), st.sem("x_split")
        ones_done = st.sem("ones_done")
        w_high, w_split = st.sem("w_high"), st.sem("w_split", ahead=1)
        up_done = st.sem("up_done")
        silu_done = st.sem("silu_done")
        full_done = st.sem("full_done", ahead=2)
        high_done = st.sem("high_done")
        hidden_done = st.sem("hidden_done", ahead=2)
        down_done = st.sem("down_done", ahead=HB)
        scaled_done = st.sem("scaled_done", ahead=2)
        added = st.sem("added")
        block = st.block()
        up = chip.psum[:, 0:4, :]
        down = chip.psum[:, 4:6, :]
        LOADS = 16 * (NU + 1)

        def later(pair, p, g, c, chunks):
            c += chunks
            if c < NC:
                return pair, p, g, c
            return (pair, p, g + 1, c - NC) if g < GROUPS - 1 else (pair + p, 1 - p, 0, c - NC)

        def all_experts(eng, expert):
            with eng.Fori(0, E // 2 - 1) as pair:
                expert(pair, 0, False)
                expert(pair, 1, False)
            expert(E // 2 - 1, 0, False)
            expert(E // 2 - 1, 1, True)

        @block.sync
        def _(sp):
            def load(e, p, turn):
                sp.wait_ge(w_split, e + 1)
                for u in range(NU):
                    sp.dma_start(raw_up[u][:, :], chip.dram[up_names[u]][bass.ds(e, 1)].rearrange(
                        "e p f -> (e p) f")).then_inc(loaded, 16)
                sp.dma_start(raw_down[:, :, :], chip.dram[down_name][bass.ds(e, 1)].rearrange(
                    "e p c d -> (e p) c d")).then_inc(loaded, 16)
                if turn is not None:
                    sp.wait_ge(scaled_done, 2 + (turn * 2 + p - 1) * GROUPS)
                rows = chip.weights_by_expert.rearrange("(b e) t -> e b t", b=B)[bass.ds(e, 1)]
                rows = rows.rearrange("e b t -> (e b) t").unsqueeze(0).to_broadcast([P, B, T])
                sp.dma_start(weight[p][:, :].rearrange("p (b t) -> p b t", b=B), rows).then_inc(weight_loaded[p], 16)

            load(0, 0, None)
            load(1, 1, None)
            with sp.Fori(1, E // 2) as pair:
                for p in range(2):
                    load(pair * 2 + p, p, pair)

        @block.tensor
        def _(pe):
            def ups(pair, p, g, c):
                step = (pair * 2 + p) * GROUPS + g
                if c == 0 and g == 0:
                    pe.wait_ge(w_split, pair * 2 + p + 2)
                pe.wait_ge(full_done, step * NC + c + 1)
                for u in range(NU):
                    mm = split_product(pe, up[:, c % 2 * 2 + u, :], [w[:, c * P:(c + 1) * P] for w in w_up[p][u]],
                                       [x[:, g * GROUP:(g + 1) * GROUP] for x in xn])
                mm.then_inc(up_done, 1)

            def down_product(pair, p, g, c):
                step = (pair * 2 + p) * GROUPS + g
                if c == 0:
                    pe.wait_ge(scaled_done, step + 1)
                pe.wait_ge(hidden_done, step * NC + c + 3)
                mm = split_product(pe, down[:, g % 2, :], [w[:, c, :] for w in w_down[p]],
                                   [h[:, (g * NC + c) % HB, :] for h in hidden], first=(c == 0), last=(c == NC - 1))
                mm.then_inc(down_done, 1)

            def expert(pair, p, last):
                for g in range(GROUPS):
                    for c in range(NC):
                        if not (last and g == GROUPS - 1 and c >= NC - 2):
                            ups(*later(pair, p, g, c, 2))
                        down_product(pair, p, g, c)

            pe.wait_ge(x_split, GROUPS)
            ups(0, 0, 0, 0)
            ups(0, 0, 0, 1)
            all_experts(pe, expert)

        @block.scalar
        def _(act):
            func = ACT.Silu if gated else ACT.Gelu
            for g in range(GROUPS):
                cols = slice(g * GROUP, (g + 1) * GROUP)
                act.copy(xn[0][:, cols], chip.xnT[:, cols]).then_inc(x_high, 1)
            with act.Fori(0, E) as e:
                for j in range(GROUPS * NC):
                    k, c = e * (GROUPS * NC) + j, j % NC
                    act.wait_ge(up_done, k + 1)
                    if gated:
                        act.wait_ge(full_done, k + 1)
                        act.activation(silu[:, c % 2, :], up[:, c % 2 * 2, :], func).then_inc(silu_done, 1)
                    else:
                        act.wait_ge(hidden_done, k + 1)
                        act.activation(full[:, c % 2, :], up[:, c % 2 * 2, :], func).then_inc(full_done, 1)

        @block.vector
        def _(dve):
            for g in range(GROUPS):
                cols = slice(g * GROUP, (g + 1) * GROUP)
                dve.wait_ge(x_high, g + 1)
                dve.tensor_tensor(xn[1][:, cols], chip.xnT[:, cols], xn[0][:, cols].bitcast(F32),
                                  ALU.subtract).then_inc(x_split, 1)

            def make_hidden(pair, p, g, c):
                k = ((pair * 2 + p) * GROUPS + g) * NC + c
                if gated:
                    dve.wait_ge(silu_done, k + 1)
                    dve.wait_ge(hidden_done, k + 1)
                    dve.tensor_tensor(full[:, c % 2, :], silu[:, c % 2, :], up[:, c % 2 * 2 + 1, :],
                                      ALU.mult).then_inc(full_done, 1)
                dve.wait_ge(full_done, k + 3)
                dve.wait_ge(down_done, k + 1)
                high, low = (h[:, (g * NC + c) % HB, :] for h in hidden)
                dve.tensor_copy(high, full[:, c % 2, :]).then_inc(high_done, 1)
                dve.wait_ge(high_done, k + 1)
                dve.tensor_tensor(low, full[:, c % 2, :], high.bitcast(F32), ALU.subtract).then_inc(hidden_done, 1)

            def expert(pair, p, last):
                for g in range(GROUPS):
                    step = (pair * 2 + p) * GROUPS + g
                    for c in range(NC):
                        if not (last and g == GROUPS - 1 and c >= NC - 2):
                            make_hidden(*later(pair, p, g, c, 2))
                    if g == 0:
                        dve.wait_ge(weight_loaded[p], (pair + 1) * 16)
                    dve.wait_ge(down_done, HB + (step + 1) * NC)
                    dve.wait_ge(added, step + 1)
                    dve.tensor_tensor(scaled[:, g % 2, :], down[:, g % 2, :], weight[p][:, g * GROUP:(g + 1) * GROUP],
                                      ALU.mult).then_inc(scaled_done, 1)

            make_hidden(0, 0, 0, 0)
            make_hidden(0, 0, 0, 1)
            all_experts(dve, expert)

        @block.gpsimd
        def _(pool):
            def split_weights(e, p):
                pool.wait_ge(loaded, (e + 1) * LOADS)
                pairs = [(raw_up[u][:, :], [w[:, :] for w in w_up[p][u]]) for u in range(NU)]
                pairs.append((raw_down[:, :, :], [w[:, :, :] for w in w_down[p]]))
                for raw, (high, _) in pairs:
                    one = ones[:, :] if len(raw.shape) == 2 else ones[:, :].unsqueeze(2)
                    last = pool.tensor_tensor(high, raw, one.to_broadcast(list(raw.shape)), ALU.mult)
                last.then_inc(w_high, 1)
                pool.wait_ge(w_high, e + 1)
                for raw, (high, low) in pairs:
                    last = pool.tensor_tensor(low, raw, high.bitcast(F32), ALU.subtract)
                last.then_inc(w_split, 1)

            def add(step, g):
                y = chip.yT[:, g * GROUP:(g + 1) * GROUP]
                pool.wait_ge(scaled_done, step + 3)
                pool.tensor_tensor(y, y, scaled[:, g % 2, :], ALU.add).then_inc(added, 1)

            pool.memset(ones[:, :], 1.0).then_inc(ones_done, 1)
            pool.wait_ge(ones_done, 1)
            split_weights(0, 0)
            pool.memset(chip.yT[:, :], 0.0).then_inc(added, 2)
            pool.wait_ge(added, 2)
            split_weights(1, 1)
            with pool.Fori(0, E // 2 - 1) as pair:
                for p in range(2):
                    e = pair * 2 + p
                    for g in range(GROUPS):
                        add(e * GROUPS + g, g)
                    split_weights(e + 2, p)
            with pool.Fori(E - 2, E) as e:
                for g in range(GROUPS):
                    add(e * GROUPS + g, g)


PARTS = ("high", "low")


def split_product(pe, out, weights, moving, first=True, last=True):
    (w_high, w_low), (x_high, x_low) = weights, moving
    pe.matmul(out, w_high, x_high, start=first, stop=False)
    pe.matmul(out, w_high, x_low, start=False, stop=False)
    return pe.matmul(out, w_low, x_high, start=False, stop=last)


def project_stage(chip, name, w_names, features, tokens, biases=None):
    nf = len(features)
    with Stage(chip, name) as st:
        w = st.sb("w", [P, len(w_names), P])
        bias = st.sb("bias", [P, nf]) if biases else None
        bias_row = st.sb("bias_row", [P, len(tokens), P]) if biases else None
        loaded = st.sem("loaded")
        products = st.sem("products")
        read = st.sem("banks_read", ahead=8)
        block = st.block()
        loads = len(w_names) + (2 if biases else 0)
        nt = len(tokens)

        @block.sync
        def _(sp):
            for n, wn in enumerate(w_names):
                sp.dma_start(w[:, n, :], chip.dram[wn]).then_inc(loaded, 16)
            if biases:
                sp.dma_start(bias[:, :], chip.dram[biases[0]]).then_inc(loaded, 16)
                sp.dma_start(bias_row[:, :, :].rearrange("p a d -> p (a d)"), chip.dram[biases[1]]).then_inc(loaded, 16)

        jobs = [("features", n, g) for g in range(GROUPS) for n in range(nf)] + [("tokens", 0, q) for q in range(TILES // 2)]

        @block.tensor
        def _(pe):
            pe.wait_ge(loaded, 16 * loads)
            for k, (kind, n, q) in enumerate(jobs):
                pe.wait_ge(read, k + 1)
                if kind == "features":
                    mm = pe.matmul(chip.psum[:, k % 8, :], w[:, n, :], chip.xnT[:, q * GROUP:(q + 1) * GROUP],
                                   start=True, stop=True)
                else:
                    for half in range(2):
                        t = 2 * q + half
                        mm = pe.matmul(chip.psum[:, k % 8, half * nt * P:(half + 1) * nt * P], chip.xnT[:, t * P:(t + 1) * P],
                                       w[:, nf:, :].rearrange("p a d -> p (a d)"), start=True, stop=True)
                mm.then_inc(products, 1)

        def copy(eng, k, kind, n, q):
            bank = chip.psum[:, k % 8, :]
            eng.wait_ge(products, k + 1)
            if kind == "features":
                dst = features[n][:, q * GROUP:(q + 1) * GROUP]
                if biases:
                    return eng.tensor_scalar(dst, bank, bias[:, n:n + 1], None, ALU.add)
                return eng.tensor_copy(dst, bank)
            view = bank[:, 0:2 * nt * P].rearrange("p (t a d) -> p t a d", t=2, a=nt)
            for a in range(nt):
                dst = tokens[a][:, 2 * q:2 * q + 2, :]
                if biases:
                    last = eng.tensor_tensor(dst, view[:, :, a], bias_row[:, a, :].unsqueeze(1).to_broadcast([P, 2, P]),
                                             ALU.add)
                else:
                    last = eng.tensor_copy(dst, view[:, :, a])
            return last

        @block.vector
        def _(dve):
            dve.wait_ge(loaded, 16 * loads)
            for k, job in enumerate(jobs):
                copy(dve, k, *job).then_inc(read, 1)


def output_stage(chip, name, features, w_name, bias_name):
    with Stage(chip, name) as st:
        w = st.sb("w", [P, P])
        bias = st.sb("bias", [P, 1])
        loaded, out_done = st.sem("loaded"), st.sem("out_done")
        block = st.block()

        @block.sync
        def _(sp):
            sp.dma_start(w[:, :], chip.dram[w_name]).then_inc(loaded, 16)
            sp.dma_start(bias[:, :], chip.dram[bias_name]).then_inc(loaded, 16)

        @block.tensor
        def _(pe):
            pe.wait_ge(loaded, 32)
            for g in range(GROUPS):
                pe.matmul(chip.psum[:, g, :], w[:, :], features[:, g * GROUP:(g + 1) * GROUP],
                          start=True, stop=True).then_inc(out_done, 1)

        @block.vector
        def _(dve):
            dve.wait_ge(loaded, 32)
            for g in range(GROUPS):
                dve.wait_ge(out_done, g + 1)
                dve.tensor_scalar(chip.yT[:, g * GROUP:(g + 1) * GROUP], chip.psum[:, g, :], bias[:, 0:1], None, ALU.add)


DH0 = D // H
SLOTS = 32 // DH0
ROWS = H // SLOTS


def retention_attention(chip):
    with Stage(chip, "retention") as outer:
        qT, kT = outer.sb("qT", [P, TOK]), outer.sb("kT", [P, TOK])
        k_tok, v_tok = outer.sb("k_tok", [P, TILES, P]), outer.sb("v_tok", [P, TILES, P])
        retained = outer.sb("retained", [P, TOK])
        project_stage(chip, "retention_in", ("ret_wq", "ret_wk", "ret_wk", "ret_wv"), (qT, kT), (k_tok, v_tok))
        retention_chunks(chip, qT, kT, k_tok, v_tok, retained)
        group_norm_stage(chip, retained)


def retention_chunks(chip, qT, kT, k_tok, v_tok, retained):
    with Stage(chip, "retention_chunks") as st:
        decay = st.sb("decay", [P, H, P])
        q_decay = st.sb("q_decay", [P, P])
        k_decay = st.sb("k_decay", [P, P])
        chunk_decay = st.sb("chunk_decay", [P, 1])
        same_head = st.sb("same_head", [P, P])
        slot = st.sb("slot", [P, SLOTS])
        slot_cols = st.sb("slot_cols", [P, SLOTS, P])
        vals = [st.sb(f"vals{p}", [P, SLOTS, P]) for p in range(2)]
        kc = [st.sb(f"kc{p}", [P, P]) for p in range(2)]
        qm = [st.sb(f"qm{p}", [P, SLOTS, P]) for p in range(2)]
        qd = [st.sb(f"qd{p}", [P, P]) for p in range(2)]
        kd = [st.sb(f"kd{p}", [P, P]) for p in range(2)]
        probs = st.sb("probs", [P, H, P])
        state = st.sb("state", [P, P])
        fresh = st.sb("fresh", [P, P])
        loaded = st.sem("loaded")
        prepared = st.sem("prepared")
        scores_done = st.sem("scores_done")
        probs_done = st.sem("probs_done")
        update_done = st.sem("update_done")
        inter_done = st.sem("inter_done", ahead=1)
        fresh_done = st.sem("fresh_done", ahead=1)
        state_done = st.sem("state_done", ahead=1)
        y_done = st.sem("y_done")
        y_copied = st.sem("y_copied", ahead=2)
        block = st.block()
        scores, y, update = chip.psum[:, 0:4, :], chip.psum[:, 4:6, 0:P], chip.psum[:, 6, 0:P]

        @block.sync
        def _(sp):
            sp.dma_start(decay[:, :, :], chip.dram["ret_decay"]).then_inc(loaded, 16)
            for buf, nm in ((q_decay, "ret_q_decay"), (k_decay, "ret_k_decay"), (chunk_decay, "ret_chunk_decay"),
                            (same_head, "same_head"), (slot, "slot")):
                sp.dma_start(buf[:, :], chip.dram[nm]).then_inc(loaded, 16)
            sp.dma_start(slot_cols[:, :, :], chip.dram["slot_cols"]).then_inc(loaded, 16)

        @block.gpsimd
        def _(pool):
            pool.wait_ge(loaded, 112)
            with pool.Fori(0, TILES // 2) as pair:
                for p in range(2):
                    n = pair * 2 + p
                    pool.wait_ge(y_copied, n + 1)
                    cols = bass.ts(n, P)
                    pool.tensor_copy(kc[p][:, :], kT[:, cols])
                    pool.tensor_tensor(qm[p][:, :, :], qT[:, cols].unsqueeze(1).to_broadcast([P, SLOTS, P]),
                                       slot[:, :].unsqueeze(2).to_broadcast([P, SLOTS, P]), ALU.mult)
                    pool.tensor_tensor(vals[p][:, :, :], v_tok[:, bass.ds(n, 1), :].to_broadcast([P, SLOTS, P]),
                                       slot_cols[:, :, :], ALU.mult)
                    pool.tensor_tensor(qd[p][:, :], qT[:, cols], q_decay[:, :], ALU.mult)
                    pool.tensor_tensor(kd[p][:, :], k_tok[:, bass.ds(n, 1), :].rearrange("p a d -> p (a d)"), k_decay[:, :],
                                       ALU.mult).then_inc(prepared, 1)

        @block.tensor
        def _(pe):
            def score(n, p, r):
                if r == 0:
                    pe.wait_ge(prepared, n + 1)
                rows = slice(32 * r, 32 * r + 32)
                pe.matmul(scores[:, r, :], kc[p][rows, :], qm[p][rows, :, :].rearrange("p s i -> p (s i)"),
                          start=True, stop=True).then_inc(scores_done, 1)

            def chunk(b, n, p, last):
                v = v_tok[:, bass.ds(n, 1), :].rearrange("p a d -> p (a d)")
                pe.wait_ge(fresh_done, n + 1)
                pe.matmul(update, kd[p][:, :], v, start=True, stop=True).then_inc(update_done, 1)
                pe.wait_ge(state_done, n + b + 2)
                pe.wait_ge(y_copied, n + 1)
                pe.matmul(y[:, p, :], state[:, :], qd[p][:, :], start=True, stop=False,
                          skip_group_check=True).then_inc(inter_done, 1)
                for r in range(ROWS):
                    pe.wait_ge(probs_done, n * ROWS + r + 1)
                    rows = slice(32 * r, 32 * r + 32)
                    for s in range(SLOTS):
                        h = r * SLOTS + s
                        mm = pe.matmul(y[rows, p, :], vals[p][:, s, rows], probs[:, h, :],
                                       start=False, stop=(h == H - 1), skip_group_check=True)
                    if r == ROWS - 1:
                        mm.then_inc(y_done, 1)
                    if not last:
                        score(n + 1, 1 - p, r)

            with pe.Fori(0, B) as b:
                for r in range(ROWS):
                    score(b * PER_B, 0, r)
                with pe.Fori(0, PER_B // 2 - 1) as pair:
                    for p in range(2):
                        chunk(b, b * PER_B + pair * 2 + p, p, False)
                for p in range(2):
                    chunk(b, b * PER_B + PER_B - 2 + p, p, p == 1)

        @block.vector
        def _(dve):
            dve.wait_ge(loaded, 112)
            with dve.Fori(0, B) as b:
                dve.wait_ge(inter_done, b * PER_B + 1)
                dve.wait_ge(state_done, b * (PER_B + 1) + 1)
                dve.memset(state[:, :], 0.0).then_inc(state_done, 1)
                with dve.Fori(0, PER_B) as c:
                    n = b * PER_B + c
                    for r in range(ROWS):
                        dve.wait_ge(scores_done, n * ROWS + r + 1)
                        heads = slice(r * SLOTS, (r + 1) * SLOTS)
                        dve.tensor_tensor(probs[:, heads, :].rearrange("p s i -> p (s i)"), scores[:, r, :],
                                          decay[:, heads, :].rearrange("p s i -> p (s i)"), ALU.mult).then_inc(probs_done, 1)
                    dve.wait_ge(update_done, n + 1)
                    dve.wait_ge(state_done, n + b + 2)
                    dve.tensor_tensor(fresh[:, :], update, same_head[:, :], ALU.mult).then_inc(fresh_done, 1)
                    dve.wait_ge(fresh_done, n + 2)
                    dve.wait_ge(inter_done, n + 2)
                    dve.scalar_tensor_tensor(state[:, :], state[:, :], chunk_decay[:, 0:1], fresh[:, :], ALU.mult,
                                             ALU.add).then_inc(state_done, 1)

        @block.scalar
        def _(act):
            with act.Fori(0, TILES // 2) as pair:
                for p in range(2):
                    n = pair * 2 + p
                    act.wait_ge(y_done, n + 1)
                    act.copy(retained[:, bass.ts(n, P)], y[:, p, :]).then_inc(y_copied, 1)


def group_norm_stage(chip, retained):
    with Stage(chip, "group_norm") as st:
        w = st.sb("w", [P, P])
        affine = st.sb("affine", [P, 2])
        head_mean = st.sb("head_mean", [P, P])
        y = st.sb("y", [P, TOK])
        stats = st.sb("stats", [P, GROUPS, 6])
        moments = st.sb("moments", [P, B, 2])
        mean_of = st.sb("mean_of", [P, B])
        off = st.sb("off", [P, B])
        var_of = st.sb("var_of", [P, B])
        scale, shift = st.sb("scale", [P, B]), st.sb("shift", [P, B])
        loaded, own = st.sem("loaded"), st.sem("dve_steps")
        asked = st.sem("asked")
        averaged = st.sem("averaged")
        var_done, std_done = st.sem("var_done"), st.sem("std_done")
        normed, out_done = st.sem("normed"), st.sem("out_done")
        block = st.block()
        psum = chip.psum

        @block.sync
        def _(sp):
            sp.dma_start(w[:, :], chip.dram["ret_wo"]).then_inc(loaded, 16)
            sp.dma_start(affine[:, :], chip.dram["ret_affine"]).then_inc(loaded, 16)
            sp.dma_start(head_mean[:, :], chip.dram["head_mean"]).then_inc(loaded, 16)

        @block.tensor
        def _(pe):
            pe.wait_ge(loaded, 48)
            for k, v in enumerate((moments[:, :, 0], off[:, :])):
                pe.wait_ge(asked, k + 1)
                pe.matmul(psum[:, 4, k * B:(k + 1) * B], head_mean[:, :], v, start=True, stop=True).then_inc(averaged, 1)
            for g in range(GROUPS):
                pe.wait_ge(normed, g + 1)
                pe.matmul(psum[:, g, :], w[:, :], y[:, g * GROUP:(g + 1) * GROUP], start=True,
                          stop=True).then_inc(out_done, 1)

        @block.vector
        def _(dve):
            done = Chain(dve, own).done
            for g in range(GROUPS):
                last = dve.bn_stats(stats[:, g, :], retained[:, g * GROUP:(g + 1) * GROUP])
            done(last)
            for b in range(B):
                last = dve.bn_aggr(moments[:, b, :], stats[:, 2 * b:2 * b + 2, :].rearrange("p a s -> p (a s)"))
            last.then_inc(asked, 1)
            dve.wait_ge(averaged, 1)
            done(dve.tensor_copy(mean_of[:, :], psum[:, 4, 0:B]))
            done(dve.tensor_tensor(off[:, :], moments[:, :, 0], mean_of[:, :], ALU.subtract))
            done(dve.tensor_tensor(off[:, :], off[:, :], off[:, :], ALU.mult))
            dve.tensor_tensor(off[:, :], off[:, :], moments[:, :, 1], ALU.add).then_inc(asked, 1)
            dve.wait_ge(averaged, 2)
            dve.tensor_scalar(var_of[:, :], psum[:, 4, B:2 * B], EPS, None, ALU.add).then_inc(var_done, 1)
            dve.wait_ge(std_done, 1)
            dve.wait_ge(loaded, 48)
            done(dve.reciprocal(scale[:, :], var_of[:, :]))
            done(dve.tensor_scalar(scale[:, :], scale[:, :], affine[:, 0:1], None, ALU.mult))
            done(dve.tensor_tensor(shift[:, :], mean_of[:, :], scale[:, :], ALU.mult))
            done(dve.tensor_scalar(shift[:, :], shift[:, :], -1.0, affine[:, 1:2], ALU.mult, ALU.add))
            for g in range(GROUPS):
                b = g // (GROUPS // B)
                dve.tensor_scalar(y[:, g * GROUP:(g + 1) * GROUP], retained[:, g * GROUP:(g + 1) * GROUP], scale[:, b:b + 1], shift[:, b:b + 1],
                                  ALU.mult, ALU.add).then_inc(normed, 1)
            for g in range(GROUPS):
                dve.wait_ge(out_done, g + 1)
                dve.tensor_copy(chip.yT[:, g * GROUP:(g + 1) * GROUP], psum[:, g, :])

        @block.scalar
        def _(act):
            act.wait_ge(var_done, 1)
            act.activation(var_of[:, :], var_of[:, :], ACT.Sqrt).then_inc(std_done, 1)


def window_attention(chip):
    with Stage(chip, "window") as outer:
        qT, kT = outer.sb("qT", [P, TOK]), outer.sb("kT", [P, TOK])
        v_tok = outer.sb("v_tok", [P, TILES, P])
        project_stage(chip, "window_in", ("win_wq", "win_wk", "win_wv"), (qT, kT), (v_tok,), ("win_bias_qk", "win_bias_v"))
        attended = outer.sb("attended", [P, TOK])
        window_chunks(chip, qT, kT, v_tok, attended)
        output_stage(chip, "window_out", attended, "win_wo", "win_bo")


def window_chunks(chip, qT, kT, v_tok, attended):
    with Stage(chip, "window_chunks") as st:
        slope = st.sb("slope", [P, ROWS, 2, SLOTS, P])
        slot = st.sb("slot", [P, SLOTS])
        slot_cols = st.sb("slot_cols", [P, SLOTS, P])
        keys = [st.sb(f"keys{p}", [P, 2, SLOTS, P]) for p in range(2)]
        qc = [st.sb(f"qc{p}", [P, P]) for p in range(2)]
        vals = [st.sb(f"vals{p}", [P, 2, SLOTS, P]) for p in range(2)]
        biased = [st.sb(f"biased{p}", [P, 2, SLOTS, P]) for p in range(2)]
        expd = [st.sb(f"expd{p}", [P, 2, SLOTS, P]) for p in range(2)]
        probsT = [st.sb(f"probsT{p}", [P, 2, SLOTS, P]) for p in range(2)]
        low = st.sb("low", [P, 2, SLOTS])
        sums = st.sb("sums", [P, 2, H])
        inverse = st.sb("inverse", [P, H])
        spread_inv = [st.sb(f"spread_inv{p}", [P, H, DH0]) for p in range(2)]
        inverseT = st.sb("inverseT", [P, 2, P])
        loaded = st.sem("loaded")
        prepared, prepared_v = st.sem("prepared"), st.sem("prepared_v")
        scores_done = st.sem("scores_done", ahead=2 * ROWS)
        biased_done = st.sem("biased_done", ahead=2)
        max_done = st.sem("max_done")
        exp_done = st.sem("exp_done", ahead=2 * SLOTS)
        turned = st.sem("turned", ahead=2)
        own_ready = st.sem("own_ready", ahead=1)
        other_ready = st.sem("other_ready", ahead=1)
        used = st.sem("used", ahead=2 * ROWS)
        inverse_done, spread_done = st.sem("inverse_done"), st.sem("spread_done", ahead=1)
        inverse_turned, inverse_copied = st.sem("inverse_turned", ahead=2), st.sem("inverse_copied")
        y_done = st.sem("y_done", ahead=2)
        block = st.block()
        psum = chip.psum

        def tile_loop(eng, body):
            with eng.Fori(0, B) as b:
                body(b, 0, 0, True, False, False)
                body(b, 1, 1, False, True, False)
                with eng.Fori(1, PER_B // 2 - 1) as pair:
                    body(b, pair * 2, 0, False, False, False)
                    body(b, pair * 2 + 1, 1, False, False, False)
                body(b, PER_B - 2, 0, False, False, False)
                body(b, PER_B - 1, 1, False, False, True)

        def later(b, c, p, r, first, last, steps):
            if r + steps < ROWS:
                return b, c, p, r + steps, first
            return None if last else (b, c + 1, 1 - p, r + steps - ROWS, False)

        def place(first, a, h):
            return (h // 2, h % 2) if first else (a, h)

        def half_of(buf, first, half):
            return buf[:, half, 0:2 if first else SLOTS, :].rearrange("p s i -> p (s i)")

        def half_of_bank(first, half):
            return psum[:, 4 + half, 0:2 * P if first else SLOTS * P]

        @block.sync
        def _(sp):
            sp.dma_start(slope[:, :, :, :, :].rearrange("p r a s j -> p (r a s j)"), chip.dram["win_slope"]).then_inc(loaded, 16)
            sp.dma_start(slot[:, :], chip.dram["slot"]).then_inc(loaded, 16)
            sp.dma_start(slot_cols[:, :, :], chip.dram["slot_cols"]).then_inc(loaded, 16)

        @block.gpsimd
        def _(pool):
            pool.wait_ge(loaded, 48)

            def prepare(b, c, p, first):
                n = b * PER_B + c
                cols = bass.ts(n, P)
                pool.wait_ge(scores_done, (n + 1) * ROWS)
                pool.tensor_copy(qc[p][:, :], qT[:, cols])
                for a in range(1 if first else 2):
                    last = pool.tensor_tensor(keys[p][:, a, :, :], kT[:, bass.ts(n - a, P)].unsqueeze(1).to_broadcast([P, SLOTS, P]),
                                              slot[:, :].unsqueeze(2).to_broadcast([P, SLOTS, P]), ALU.mult)
                last.then_inc(prepared, 1)
                pool.wait_ge(used, (n + 1) * ROWS)
                for a in range(1 if first else 2):
                    last = pool.tensor_tensor(vals[p][:, a, :, :], v_tok[:, bass.ds(n - a, 1), :].to_broadcast([P, SLOTS, P]),
                                              slot_cols[:, :, :], ALU.mult)
                last.then_inc(prepared_v, 1)

            tile_loop(pool, lambda b, c, p, first, second, last: prepare(b, c, p, first))

        @block.tensor
        def _(pe):
            def scores(b, c, p, r, first):
                n = b * PER_B + c
                s = n * ROWS + r
                if r == 0:
                    pe.wait_ge(prepared, n + 1)
                pe.wait_ge(biased_done, s + 1)
                rows = slice(32 * r, 32 * r + 32)
                for a in range(1 if first else 2):
                    mm = pe.matmul(psum[:, r % 2 * 2 + a, :], qc[p][rows, :],
                                   keys[p][rows, a, :, :].rearrange("p s j -> p (s j)"), start=True, stop=True)
                mm.then_inc(scores_done, 1)

            def turn(b, c, p, r, first):
                s = (b * PER_B + c) * ROWS + r
                pe.wait_ge(exp_done, (s + 3) * SLOTS)
                pe.wait_ge(own_ready, s + 1)
                pe.wait_ge(other_ready, s + 1)
                for a in range(1 if first else 2):
                    for h in range(SLOTS):
                        bank, col = place(first, a, h)
                        mm = nc_t(pe, psum[:, 4 + bank, col * P:(col + 1) * P], expd[r % 2][:, a, h, :], chip)
                mm.then_inc(turned, 1)

            def times_v(b, c, p, r, first):
                n = b * PER_B + c
                s = n * ROWS + r
                if r == 0:
                    pe.wait_ge(prepared_v, n + 1)
                    pe.wait_ge(y_done, n + 1)
                pe.wait_ge(own_ready, s + 2)
                pe.wait_ge(other_ready, s + 2)
                rows = slice(32 * r, 32 * r + 32)
                blocks = 1 if first else 2
                for a in range(blocks):
                    for h in range(SLOTS):
                        half, col = place(first, a, h)
                        mm = pe.matmul(psum[rows, 6 + p, 0:P], vals[p][:, a, h, rows], probsT[r % 2][:, half, col, :],
                                       start=(a == 0 and h == 0), stop=(a == blocks - 1 and h == SLOTS - 1))
                mm.then_inc(used, 1)

            def finish(b, c, p, first):
                n = b * PER_B + c
                times_v(b, c, p, ROWS - 1, first)
                pe.wait_ge(spread_done, n + 2)
                nc_t(pe, psum[:, 6 + p, P:2 * P], spread_inv[p][:, :, :].rearrange("p h e -> p (h e)"),
                     chip).then_inc(inverse_turned, 1)

            def tile(b, c, p, first, second, last):
                if first:
                    scores(b, c, p, 0, True)
                    scores(b, c, p, 1, True)
                for r in range(ROWS):
                    ahead = later(b, c, p, r, first, last, 2)
                    if ahead:
                        scores(*ahead)
                    turn(b, c, p, r, first)
                    if r > 0:
                        times_v(b, c, p, r - 1, first)
                    elif not first:
                        finish(b, c - 1, 1 - p, second)
                if last:
                    finish(b, c, p, False)

            tile_loop(pe, tile)

        @block.vector
        def _(dve):
            dve.wait_ge(loaded, 48)

            def bias_and_max(b, c, p, r, first):
                s = (b * PER_B + c) * ROWS + r
                dve.wait_ge(scores_done, s + 1 + 2 * ROWS)
                dve.wait_ge(exp_done, (s + 1) * SLOTS)
                blocks = 1 if first else 2
                for a in range(blocks):
                    last = dve.scalar_tensor_tensor(
                        biased[r % 2][:, a, :, :].rearrange("p s j -> p (s j)"), psum[:, r % 2 * 2 + a, :], float(DH0) ** -0.5,
                        slope[:, r, a, :, :].rearrange("p s j -> p (s j)"), ALU.mult, ALU.add)
                last.then_inc(biased_done, 1)
                dve.wait_ge(biased_done, s + 3)
                dve.tensor_reduce(low[:, r % 2, :], biased[r % 2][:, 0:blocks, :, :].rearrange("p a s j -> p s a j"),
                                  mybir.AxisListType.XY, ALU.max, negate=True).then_inc(max_done, 1)

            def copy_turned(b, c, p, r, first):
                s = (b * PER_B + c) * ROWS + r
                dve.wait_ge(turned, s + 3)
                dve.wait_ge(used, s + 7)
                dve.tensor_copy(half_of(probsT[r % 2], first, 0), half_of_bank(first, 0)).then_inc(own_ready, 1)

            def invert(b, c, p):
                n = b * PER_B + c
                dve.wait_ge(exp_done, (n + 1) * ROWS * SLOTS + 2 * SLOTS)
                dve.wait_ge(spread_done, n + 1)
                dve.reciprocal(inverse[:, :], sums[:, p, :]).then_inc(inverse_done, 1)
                dve.wait_ge(inverse_done, n + 1)
                dve.wait_ge(inverse_turned, n + 1)
                dve.tensor_copy(spread_inv[p][:, :, :], inverse[:, :].unsqueeze(2).to_broadcast([P, H, DH0])).then_inc(
                    spread_done, 1)

            def finish(b, c, p):
                n = b * PER_B + c
                dve.wait_ge(used, (n + 3) * ROWS)
                dve.wait_ge(inverse_copied, n + 1)
                dve.tensor_tensor(attended[:, bass.ts(n, P)], psum[:, 6 + p, 0:P], inverseT[:, p, :],
                                  ALU.mult).then_inc(y_done, 1)

            def tile(b, c, p, first, second, last):
                if first:
                    bias_and_max(b, c, p, 0, True)
                    bias_and_max(b, c, p, 1, True)
                for r in range(ROWS):
                    ahead = later(b, c, p, r, first, last, 2)
                    if ahead:
                        bias_and_max(*ahead)
                    copy_turned(b, c, p, r, first)
                    if r == 1 and not first:
                        finish(b, c - 1, 1 - p)
                invert(b, c, p)
                if last:
                    finish(b, c, p)

            tile_loop(dve, tile)

        @block.scalar
        def _(act):
            def exponentials(b, c, p, r, first):
                s = (b * PER_B + c) * ROWS + r
                act.wait_ge(max_done, s + 1)
                act.wait_ge(turned, s + 1)
                for h in range(SLOTS):
                    act.activation(expd[r % 2][:, 0:1 if first else 2, h, :], biased[r % 2][:, 0:1 if first else 2, h, :], ACT.Exp,
                                   bias=low[:, r % 2, h:h + 1],
                                   accum_out=sums[:, p, r * SLOTS + h:r * SLOTS + h + 1]).then_inc(exp_done, 1)

            def copy_turned(b, c, p, r, first):
                s = (b * PER_B + c) * ROWS + r
                act.wait_ge(turned, s + 3)
                act.wait_ge(used, s + 7)
                act.copy(half_of(probsT[r % 2], first, 1), half_of_bank(first, 1)).then_inc(other_ready, 1)

            def copy_inverse(b, c, p):
                n = b * PER_B + c
                act.wait_ge(inverse_turned, n + 3)
                act.wait_ge(y_done, n + 1)
                act.copy(inverseT[:, p, :], psum[:, 6 + p, P:2 * P]).then_inc(inverse_copied, 1)

            def tile(b, c, p, first, second, last):
                if first:
                    exponentials(b, c, p, 0, True)
                for r in range(ROWS):
                    ahead = later(b, c, p, r, first, last, 1)
                    if ahead:
                        exponentials(*ahead)
                    copy_turned(b, c, p, r, first)
                    if r == 0 and not first:
                        copy_inverse(b, c - 1, 1 - p)
                if last:
                    copy_inverse(b, c, p)

            tile_loop(act, tile)


WIDE = 64
HID = H * WIDE
BLOCKS = HID // P
RMS_EPS = 2.0 ** -23


def gated_attention(chip):
    with Stage(chip, "gla") as outer:
        reach = outer.sb("reach", [P, TILES, H])
        gained = outer.sb("gained", [P, TILES, H])
        left = outer.sb("left", [P, TILES, H])
        whole = outer.sb("whole", [P, TILES, BLOCKS])
        reach_rows = chip.nc.dram_tensor("reach_rows", (H, TOK), F32).ap()
        decay_stage(chip, reach, gained, left, whole, reach_rows)
        gated_chunks(chip, reach, gained, left, whole, reach_rows)


def decay_stage(chip, reach, gained, left, whole, reach_rows):
    N = TILES * H
    with Stage(chip, "decay") as st:
        wd = st.sb("wd", [P, H])
        bd = st.sb("bd", [P, H])
        sums = st.sb("sums", [P, 3, P])
        z, size, log1p, g = (st.sb(n, [P, TILES, H]) for n in ("z", "size", "log1p", "g"))
        reachT = st.sb("reachT", [H, TOK])
        loaded, logits_done, own = st.sem("loaded"), st.sem("logits_done"), st.sem("dve_steps")
        asked, answered = st.sem("asked"), st.sem("answered")
        g_done, sums_done, copied = st.sem("g_done"), st.sem("sums_done"), st.sem("copied")
        turned, stored, rows_copied = st.sem("turned"), st.sem("stored"), st.sem("rows_copied")
        block = st.block()
        psum = chip.psum
        logits = psum[:, 0, 0:N].rearrange("p (t h) -> p t h", h=H)

        @block.sync
        def _(sp):
            sp.dma_start(wd[:, :], chip.dram["gla_wd"]).then_inc(loaded, 16)
            sp.dma_start(bd[:, :], chip.dram["gla_bd"]).then_inc(loaded, 16)
            sp.dma_start(sums[:, :, :], chip.dram["gla_sums"]).then_inc(loaded, 16)
            sp.wait_ge(rows_copied, 4)
            sp.dma_start(reach_rows, reachT[:, :]).then_inc(stored, 16)
            sp.wait_ge(stored, 16)

        @block.tensor
        def _(pe):
            pe.wait_ge(loaded, 48)
            for t in range(TILES):
                mm = pe.matmul(logits[:, t, :], chip.xnT[:, t * P:(t + 1) * P], wd[:, :], start=True, stop=True)
            mm.then_inc(logits_done, 1)
            pe.wait_ge(g_done, 1)
            for k in range(3):
                mm = pe.matmul(psum[:, 1 + k, 0:N], sums[:, k, :], g[:, :, :].rearrange("p t h -> p (t h)"), start=True, stop=True)
            mm.then_inc(sums_done, 1)
            pe.wait_ge(copied, 1)
            for t in range(TILES):
                turn = nc_t(pe, psum[0:H, 4 + t // 4, t % 4 * P:(t % 4 + 1) * P], reach[:, t, :], chip)
                if t % 4 == 3:
                    turn.then_inc(turned, 1)

        @block.vector
        def _(dve):
            done = Chain(dve, own).done
            dve.wait_ge(logits_done, 1)
            done(dve.tensor_tensor(z[:, :, :], logits, bd[:, :].unsqueeze(1).to_broadcast([P, TILES, H]), ALU.add))
            done(dve.tensor_scalar(size[:, :, :], z[:, :, :], -1.0, None, ALU.mult))
            dve.tensor_tensor(size[:, :, :], size[:, :, :], z[:, :, :], ALU.min).then_inc(asked, 1)
            dve.wait_ge(answered, 1)
            dve.tensor_scalar(log1p[:, :, :], log1p[:, :, :], 1.0, None, ALU.add).then_inc(asked, 1)
            dve.wait_ge(answered, 2)
            done(dve.scalar_tensor_tensor(g[:, :, :], z[:, :, :], 0.0, log1p[:, :, :], ALU.max, ALU.add))
            dve.tensor_scalar(g[:, :, :], g[:, :, :], -1.0, None, ALU.mult).then_inc(g_done, 1)
            dve.wait_ge(sums_done, 1)
            dve.tensor_copy(reach[:, :, :].rearrange("p t h -> p (t h)"), psum[:, 1, 0:N]).then_inc(copied, 1)
            for q in range(4):
                dve.wait_ge(turned, q + 1)
                dve.tensor_copy(reachT[:, q * GROUP:(q + 1) * GROUP], psum[0:H, 4 + q, :]).then_inc(rows_copied, 1)

        @block.scalar
        def _(act):
            act.wait_ge(asked, 1)
            act.activation(log1p[:, :, :], size[:, :, :], ACT.Exp).then_inc(answered, 1)
            act.wait_ge(asked, 2)
            act.activation(log1p[:, :, :], log1p[:, :, :], ACT.Ln).then_inc(answered, 1)
            act.wait_ge(sums_done, 1)
            act.activation(left[:, :, :].rearrange("p t h -> p (t h)"), psum[:, 2, 0:N], ACT.Exp)
            pairs = psum[:, 3, 0:N].rearrange("p (t m two) -> p t m two", m=BLOCKS, two=2)
            for half in range(2):
                rows = slice(half * WIDE, (half + 1) * WIDE)
                act.activation(whole[rows, :, :], pairs[rows, :, :, half], ACT.Exp)
            act.wait_ge(copied, 1)
            act.activation(gained[:, :, :], reach[:, :, :], ACT.Exp)


def rows_of_chunks(eng, start, chunk):
    with eng.Fori(0, B) as b:
        start(b)
        with eng.Fori(0, PER_B // 2 - 1) as pair:
            for p in range(2):
                chunk(b, b * PER_B + pair * 2 + p, p, False)
        for p in range(2):
            chunk(b, b * PER_B + PER_B - 2 + p, p, p == 1)


def by_head(buf, width=WIDE):
    return buf[:, :].rearrange("p (h e) -> p h e", e=width)


def spread(v, width=WIDE):
    return v[:, :].unsqueeze(2).to_broadcast([P, v.shape[1], width])


def head_of(k):
    return k // 8 * 8 + k % 4 * 2 + k // 4 % 2


def gated_chunks(chip, reach, gained, left, whole, reach_rows):
    with Stage(chip, "gla_chunks") as st:
        def count(name):
            return st.sem(name, ahead=1)

        w_tok = st.sb("w_tok", [P, 4, HID])
        wq = st.sb("wq", [P, HID])
        wo = st.sb("wo", [P, BLOCKS, D])
        norm_w = st.sb("norm_w", [P, BLOCKS])
        causal = st.sb("causal", [P, P])
        xc = [st.sb(f"xc{p}", [P, P]) for p in range(2)]
        reach_c, gained_c, left_c = (st.sb(n, [P, H]) for n in ("reach_c", "gained_c", "left_c"))
        whole_c = st.sb("whole_c", [P, BLOCKS])
        reach_bc = st.sb("reach_bc", [P, H, P])
        gate, k_tok, v_tok, v_left, og, o, square = (
            st.sb(n, [P, HID]) for n in ("gate", "k_tok", "v_tok", "v_left", "og", "o", "square"))
        qT, kT, oT = (st.sb(n, [P, BLOCKS, P]) for n in ("qT", "kT", "oT"))
        decay, probs = st.sb("decay", [P, H, P]), st.sb("probs", [P, H, P])
        power, rstd = st.sb("power", [P, 1]), st.sb("rstd", [P, 1])
        state = st.sb("state", [P, BLOCKS, WIDE])
        loaded = st.sem("loaded")
        x_in = count("x_in")
        small_in = count("small_in")
        rows_in = st.sem("rows_in")
        k_done, gate_done, v_done, og_done, q_done = (count(n + "_done") for n in ("k", "gate", "v", "og", "q"))
        gate_ready, k_ready, v_ready, og_ready, q_ready = (count(n + "_ready") for n in ("gate", "k", "v", "og", "q"))
        kt_done, kt_ready = count("kt_done"), count("kt_ready")
        arg_done, decay_done = count("arg_done"), count("decay_done")
        score_done, probs_done = count("score_done"), count("probs_done")
        v_left_done, past_done, past_read = count("v_left_done"), count("past_done"), count("past_read")
        intra_done, o_done = count("intra_done"), count("o_done")
        update_done, decayed = count("update_done"), count("decayed")
        state_done = count("state_done")
        power_done, shifted, std_done, rstd_done = (count(n) for n in ("power_done", "shifted", "std_done", "rstd_done"))
        o_ready, ot_done, ot_ready, y_done, y_read = (count(n) for n in ("o_ready", "ot_done", "ot_ready", "y_done", "y_read"))
        block = st.block()
        psum = chip.psum
        R = 4

        def two(n):
            return psum[:, n:n + 2, :].rearrange("p a f -> p (a f)")

        k_ps, q_ps, gate_ps, past_ps, oT_ps = two(0), two(0), two(2), two(2), two(2)
        v_ps, kT_ps, intra_ps, og_ps = two(4), two(4), two(4), two(6)
        score_ps = [psum[:, m, :] for m in (0, 1, 6, 7)]
        update_ps = psum[:, 0, :].rearrange("p (m e) -> p m e", e=WIDE)
        y_ps = psum[:, 2, 0:P]

        @block.sync
        def _(sp):
            for k, nm in enumerate(("gla_wk", "gla_wg", "gla_wv", "gla_wog")):
                sp.dma_start(w_tok[:, k, :], chip.dram[nm]).then_inc(loaded, 16)
            for buf, nm in ((wq[:, :], "gla_wq"), (wo[:, :, :], "gla_wo"), (norm_w[:, :], "gla_norm_w"), (causal[:, :], "causal")):
                sp.dma_start(buf, chip.dram[nm]).then_inc(loaded, 16)
            with sp.Fori(0, TILES) as n:
                sp.wait_ge(arg_done, n + 1)
                sp.dma_start(reach_bc[:, :, :], reach_rows[:, bass.ts(n, P)].unsqueeze(0).to_broadcast([P, H, P])).then_inc(rows_in, 16)

        @block.gpsimd
        def _(pool):
            pool.wait_ge(loaded, 128)
            with pool.Fori(0, TILES // 2) as pair:
                for p in range(2):
                    n = pair * 2 + p
                    pool.wait_ge(past_done, n + 1)
                    pool.tensor_copy(xc[p][:, :], chip.xnT[:, bass.ts(n, P)]).then_inc(x_in, 1)
                    pool.wait_ge(arg_done, n + 1)
                    pool.wait_ge(past_read, n + 1)
                    pool.wait_ge(v_left_done, n + 1)
                    pool.wait_ge(decayed, n + 1)
                    for dst, src in ((reach_c, reach), (gained_c, gained), (left_c, left), (whole_c, whole)):
                        last = pool.tensor_copy(dst[:, :], src[:, bass.ds(n, 1), :].rearrange("p a h -> p (a h)"))
                    last.then_inc(small_in, 1)
                    pool.wait_ge(small_in, n + 2)
                    pool.wait_ge(v_ready, n + 2)
                    pool.wait_ge(update_done, n + 1)
                    pool.tensor_tensor(by_head(v_left), by_head(v_tok), spread(left_c), ALU.mult).then_inc(v_left_done, 1)

        @block.tensor
        def _(pe):
            pe.wait_ge(loaded, 128)

            def token_major(out, which, p):
                for half in range(2):
                    cols = slice(half * GROUP, (half + 1) * GROUP)
                    mm = pe.matmul(out[:, cols], xc[p][:, :], w_tok[:, which, cols], start=True, stop=True)
                return mm

            def ahead(b, n, p):
                pe.wait_ge(x_in, n + 2)
                pe.wait_ge(state_done, n + b + 2)
                token_major(k_ps, 0, p).then_inc(k_done, 1)
                pe.wait_ge(probs_done, n * R + 1)
                token_major(og_ps, 3, p).then_inc(og_done, 1)
                pe.wait_ge(o_done, n + 1)
                token_major(v_ps, 2, p).then_inc(v_done, 1)

            def chunk(b, n, p, last):
                pe.wait_ge(y_read, n + 1)
                token_major(gate_ps, 1, p).then_inc(gate_done, 1)
                pe.wait_ge(k_ready, n + 2)
                for m in range(BLOCKS):
                    mm = pe.matmul(q_ps[:, m * P:(m + 1) * P], wq[:, m * P:(m + 1) * P], xc[p][:, :], start=True, stop=True)
                mm.then_inc(q_done, 1)
                pe.wait_ge(v_ready, n + 2)
                for m in range(BLOCKS):
                    mm = nc_t(pe, kT_ps[:, m * P:(m + 1) * P], k_tok[:, m * P:(m + 1) * P], chip)
                mm.then_inc(kt_done, 1)
                pe.wait_ge(q_ready, n + 2)
                pe.wait_ge(state_done, n + b + 2)
                for h in range(H):
                    rows = slice(h % 2 * WIDE, h % 2 * WIDE + WIDE)
                    place = (h % 2 * BLOCKS + h // 2) * WIDE
                    mm = pe.matmul(past_ps[:, place:place + WIDE], qT[rows, h // 2, :], state[rows, h // 2, :],
                                   start=True, stop=True)
                mm.then_inc(past_done, 1)
                pe.wait_ge(kt_ready, n + 2)
                for k in range(H):
                    if k == H // 2:
                        pe.wait_ge(og_ready, n + 2)
                    r, s = k // (2 * R) * 2 + k % 2, k // 2 % R
                    h = head_of(r * R + s)
                    rows = slice(h % 2 * WIDE, h % 2 * WIDE + WIDE)
                    mm = pe.matmul(score_ps[r][:, s * P:(s + 1) * P], kT[rows, h // 2, :], qT[rows, h // 2, :],
                                   start=True, stop=True)
                    if s == R - 1:
                        mm.then_inc(score_done, 1)
                pe.wait_ge(v_left_done, n + 2)
                pe.wait_ge(probs_done, n * R + 2)
                for h in range(H):
                    rows = slice(h % 2 * WIDE, h % 2 * WIDE + WIDE)
                    cols = slice(h * WIDE, (h + 1) * WIDE)
                    mm = pe.matmul(update_ps[rows, h // 2, :], k_tok[:, cols], v_left[:, cols], start=True, stop=True)
                mm.then_inc(update_done, 1)
                for k in range(H):
                    if k % R == 0:
                        pe.wait_ge(probs_done, n * R + k // R + 2)
                    h = head_of(k)
                    cols = slice(h * WIDE, (h + 1) * WIDE)
                    mm = pe.matmul(intra_ps[:, cols], probs[:, k, :], v_tok[:, cols], start=True, stop=True)
                mm.then_inc(intra_done, 1)
                if not last:
                    ahead(b, n + 1, 1 - p)
                pe.wait_ge(o_ready, n + 2)
                for m in range(BLOCKS):
                    mm = nc_t(pe, oT_ps[:, m * P:(m + 1) * P], o[:, m * P:(m + 1) * P], chip)
                mm.then_inc(ot_done, 1)
                pe.wait_ge(ot_ready, n + 2)
                for m in range(BLOCKS):
                    mm = pe.matmul(y_ps, wo[:, m, :], oT[:, m, :], start=(m == 0), stop=(m == BLOCKS - 1))
                mm.then_inc(y_done, 1)

            rows_of_chunks(pe, lambda b: ahead(b, b * PER_B, 0), chunk)

        @block.vector
        def _(dve):
            dve.wait_ge(loaded, 128)

            def decay_args(n):
                dve.wait_ge(small_in, n + 2)
                dve.wait_ge(rows_in, (n + 1) * 16)
                dve.wait_ge(probs_done, n * R + 1)
                for k in range(H):
                    h = head_of(k)
                    last = dve.scalar_tensor_tensor(decay[:, k, :], reach_bc[:, h, :], reach_c[:, h:h + 1], causal[:, :],
                                                    ALU.subtract, ALU.add)
                last.then_inc(arg_done, 1)

            def take_v(n):
                dve.wait_ge(v_done, n + 2)
                dve.wait_ge(intra_done, n + 1)
                dve.wait_ge(v_left_done, n + 1)
                dve.tensor_copy(v_tok[:, :], v_ps).then_inc(v_ready, 1)

            def start(b):
                dve.wait_ge(past_done, b * PER_B + 1)
                dve.wait_ge(state_done, b * (PER_B + 1) + 1)
                dve.memset(state[:, :, :], 0.0).then_inc(state_done, 1)
                decay_args(b * PER_B)
                take_v(b * PER_B)

            def chunk(b, n, p, last):
                dve.wait_ge(gate_ready, n + 2)
                dve.wait_ge(update_done, n + 1)
                dve.tensor_tensor(k_tok[:, :], gate[:, :], k_ps, ALU.mult).then_inc(k_ready, 1)
                dve.wait_ge(kt_done, n + 2)
                dve.tensor_copy(kT[:, :, :].rearrange("p m i -> p (m i)"), kT_ps).then_inc(kt_ready, 1)
                dve.wait_ge(past_done, n + 2)
                dve.wait_ge(small_in, n + 2)
                dve.wait_ge(ot_done, n + 1)
                dve.tensor_tensor(by_head(o).rearrange("p (m two) e -> p m two e", two=2),
                                  past_ps.rearrange("p (two m e) -> p m two e", two=2, e=WIDE),
                                  spread(gained_c).rearrange("p (m two) e -> p m two e", two=2), ALU.mult).then_inc(past_read, 1)
                dve.wait_ge(decay_done, n + 2)
                for r in range(R):
                    dve.wait_ge(score_done, n * R + r + 2)
                    dve.wait_ge(intra_done, n + 1)
                    heads = slice(r * R, (r + 1) * R)
                    dve.tensor_tensor(probs[:, heads, :].rearrange("p s i -> p (s i)"), score_ps[r],
                                      decay[:, heads, :].rearrange("p s i -> p (s i)"), ALU.mult).then_inc(probs_done, 1)
                dve.wait_ge(state_done, n + b + 2)
                dve.tensor_tensor(state[:, :, :], state[:, :, :], spread(whole_c), ALU.mult).then_inc(decayed, 1)
                dve.wait_ge(update_done, n + 2)
                dve.wait_ge(decayed, n + 2)
                dve.tensor_tensor(state[:, :, :], state[:, :, :], update_ps, ALU.add).then_inc(state_done, 1)
                dve.wait_ge(intra_done, n + 2)
                dve.wait_ge(past_read, n + 2)
                dve.tensor_tensor(o[:, :], o[:, :], intra_ps, ALU.add).then_inc(o_done, 1)
                dve.wait_ge(power_done, n + 2)
                dve.tensor_scalar(rstd[:, :], power[:, :], 1.0 / HID, RMS_EPS, ALU.mult, ALU.add).then_inc(shifted, 1)
                dve.wait_ge(std_done, n + 2)
                dve.reciprocal(rstd[:, :], rstd[:, :]).then_inc(rstd_done, 1)
                dve.wait_ge(rstd_done, n + 2)
                dve.wait_ge(og_ready, n + 2)
                dve.scalar_tensor_tensor(o[:, :], o[:, :], rstd[:, 0:1], og[:, :], ALU.mult, ALU.mult).then_inc(o_ready, 1)
                if not last:
                    take_v(n + 1)
                dve.wait_ge(ot_done, n + 2)
                dve.wait_ge(y_done, n + 1)
                dve.tensor_tensor(oT[:, :, :], oT_ps.rearrange("p (m i) -> p m i", i=P), spread(norm_w, P),
                                  ALU.mult).then_inc(ot_ready, 1)
                if not last:
                    decay_args(n + 1)

            rows_of_chunks(dve, start, chunk)

        @block.scalar
        def _(act):
            def take_og(n):
                act.wait_ge(og_done, n + 2)
                act.wait_ge(o_ready, n + 1)
                act.activation(og[:, :], og_ps, ACT.Sigmoid).then_inc(og_ready, 1)

            def chunk(b, n, p, last):
                act.wait_ge(gate_done, n + 2)
                act.wait_ge(k_ready, n + 1)
                act.activation(gate[:, :], gate_ps, ACT.Sigmoid).then_inc(gate_ready, 1)
                act.wait_ge(q_done, n + 2)
                act.wait_ge(score_done, n * R + 1)
                act.copy(qT[:, :, :].rearrange("p m i -> p (m i)"), q_ps).then_inc(q_ready, 1)
                act.wait_ge(arg_done, n + 2)
                act.activation(decay[:, :, :], decay[:, :, :], ACT.Exp).then_inc(decay_done, 1)
                act.wait_ge(o_done, n + 2)
                act.activation(square[:, :], o[:, :], ACT.Square, accum_out=power[:, :]).then_inc(power_done, 1)
                act.wait_ge(shifted, n + 2)
                act.activation(rstd[:, :], rstd[:, :], ACT.Sqrt).then_inc(std_done, 1)
                if not last:
                    take_og(n + 1)
                act.wait_ge(y_done, n + 2)
                act.copy(chip.yT[:, bass.ts(n, P)], y_ps).then_inc(y_read, 1)

            rows_of_chunks(act, lambda b: take_og(b * PER_B), chunk)


FINITE = 3e38
R_BANKS, R_HEADS = 4, 4


def feature_attention(chip):
    W1 = WIDE + 1
    with Stage(chip, "features") as st:
        def count(name):
            return st.sem(name, ahead=1)

        wq, wk, wv = (st.sb(n, [P, HID]) for n in ("wq", "wk", "wv"))
        wo = st.sb("wo", [P, BLOCKS, D])
        bo = st.sb("bo", [P, 1])
        omega = st.sb("omega", [P, P])
        half_norm = st.sb("half_norm", [P, P])
        allowed = st.sb("allowed", [P, P])
        xc = [st.sb(f"xc{p}", [P, P]) for p in range(2)]
        qT, kT, q2, k2, phi_q, phi_k, oT = (st.sb(n, [P, BLOCKS, P]) for n in ("qT", "kT", "q2", "k2", "phi_q", "phi_k", "oT"))
        k_tok, o = st.sb("k_tok", [P, HID]), st.sb("o", [P, H, WIDE])
        v_tok = st.sb("v_tok", [P, H, W1])
        probs = st.sb("probs", [P, H, P])
        z = st.sb("z", [P, R_BANKS, R_HEADS])
        state = st.sb("state", [P, BLOCKS, W1])
        loaded, ones_done, x_in = st.sem("loaded"), st.sem("ones_done"), count("x_in")
        q_done, k_done, v_done = count("q_done"), count("k_done"), count("v_done")
        q_ready, k_ready, v_ready = count("q_ready"), count("k_ready"), count("v_ready")
        squares = count("squares")
        arg_done, phi_ready = count("arg_done"), count("phi_ready")
        kt_done, kt_ready = count("kt_done"), count("kt_ready")
        score_done, probs_done = count("score_done"), count("probs_done")
        past_done, update_done = count("past_done"), count("update_done")
        state_done = count("state_done")
        out_done, z_steps, o_ready = count("out_done"), count("z_steps"), count("o_ready")
        ot_done, ot_ready, y_done, y_read = count("ot_done"), count("ot_ready"), count("y_done"), count("y_read")
        block = st.block()
        psum = chip.psum
        R = R_BANKS

        def two(n):
            return psum[:, n:n + 2, :].rearrange("p a f -> p (a f)")

        q_ps, k_ps, v_ps, kt_ps, oT_ps = two(0), two(2), two(4), two(6), two(6)
        out_ps = psum[:, 4:8, 0:R_HEADS * W1].rearrange("p r (s w) -> p r s w", w=W1)
        update_ps = psum[:, 0:2, 0:R_HEADS * W1].rearrange("p a (m w) -> p a m w", w=W1)
        y_ps = psum[:, 6, 0:P]

        def flat(buf):
            return buf[:, :, :].rearrange("p m i -> p (m i)")

        @block.sync
        def _(sp):
            for buf, nm in ((wq[:, :], "fea_wq"), (wk[:, :], "fea_wk"), (wv[:, :], "fea_wv"), (wo[:, :, :], "fea_wo"),
                            (bo[:, :], "fea_bo"), (omega[:, :], "fea_omega"), (half_norm[:, :], "fea_half_norm"),
                            (allowed[:, :], "allowed")):
                sp.dma_start(buf, chip.dram[nm]).then_inc(loaded, 16)

        @block.gpsimd
        def _(pool):
            pool.memset(v_tok[:, :, :], 1.0).then_inc(ones_done, 1)
            with pool.Fori(0, TILES // 2) as pair:
                for p in range(2):
                    n = pair * 2 + p
                    pool.wait_ge(v_done, n + 1)
                    pool.tensor_copy(xc[p][:, :], chip.xnT[:, bass.ts(n, P)]).then_inc(x_in, 1)
                    for k, (ready, src, dst) in enumerate(((q_ready, qT, q2), (k_ready, kT, k2))):
                        pool.wait_ge(ready, n + 2)
                        pool.wait_ge(arg_done, 2 * n + 1)
                        pool.tensor_tensor(dst[:, :, :], src[:, :, :], src[:, :, :], ALU.mult).then_inc(squares, 1)

        @block.tensor
        def _(pe):
            pe.wait_ge(loaded, 128)

            def ahead(b, n, p):
                pe.wait_ge(x_in, n + 2)
                pe.wait_ge(state_done, n + b + 2)
                pe.wait_ge(probs_done, n * R + 1)
                for ps, w, sem in ((q_ps, wq, q_done), (k_ps, wk, k_done)):
                    for m in range(BLOCKS):
                        mm = pe.matmul(ps[:, m * P:(m + 1) * P], w[:, m * P:(m + 1) * P], xc[p][:, :], start=True, stop=True)
                    mm.then_inc(sem, 1)
                pe.wait_ge(o_ready, n + 1)
                for half in range(2):
                    cols = slice(half * GROUP, (half + 1) * GROUP)
                    mm = pe.matmul(v_ps[:, cols], xc[p][:, :], wv[:, cols], start=True, stop=True)
                mm.then_inc(v_done, 1)

            def chunk(b, n, p, last):
                for k, (ps, raw, sq) in enumerate(((q_ps, qT, q2), (k_ps, kT, k2))):
                    pe.wait_ge(squares, 2 * n + k + 2)
                    for half in range(2):
                        cols = slice(half * GROUP, (half + 1) * GROUP)
                        pe.matmul(ps[:, cols], omega[:, :], flat(raw)[:, cols], start=True, stop=False)
                        mm = pe.matmul(ps[:, cols], half_norm[:, :], flat(sq)[:, cols], start=False, stop=True)
                    mm.then_inc(arg_done, 1)
                pe.wait_ge(phi_ready, 2 * n + 3)
                pe.wait_ge(y_read, n + 1)
                for m in range(BLOCKS):
                    mm = nc_t(pe, kt_ps[:, m * P:(m + 1) * P], phi_k[:, m, :], chip)
                mm.then_inc(kt_done, 1)
                for k in range(H):
                    r, s = k // (2 * R_HEADS) * 2 + k % 2, k // 2 % R_HEADS
                    h = head_of(r * R_HEADS + s)
                    rows = slice(h % 2 * WIDE, h % 2 * WIDE + WIDE)
                    mm = pe.matmul(psum[:, r, s * P:(s + 1) * P], phi_k[rows, h // 2, :], phi_q[rows, h // 2, :],
                                   start=True, stop=True)
                    if s == R_HEADS - 1:
                        mm.then_inc(score_done, 1)
                pe.wait_ge(v_ready, n + 2)
                pe.wait_ge(kt_ready, n + 2)
                pe.wait_ge(state_done, n + b + 2)
                for k in range(H):
                    r, s = k // (2 * R_HEADS) * 2 + k % 2, k // 2 % R_HEADS
                    h = head_of(r * R_HEADS + s)
                    rows = slice(h % 2 * WIDE, h % 2 * WIDE + WIDE)
                    mm = pe.matmul(out_ps[:, r, s, :], phi_q[rows, h // 2, :], state[rows, h // 2, :],
                                   start=(s == 0), stop=False, skip_group_check=True)
                mm.then_inc(past_done, 1)
                pe.wait_ge(probs_done, n * R + 3)
                for h in range(H):
                    rows = slice(h % 2 * WIDE, h % 2 * WIDE + WIDE)
                    m = h // 2
                    mm = pe.matmul(update_ps[rows, m // R_HEADS, m % R_HEADS, :], k_tok[:, h * WIDE:(h + 1) * WIDE],
                                   v_tok[:, h, :], start=True, stop=True)
                mm.then_inc(update_done, 1)
                for k in range(H):
                    if k % R_HEADS == 0:
                        pe.wait_ge(probs_done, n * R + k // R_HEADS + 2)
                    mm = pe.matmul(out_ps[:, k // R_HEADS, k % R_HEADS, :], probs[:, k, :], v_tok[:, head_of(k), :],
                                   start=False, stop=(k % R_HEADS == R_HEADS - 1), skip_group_check=True)
                mm.then_inc(out_done, 1)
                if not last:
                    ahead(b, n + 1, 1 - p)
                pe.wait_ge(o_ready, n + 2)
                for m in range(BLOCKS):
                    mm = nc_t(pe, oT_ps[:, m * P:(m + 1) * P], o[:, 2 * m:2 * m + 2, :].rearrange("p a e -> p (a e)"), chip)
                mm.then_inc(ot_done, 1)
                pe.wait_ge(ot_ready, n + 2)
                for m in range(BLOCKS):
                    mm = pe.matmul(y_ps, wo[:, m, :], oT[:, m, :], start=(m == 0), stop=(m == BLOCKS - 1))
                mm.then_inc(y_done, 1)

            rows_of_chunks(pe, lambda b: ahead(b, b * PER_B, 0), chunk)

        @block.vector
        def _(dve):
            dve.wait_ge(loaded, 128)
            dve.wait_ge(ones_done, 1)

            def take_qk(n):
                for done, ready, ps, dst in ((q_done, q_ready, q_ps, qT), (k_done, k_ready, k_ps, kT)):
                    dve.wait_ge(done, n + 2)
                    dve.wait_ge(squares, 2 * n + 1)
                    dve.wait_ge(arg_done, 2 * n + 1)
                    dve.tensor_copy(flat(dst), ps).then_inc(ready, 1)

            def start(b):
                dve.wait_ge(past_done, b * PER_B + 1)
                dve.wait_ge(state_done, b * (PER_B + 1) + 1)
                dve.memset(state[:, :, :], 0.0).then_inc(state_done, 1)
                take_qk(b * PER_B)

            def chunk(b, n, p, last):
                dve.wait_ge(kt_done, n + 2)
                dve.wait_ge(update_done, n + 1)
                dve.tensor_copy(k_tok[:, :], kt_ps).then_inc(kt_ready, 1)
                for r in range(R):
                    dve.wait_ge(score_done, n * R + r + 2)
                    dve.wait_ge(out_done, n + 1)
                    heads = slice(r * R_HEADS, (r + 1) * R_HEADS)
                    dve.scalar_tensor_tensor(probs[:, heads, :], psum[:, r, :].rearrange("p (s i) -> p s i", i=P), FINITE,
                                             allowed[:, :].unsqueeze(1).to_broadcast([P, R_HEADS, P]), ALU.min,
                                             ALU.mult).then_inc(probs_done, 1)
                dve.wait_ge(update_done, n + 2)
                dve.wait_ge(past_done, n + 2)
                dve.wait_ge(state_done, n + b + 2)
                halves = state[:, :, :].rearrange("p (a m) w -> p a m w", a=2)
                dve.tensor_tensor(halves, halves, update_ps, ALU.add).then_inc(state_done, 1)
                dve.wait_ge(out_done, n + 2)
                dve.wait_ge(o_ready, n + 1)
                dve.tensor_scalar(z[:, :, :], out_ps[:, :, :, WIDE], WIDE * 1e-6, None, ALU.add).then_inc(z_steps, 1)
                dve.wait_ge(z_steps, 2 * n + 2)
                dve.reciprocal(z[:, :, :], z[:, :, :]).then_inc(z_steps, 1)
                dve.wait_ge(z_steps, 2 * n + 3)
                dve.wait_ge(ot_done, n + 1)
                dve.tensor_tensor(o[:, :, :].rearrange("p (r s) e -> p r s e", s=R_HEADS), out_ps[:, :, :, 0:WIDE],
                                  z[:, :, :].unsqueeze(3).to_broadcast([P, R, R_HEADS, WIDE]), ALU.mult).then_inc(o_ready, 1)
                if not last:
                    take_qk(n + 1)

            rows_of_chunks(dve, start, chunk)

        @block.scalar
        def _(act):
            act.wait_ge(loaded, 128)
            act.wait_ge(ones_done, 1)

            def chunk(b, n, p, last):
                act.wait_ge(v_done, n + 2)
                act.wait_ge(out_done, n + 1)
                act.copy(v_tok[:, :, 0:WIDE], v_ps.rearrange("p (h e) -> p h e", e=WIDE)).then_inc(v_ready, 1)
                for k, (ps, dst) in enumerate(((q_ps, phi_q), (k_ps, phi_k))):
                    act.wait_ge(arg_done, 2 * n + k + 2)
                    act.wait_ge(past_done, n + 1)
                    act.wait_ge(score_done, n * R + 1)
                    act.activation(flat(dst), ps, ACT.Exp).then_inc(phi_ready, 1)
                act.wait_ge(ot_done, n + 2)
                act.wait_ge(y_done, n + 1)
                act.copy(flat(oT), oT_ps).then_inc(ot_ready, 1)
                act.wait_ge(y_done, n + 2)
                act.activation(chip.yT[:, bass.ts(n, P)], y_ps, ACT.Identity, bias=bo[:, 0:1]).then_inc(y_read, 1)

            rows_of_chunks(act, lambda b: None, chunk)


def program(nc, dram, out, layers=None):
    with ExitStack() as ctx:
        chip = Chip(nc, dram, out, ctx)
        load_stage(chip)
        steps = [
            lambda: ffn_stage(chip, "ffn_a"), lambda: retention_attention(chip), lambda: ffn_stage(chip, "ffn_b"),
            lambda: moe1(chip, "moe1_a"), lambda: window_attention(chip), lambda: moe1(chip, "moe1_b"),
            lambda: moe2(chip, "moe2_a"), lambda: gated_attention(chip), lambda: moe2(chip, "moe2_b"),
            lambda: choice(chip, "moe3_a"), lambda: feature_attention(chip), lambda: choice(chip, "moe3_b"),
        ]
        scale = None
        for n, step in enumerate(steps):
            if layers is not None and n not in layers:
                continue
            norm_stage(chip, f"norm{n}", scale)
            step()
            scale = 1.0 if n % 3 == 1 else 0.5
        store_stage(chip, scale)


def moe1(chip, name):
    router_stage(chip, name + "_router", "moe1_router", "sum")
    experts_stage(chip, name, 512, True, ("moe1_gate", "moe1_up"), "moe1_down")


def moe2(chip, name):
    router_stage(chip, name + "_router", "moe2_router", "softmax")
    experts_stage(chip, name, 256, True, ("moe2_gate", "moe2_up"), "moe2_down")


def choice(chip, name):
    router_stage(chip, name + "_router", "moe3_router", "choice")
    experts_stage(chip, name, 512, False, ("moe3_up",), "moe3_down")


def _arrays(i):
    import numpy as np

    f = np.float32

    def chunked(w):
        return np.swapaxes(w.reshape(*w.shape[:-2], -1, P, w.shape[-1]), -3, -2)

    def column(v):
        return v.reshape(-1, P).T

    head = np.arange(D) // DH0
    gamma = 1.0 - 2.0 ** (-5.0 - np.arange(H))
    pos = np.arange(P)
    ahead = pos[None, :] - pos[:, None]
    root = np.sqrt(DH0)
    decay = np.where(ahead >= 0, gamma[:, None, None] ** np.maximum(ahead, 0), 0.0) / root
    same_head = (head[:, None] == head[None, :]).astype(f)
    start = 2.0 ** -(2.0 ** -(np.log2(H) - 3))
    slopes = np.array([start * start ** h for h in range(H)])
    FAR = -1e30
    back = pos[:, None] - pos[None, :]
    slope = np.stack([np.where(back >= 0, -back * slopes[:, None, None], FAR),
                      np.where(back < 0, -(back + P) * slopes[:, None, None], FAR)])
    slope = slope.reshape(2, ROWS, SLOTS, P, P).transpose(3, 1, 0, 2, 4).reshape(P, -1)
    upto = (ahead >= 0).astype(f)
    two = np.kron(np.eye(2, dtype=f), np.ones((WIDE, WIDE), f))
    omega = np.zeros((P, P), f)
    for k in range(2):
        omega[k * WIDE:(k + 1) * WIDE, k * WIDE:(k + 1) * WIDE] = i["L3_attn_omega"].T
    places = [head_of(k) for k in range(H)]
    wo3 = i["L3_attn_wo"].T.reshape(H, WIDE, D)[places].reshape(HID, D)
    return {
        "fea_wq": i["L3_attn_wq"].T, "fea_wk": i["L3_attn_wk"].T, "fea_wv": i["L3_attn_wv"].T, "fea_wo": chunked(wo3),
        "fea_bo": column(i["L3_attn_bo"]), "fea_omega": omega, "fea_half_norm": f(-0.5) * two, "allowed": upto,
        "gla_wd": i["L2_attn_Wd"].T, "gla_bd": np.tile(i["L2_attn_bd"], (P, 1)),
        "gla_sums": np.stack([upto, 1 - upto, np.ones_like(upto)], 1),
        "gla_wk": i["L2_attn_Wk"].T, "gla_wg": i["L2_attn_Wg"].T, "gla_wv": i["L2_attn_Wv"].T, "gla_wog": i["L2_attn_Wog"].T,
        "gla_wq": i["L2_attn_Wq"].T, "gla_wo": chunked(i["L2_attn_Wo"].T), "gla_norm_w": column(i["L2_attn_norm_w"]),
        "causal": np.where(ahead >= 0, 0.0, FAR).astype(f),
        "win_slope": slope.astype(f),
        "win_wq": i["L1_attn_wq"].T, "win_wk": i["L1_attn_wk"].T, "win_wv": i["L1_attn_wv"].T, "win_wo": i["L1_attn_wo"].T,
        "win_bias_qk": np.stack([i["L1_attn_bq"], i["L1_attn_bk"]], 1), "win_bias_v": np.tile(i["L1_attn_bv"], (P, 1)),
        "win_bo": column(i["L1_attn_bo"]),
        "same_head": same_head, "head_mean": same_head / f(DH0),
        "slot": (head[:, None] % SLOTS == np.arange(SLOTS)).astype(f),
        "slot_cols": np.tile((head[None, :] % SLOTS == np.arange(SLOTS)[:, None]).astype(f), (P, 1, 1)),
        "ret_decay": decay.transpose(1, 0, 2).astype(f),
        "ret_q_decay": (gamma[head][:, None] ** (pos + 1) / root).astype(f),
        "ret_k_decay": (gamma[head][None, :] ** (P - 1 - pos[:, None])).astype(f),
        "ret_chunk_decay": (gamma[head][:, None] ** P).astype(f),
        "ret_wq": i["L0_attn_W_q"].T, "ret_wk": i["L0_attn_W_k"].T, "ret_wv": i["L0_attn_W_v"].T, "ret_wo": i["L0_attn_W_o"].T,
        "ret_affine": np.stack([i["L0_attn_gn_weight"], i["L0_attn_gn_bias"]], 1),
        "x": i["L0_attn_x"],
        "ident": np.eye(P, dtype=f),
        "descending": np.tile(np.arange(E, 0, -1).astype(f), (P, 1)),
        "place": np.tile(np.array([2.0 ** (3 * (ROUNDS - 1 - n)) for n in range(ROUNDS)], f), (P, 1)),
        "trials": np.array([[r << 3 * (ROUNDS - 1 - n) for n in range(ROUNDS)] for r in range(TRIAL_COUNT)
                            for _ in range(B * E)], np.int32),
        "same_row": np.array([[i // (B * E) > 0 and (i - j) % (B * E) == 0 for j in range(P)] for i in range(P)], f),
        "ffn_w1": i["L0_ffn_W1"], "ffn_b1": column(i["L0_ffn_b1"]), "ffn_w2": chunked(i["L0_ffn_W2"]), "ffn_b2": column(i["L0_ffn_b2"]),
        "moe1_router": i["L1_ffn_Wr"], "moe1_gate": i["L1_ffn_Wg"], "moe1_up": i["L1_ffn_Wu"], "moe1_down": chunked(i["L1_ffn_Wd"]),
        "moe2_router": i["L2_ffn_router_kernel_DE"], "moe2_gate": i["L2_ffn_kernel_gating_EDF"],
        "moe2_up": i["L2_ffn_kernel_up_EDF"], "moe2_down": chunked(i["L2_ffn_kernel_down_EFD"]),
        "moe3_router": i["L3_ffn_gate_w"].T, "moe3_up": i["L3_ffn_w1"], "moe3_down": chunked(i["L3_ffn_w2"]),
    }


def kernel(**inputs):
    import numpy as np
    import concourse.bacc as bacc
    from concourse.bass_utils import run_bass_kernel_spmd

    nc = bacc.Bacc("TRN2", target_bir_lowering=False, num_devices=1)
    arrays, dram = {}, {}
    for name, a in _arrays({k: np.asarray(v) for k, v in inputs.items()}).items():
        arrays["in_" + name] = np.ascontiguousarray(a)
        dram[name] = nc.dram_tensor("in_" + name, a.shape, mybir.dt.from_np(a.dtype), kind="ExternalInput").ap()
    out = nc.dram_tensor("out_x", (B, T, D), F32, kind="ExternalOutput").ap()
    program(nc, dram, out)
    r = run_bass_kernel_spmd(nc, [arrays], core_ids=[0])
    return r.results[0]["out_x"]
```

```python
from contextlib import ExitStack

import concourse.bass as bass
from concourse import mybir
from concourse.alu_op_type import AluOpType as ALU

ACT = mybir.ActivationFunctionType
F32 = mybir.dt.float32
I32 = mybir.dt.int32
F32R = mybir.dt.float32r
AX_X = mybir.AxisListType.X

P = 128
B, T, D = 2, 1024, 128
TOK = B * T
TILES = TOK // P
PER_B = T // P
GROUP = 512
GROUPS = TOK // GROUP
E = 8
H = 16
EPS = 1e-5
SEMAPHORES = 150
STAGE_SEMAPHORES = 62


class Chip:

    def __init__(self, nc, dram, out, ctx):
        self.nc, self.dram, self.out, self.ctx = nc, dram, out, ctx
        self.used_semaphores = []
        sb = self.sb
        self.x = sb("x_residual", [P, TILES, D])
        self.xnT = sb("xn_features", [P, TOK])
        self.yT = sb("y_features", [P, TOK])
        self.ident = sb("ident", [P, P])
        self.psum = ctx.enter_context(nc.psum_tensor("banks", [P, 8, GROUP], F32))
        self.weights_by_expert = nc.dram_tensor("weights_by_expert", (B * E, T), F32).ap()

    def sb(self, name, shape, dtype=F32):
        return self.ctx.enter_context(self.nc.sbuf_tensor(name, shape, dtype))


class Stage:

    def __init__(self, chip, name):
        self.chip, self.nc, self.name, self.ctx = chip, chip.nc, name, ExitStack()

    def __enter__(self):
        if len(self.chip.used_semaphores) > SEMAPHORES - STAGE_SEMAPHORES:
            self.nc.clear_and_free_semaphores(self.chip.used_semaphores)
            self.nc.all_engine_barrier()
            self.chip.used_semaphores = []
        return self

    def __exit__(self, *a):
        return self.ctx.__exit__(*a)

    def sb(self, name, shape, dtype=F32):
        return self.ctx.enter_context(self.nc.sbuf_tensor(f"{self.name}_{name}", shape, dtype))

    def sem(self, name, ahead=0):
        semaphore = self.nc.alloc_semaphore(f"{self.name}_{name}")
        self.chip.used_semaphores.append(semaphore)
        if ahead:
            self.nc.sync.sem_inc(semaphore, ahead)
        return semaphore

    def block(self):
        return self.ctx.enter_context(self.nc.Block())


class Chain:

    def __init__(self, engine, sem, start=0):
        self.engine, self.sem, self.n = engine, sem, start

    def done(self, instruction):
        instruction.then_inc(self.sem, 1)
        self.n = self.n + 1
        self.engine.wait_ge(self.sem, self.n)


def load_stage(chip):
    with Stage(chip, "load") as st:
        loaded = st.sem("loaded")
        block = st.block()

        @block.sync
        def _(sp):
            xs = chip.dram["x"].rearrange("b (t p) d -> p (b t) d", p=P)
            for q in range(4):
                tiles = slice(4 * q, 4 * q + 4)
                sp.dma_start(chip.x[:, tiles, :], xs[:, tiles, :]).then_inc(loaded, 16)
            sp.dma_start(chip.ident[:, :], chip.dram["ident"]).then_inc(loaded, 16)
            sp.wait_ge(loaded, 80)


def norm_stage(chip, name, scale, loads=()):
    Q = 4
    with Stage(chip, name) as st:
        xn = st.sb("xn", [P, TILES, D])
        stats = st.sb("stats", [P, TILES, 6])
        moments = st.sb("moments", [P, TILES, 2])
        rstd, var, shift = st.sb("rstd", [P, TILES]), st.sb("var", [P, TILES]), st.sb("shift", [P, TILES])
        preloaded = st.sem("preloaded")
        y_turned = st.sem("y_turned")
        x_added, stats_done, moments_done = st.sem("x_added"), st.sem("stats_done"), st.sem("moments_done")
        var_done, std_done, rstd_done = st.sem("var_done"), st.sem("std_done"), st.sem("rstd_done")
        affine_ready = st.sem("affine_ready")
        xn_ready = st.sem("xn_ready")
        xn_turned = st.sem("xn_turned")
        block = st.block()
        x, psum = chip.x, chip.psum

        @block.sync
        def _(sp):
            for buf, array in loads:
                sp.dma_start(buf, array).then_inc(preloaded, 16)
            if loads:
                sp.wait_ge(preloaded, 16 * len(loads))

        @block.tensor
        def _(pe):
            if scale is not None:
                for t in range(TILES):
                    turn = nc_t(pe, psum[:, t // 4, t % 4 * P:(t % 4 + 1) * P], chip.yT[:, t * P:(t + 1) * P], chip)
                    if t % 4 == 3:
                        turn.then_inc(y_turned, 1)
            for t in range(TILES):
                if t % 4 == 0:
                    pe.wait_ge(xn_ready, t // 4 + 1)
                turn = nc_t(pe, psum[:, 4 + t // 4, t % 4 * P:(t % 4 + 1) * P], xn[:, t, :], chip)
                if t % 4 == 3:
                    turn.then_inc(xn_turned, 1)

        @block.vector
        def _(dve):
            def moments_of(q):
                tiles = slice(4 * q, 4 * q + 4)
                if scale is not None:
                    dve.wait_ge(y_turned, q + 1)
                    flat = x[:, tiles, :].rearrange("p t d -> p (t d)")
                    dve.scalar_tensor_tensor(flat, psum[:, q, :], scale, flat, ALU.mult, ALU.add).then_inc(x_added, 1)
                    dve.wait_ge(x_added, q + 1)
                for t in range(4 * q, 4 * q + 4):
                    last = dve.bn_stats(stats[:, t, :], x[:, t, :])
                last.then_inc(stats_done, 1)
                dve.wait_ge(stats_done, q + 1)
                for t in range(4 * q, 4 * q + 4):
                    last = dve.bn_aggr(moments[:, t, :], stats[:, t, :])
                last.then_inc(moments_done, 1)
                dve.wait_ge(moments_done, q + 1)
                dve.tensor_scalar(var[:, tiles], moments[:, tiles, 1], EPS, None, ALU.add).then_inc(var_done, 1)

            def affine_of(q):
                tiles = slice(4 * q, 4 * q + 4)
                dve.wait_ge(std_done, q + 1)
                dve.reciprocal(rstd[:, tiles], var[:, tiles]).then_inc(rstd_done, 1)
                dve.wait_ge(rstd_done, q + 1)
                dve.scalar_tensor_tensor(shift[:, tiles], moments[:, tiles, 0], -1.0, rstd[:, tiles], ALU.mult,
                                         ALU.mult).then_inc(affine_ready, 1)

            moments_of(0)
            for q in range(1, Q):
                moments_of(q)
                affine_of(q - 1)
            affine_of(Q - 1)

        @block.scalar
        def _(act):
            def root(q):
                act.wait_ge(var_done, q + 1)
                act.activation(var[:, 4 * q:4 * q + 4], var[:, 4 * q:4 * q + 4], ACT.Sqrt).then_inc(std_done, 1)

            def normalise(q):
                act.wait_ge(affine_ready, q + 1)
                for t in range(4 * q, 4 * q + 4):
                    last = act.activation(xn[:, t, :], x[:, t, :], ACT.Identity, bias=shift[:, t:t + 1], scale=rstd[:, t:t + 1])
                last.then_inc(xn_ready, 1)

            def copy_turned(q):
                act.wait_ge(xn_turned, q + 1)
                act.copy(chip.xnT[:, q * GROUP:(q + 1) * GROUP], psum[:, 4 + q, :])

            root(0)
            for q in range(Q):
                if q < Q - 1:
                    root(q + 1)
                normalise(q)
                if q > 0:
                    copy_turned(q - 1)
            copy_turned(Q - 1)


def nc_t(pe, out, in_, chip):
    return pe.transpose(out, in_, chip.ident[0:in_.shape[0], 0:in_.shape[0]])


def store_stage(chip, scale):
    with Stage(chip, "store") as st:
        y_turned = st.sem("y_turned")
        x_added = st.sem("x_added")
        stored = st.sem("stored")
        block = st.block()

        @block.tensor
        def _(pe):
            for t in range(TILES):
                turn = nc_t(pe, chip.psum[:, t // 4, t % 4 * P:(t % 4 + 1) * P], chip.yT[:, t * P:(t + 1) * P], chip)
                if t % 4 == 3:
                    turn.then_inc(y_turned, 1)

        @block.vector
        def _(dve):
            for q in range(4):
                dve.wait_ge(y_turned, q + 1)
                tiles = chip.x[:, 4 * q:4 * q + 4, :].rearrange("p t d -> p (t d)")
                dve.scalar_tensor_tensor(tiles, chip.psum[:, q, :], scale, tiles, ALU.mult,
                                         ALU.add).then_inc(x_added, 1)

        @block.sync
        def _(sp):
            out = chip.out.rearrange("b (t p) d -> p (b t) d", p=P)
            for q in range(4):
                sp.wait_ge(x_added, q + 1)
                tiles = slice(4 * q, 4 * q + 4)
                sp.dma_start(out[:, tiles, :], chip.x[:, tiles, :]).then_inc(stored, 16)
            sp.wait_ge(stored, 64)


def ffn_stage(chip, name, norm):
    F = 512
    NC = F // P
    with Stage(chip, name) as st:
        w1 = st.sb("w1", [P, F])
        w2 = st.sb("w2", [P, NC, D])
        b1 = st.sb("b1", [P, NC])
        b2 = st.sb("b2", [P, 1])
        hidden = st.sb("hidden", [P, NC, GROUP])
        norm([(w1[:, :], chip.dram["ffn_w1"]), (w2[:, :, :], chip.dram["ffn_w2"]),
              (b1[:, :], chip.dram["ffn_b1"]), (b2[:, :], chip.dram["ffn_b2"])])
        up_done = st.sem("up_done")
        relu_done = st.sem("relu_done", ahead=NC)
        down_done = st.sem("down_done", ahead=1)
        y_copied = st.sem("y_copied", ahead=2)
        block = st.block()
        up, down = chip.psum[:, 0:NC, :], chip.psum[:, NC:NC + 2, :]

        @block.tensor
        def _(pe):
            with pe.Fori(0, GROUPS // 2) as pair:
                for q in range(2):
                    g = pair * 2 + q
                    for c in range(NC):
                        pe.wait_ge(relu_done, g * NC + c + 1)
                        pe.matmul(up[:, c, :], w1[:, c * P:(c + 1) * P], chip.xnT[:, bass.ts(g, GROUP)],
                                  start=True, stop=True).then_inc(up_done, 1)
                    pe.wait_ge(y_copied, g + 1)
                    for c in range(NC):
                        pe.wait_ge(relu_done, NC + g * NC + c + 1)
                        mm = pe.matmul(down[:, q, :], w2[:, c, :], hidden[:, c, :], start=(c == 0), stop=(c == NC - 1))
                    mm.then_inc(down_done, 1)

        @block.scalar
        def _(act):
            with act.Fori(0, GROUPS) as g:
                act.wait_ge(down_done, g + 1)
                for c in range(NC):
                    act.wait_ge(up_done, g * NC + c + 1)
                    act.activation(hidden[:, c, :], up[:, c, :], ACT.Relu, bias=b1[:, c:c + 1]).then_inc(relu_done, 1)

        @block.vector
        def _(dve):
            with dve.Fori(0, GROUPS // 2) as pair:
                for q in range(2):
                    g = pair * 2 + q
                    dve.wait_ge(down_done, g + 2)
                    dve.tensor_scalar(chip.yT[:, bass.ts(g, GROUP)], down[:, q, :], b2[:, 0:1], None,
                                      ALU.add).then_inc(y_copied, 1)


TRIAL_COUNT = 8
ROUNDS = 10


def router_programs(chip, st, mode, wr, descending, search):
    J = PER_B
    TRIALS = TRIAL_COUNT if mode == "choice" else 1
    prob = st.sb("prob", [P, TILES, E])
    pick = st.sb("pick", [P, TILES, E])
    rank = st.sb("rank", [P, TILES, E])
    first = st.sb("first", [P, TILES, E])
    comb = st.sb("comb", [P, J, TRIALS, B, E])
    best = st.sb("best", [P, TILES])
    best2 = st.sb("best2", [P, TILES])
    part = st.sb("part", [P, TILES])
    share = st.sb("share", [P, TILES])
    combT = st.sb("combT", [B * E, T])
    logits_done = st.sem("logits_done")
    shifted = st.sem("shifted")
    exp_done = st.sem("exp_done")
    own = st.sem("dve_steps")
    comb_ready = st.sem("comb_ready")
    comb_turned = st.sem("comb_turned")
    comb_copied = st.sem("comb_copied")
    stored = st.sem("stored")
    logits = chip.psum[:, 6, 0:TILES * E].rearrange("p (t e) -> p t e", e=E)
    turned = chip.psum[0:TRIALS * B * E, 6:8, :]
    reached = chip.psum[:, 5, 0:1]
    if mode == "choice":
        place, trials, same_row = search
        ones = st.sb("ones", [P, 1])
        low = st.sb("low", [P, 1], I32)
        trial = st.sb("trial", [P, 1], I32)
        keep = st.sb("keep", [P, 1], I32)
        count = st.sb("count", [P, 1])
        enough = st.sb("enough", [P, 1])
        all_rows = st.sb("all_rows", [P, T])
        above_all = st.sb("above_all", [P, T])
        above = above_all[0:B * E, :]
        equal = st.sb("equal", [B * E, T])
        order = st.sb("order", [B * E, T])
        room = st.sb("room", [B * E, 1])
        compared, summed = st.sem("compared", ahead=1), st.sem("summed", ahead=1)

    def each(v):
        return v[:, :].unsqueeze(2).to_broadcast([P, TILES, E])

    def on_sync(sp):
        sp.wait_ge(comb_copied, 3 if mode == "choice" else 2)
        sp.dma_start(chip.weights_by_expert, combT[:, :]).then_inc(stored, 16)
        sp.wait_ge(stored, 16)

    def on_tensor_logits(pe):
        for t in range(TILES):
            mm = pe.matmul(logits[:, t, :], chip.xnT[:, t * P:(t + 1) * P], wr[:, :], start=True, stop=True)
        mm.then_inc(logits_done, 1)

    def on_tensor_turn(pe):
        pe.wait_ge(comb_ready, 1)
        for j in range(J):
            turn = nc_t(pe, turned[:, j // 4, j % 4 * P:(j % 4 + 1) * P],
                        comb[:, j, :, :, :].rearrange("p r b e -> p (r b e)"), chip)
            if j % 4 == 3:
                turn.then_inc(comb_turned, 1)
        if mode == "choice":
            with pe.Fori(0, ROUNDS) as i:
                pe.wait_ge(compared, i + 2)
                pe.matmul(reached, same_row[:, :], enough[:, :], start=True, stop=True).then_inc(summed, 1)

    def on_scalar(act):
        act.wait_ge(shifted, 1)
        act.activation(prob[:, :, :], prob[:, :, :], ACT.Exp).then_inc(exp_done, 1)
        if mode == "softmax":
            act.wait_ge(shifted, 2)
            act.activation(part[:, :], part[:, :], ACT.Exp).then_inc(exp_done, 1)

    def choose(dve, chain):
        CAP = T * 2 // E
        done = chain.done
        done(dve.memset(ones[:, :], 1.0))
        done(dve.memset(low[:, :], 0))
        start = chain.n
        with dve.Fori(0, ROUNDS) as i:
            step = Chain(dve, own, i * 4 + start)
            step.done(dve.tensor_tensor(trial[:, :], low[:, :], trials[:, bass.ds(i, 1)], ALU.bitwise_or))
            step.done(dve.tensor_scalar(above_all[:, :], all_rows[:, :], trial[:, :].bitcast(F32), None, ALU.is_ge,
                                        ALU.add, accum_out=count[:, :]))
            dve.tensor_scalar(enough[:, :], count[:, :], float(CAP), None, ALU.is_ge).then_inc(compared, 1)
            dve.wait_ge(summed, i + 2)
            step.done(dve.tensor_scalar(keep[:, :], reached, place[:, bass.ds(i, 1)], None, ALU.mult))
            step.done(dve.tensor_tensor(low[:, :], low[:, :], keep[:, :], ALU.bitwise_or))
        chain.n = start + 4 * ROUNDS
        least = low[0:B * E, :].bitcast(F32)
        count_own = count[0:B * E, :]
        own_rows = all_rows[0:B * E, :]
        done(dve.tensor_scalar(above, own_rows, least, None, ALU.is_gt, ALU.add, accum_out=count_own))
        done(dve.tensor_scalar(equal[:, :], own_rows, least, None, ALU.is_equal))
        done(dve.tensor_scalar(room[:, :], count_own, -1.0, float(CAP), ALU.mult, ALU.add))
        done(dve.tensor_tensor_scan(order[:, :], ones[0:B * E, :].to_broadcast([B * E, T]), equal[:, :], 0.0,
                                    ALU.mult, ALU.add))
        done(dve.scalar_tensor_tensor(equal[:, :], order[:, :], room[:, 0:1], equal[:, :], ALU.is_le, ALU.mult))
        done(dve.tensor_tensor(above, above, equal[:, :], ALU.add))
        dve.tensor_tensor(combT[:, :], own_rows, above, ALU.mult).then_inc(comb_copied, 1)

    def on_vector(dve):
        chain = Chain(dve, own)
        done = chain.done
        dve.wait_ge(logits_done, 1)
        done(dve.tensor_reduce(best[:, :], logits, AX_X, ALU.max))
        dve.tensor_tensor(prob[:, :, :], logits, each(best), ALU.subtract).then_inc(shifted, 1)
        dve.wait_ge(exp_done, 1)
        done(dve.tensor_reduce(best[:, :], prob[:, :, :], AX_X, ALU.add))
        done(dve.reciprocal(share[:, :], best[:, :]))
        if mode == "choice":
            done(dve.tensor_tensor(prob[:, :, :], prob[:, :, :], each(share), ALU.mult))
            for b in range(B):
                copy = dve.tensor_copy(comb[:, :, :, b, :], prob[:, b * J:(b + 1) * J, :].unsqueeze(2).to_broadcast(
                    [P, J, TRIAL_COUNT, E]))
            copy.then_inc(comb_ready, 1)
            for h in range(2):
                dve.wait_ge(comb_turned, h + 1)
                copy = dve.tensor_copy(all_rows[:, h * GROUP:(h + 1) * GROUP], turned[:, h, :])
                copy.then_inc(comb_copied, 1)
            dve.wait_ge(comb_copied, 2)
            choose(dve, chain)
            return
        done(dve.tensor_tensor(prob[:, :, :], prob[:, :, :], each(share), ALU.mult))

        def take_best(value, selected):
            done(dve.tensor_reduce(value[:, :], prob[:, :, :], AX_X, ALU.max))
            done(dve.tensor_tensor(rank[:, :, :], prob[:, :, :], each(value), ALU.is_ge))
            done(dve.tensor_tensor(rank[:, :, :], rank[:, :, :],
                                   descending[:, :].unsqueeze(1).to_broadcast([P, TILES, E]), ALU.mult))
            done(dve.tensor_reduce(part[:, :], rank[:, :, :], AX_X, ALU.max))
            done(dve.tensor_tensor(selected[:, :, :], rank[:, :, :], each(part), ALU.is_ge))

        take_best(best, first)
        if mode == "sum":
            done(dve.tensor_copy(pick[:, :, :], prob[:, :, :]))
        done(dve.scalar_tensor_tensor(prob[:, :, :], first[:, :, :], -2.0, prob[:, :, :], ALU.mult, ALU.add))
        second = rank
        take_best(best2, second)
        by_row = comb[:, :, 0, :, :].rearrange("p j b e -> p b j e")
        if mode == "sum":
            done(dve.tensor_tensor(share[:, :], best[:, :], best2[:, :], ALU.add))
            done(dve.reciprocal(share[:, :], share[:, :]))
            done(dve.tensor_tensor(first[:, :, :], first[:, :, :], second[:, :, :], ALU.add))
            done(dve.tensor_tensor(pick[:, :, :], pick[:, :, :], each(share), ALU.mult))
            final, other, op = pick, first, ALU.mult
        else:
            dve.tensor_tensor(part[:, :], best2[:, :], best[:, :], ALU.subtract).then_inc(shifted, 1)
            dve.wait_ge(exp_done, 2)
            done(dve.tensor_scalar(share[:, :], part[:, :], 1.0, None, ALU.add))
            done(dve.reciprocal(share[:, :], share[:, :]))
            done(dve.tensor_tensor(part[:, :], part[:, :], share[:, :], ALU.mult))
            done(dve.tensor_tensor(first[:, :, :], first[:, :, :], each(share), ALU.mult))
            done(dve.tensor_tensor(second[:, :, :], second[:, :, :], each(part), ALU.mult))
            final, other, op = first, second, ALU.add
        for b in range(B):
            tiles = slice(b * J, (b + 1) * J)
            mul = dve.tensor_tensor(by_row[:, b], final[:, tiles, :], other[:, tiles, :], op)
        mul.then_inc(comb_ready, 1)
        for h in range(2):
            dve.wait_ge(comb_turned, h + 1)
            dve.tensor_copy(combT[:, h * GROUP:(h + 1) * GROUP], turned[:, h, :]).then_inc(comb_copied, 1)

    return on_sync, on_tensor_logits, on_tensor_turn, on_scalar, on_vector


def experts_stage(chip, name, norm, mode, router_name, hidden_dim, gated, up_names, down_name):
    NC = hidden_dim // P
    NU = len(up_names)
    STEPS = E * GROUPS
    with Stage(chip, name) as st:
        raw_up = [st.sb(f"raw_up{u}", [P, hidden_dim]) for u in range(NU)]
        raw_down = st.sb("raw_down", [P, NC, D])
        w_up = [[[st.sb(f"w_up{p}{u}_{part}", [P, hidden_dim], F32R) for part in PARTS] for u in range(NU)] for p in range(2)]
        w_down = [[st.sb(f"w_down{p}_{part}", [P, NC, D], F32R) for part in PARTS] for p in range(2)]
        xn = [st.sb(f"xn_{part}", [P, TOK], F32R) for part in PARTS]
        weight = [st.sb(f"weight{p}", [P, TOK]) for p in range(2)]
        ones = st.sb("one", [P, 1])
        HB = 4
        full = st.sb("full", [P, 2, GROUP])
        hidden = [st.sb(f"hidden_{part}", [P, HB, GROUP], F32R) for part in PARTS]
        silu = st.sb("silu", [P, 2, GROUP])
        scaled = st.sb("scaled", [P, 2, GROUP])
        wr, descending = st.sb("wr", [P, E]), st.sb("descending", [P, E])
        loads = [(raw_up[u][:, :], chip.dram[up_names[u]][0]) for u in range(NU)]
        loads += [(raw_down[:, :, :], chip.dram[down_name][0]), (wr[:, :], chip.dram[router_name]),
                  (descending[:, :], chip.dram["descending"])]
        search = None
        if mode == "choice":
            place = st.sb("place", [P, ROUNDS])
            trials = st.sb("trials", [P, ROUNDS], I32)
            same_row = st.sb("same_row", [P, P])
            search = place, trials, same_row
            loads += [(buf[:, :], chip.dram[nm]) for buf, nm in zip(search, ("place", "trials", "same_row"))]
        norm(loads)
        route_sync, route_logits, route_turn, route_scalar, route_vector = router_programs(
            chip, st, mode, wr, descending, search)
        LOADS = 16 * (NU + 1)
        loaded = st.sem("loaded", ahead=LOADS)
        weight_loaded = [st.sem(f"weight_loaded{p}") for p in range(2)]
        x_high, x_split = st.sem("x_high"), st.sem("x_split")
        ones_done = st.sem("one_done")
        w_high, w_split = st.sem("w_high"), st.sem("w_split", ahead=1)
        up_done = st.sem("up_done")
        silu_done = st.sem("silu_done")
        full_done = st.sem("full_done", ahead=2)
        high_done = st.sem("high_done")
        hidden_done = st.sem("hidden_done", ahead=2)
        down_done = st.sem("down_done", ahead=HB)
        scaled_done = st.sem("scaled_done", ahead=2)
        added = st.sem("added")
        block = st.block()
        up = chip.psum[:, 0:4, :]
        down = chip.psum[:, 4:6, :]

        def later(pair, p, g, c, chunks):
            c += chunks
            if c < NC:
                return pair, p, g, c
            return (pair, p, g + 1, c - NC) if g < GROUPS - 1 else (pair + p, 1 - p, 0, c - NC)

        def all_experts(eng, expert):
            with eng.Fori(0, E // 2 - 1) as pair:
                expert(pair, 0, False)
                expert(pair, 1, False)
            expert(E // 2 - 1, 0, False)
            expert(E // 2 - 1, 1, True)

        @block.sync
        def _(sp):
            def load_matrices(e):
                sp.wait_ge(w_split, e + 1)
                for u in range(NU):
                    sp.dma_start(raw_up[u][:, :], chip.dram[up_names[u]][bass.ds(e, 1)].rearrange(
                        "e p f -> (e p) f")).then_inc(loaded, 16)
                sp.dma_start(raw_down[:, :, :], chip.dram[down_name][bass.ds(e, 1)].rearrange(
                    "e p c d -> (e p) c d")).then_inc(loaded, 16)

            def load_weight(e, p, turn):
                if turn is not None:
                    sp.wait_ge(scaled_done, 2 + (turn * 2 + p - 1) * GROUPS)
                rows = chip.weights_by_expert.rearrange("(b e) t -> e b t", b=B)[bass.ds(e, 1)]
                rows = rows.rearrange("e b t -> (e b) t").unsqueeze(0).to_broadcast([P, B, T])
                sp.dma_start(weight[p][:, :].rearrange("p (b t) -> p b t", b=B), rows).then_inc(weight_loaded[p], 16)

            load_matrices(1)
            route_sync(sp)
            load_weight(0, 0, None)
            load_weight(1, 1, None)
            with sp.Fori(1, E // 2) as pair:
                for p in range(2):
                    load_matrices(pair * 2 + p)
                    load_weight(pair * 2 + p, p, pair)

        @block.tensor
        def _(pe):
            def ups(pair, p, g, c):
                step = (pair * 2 + p) * GROUPS + g
                if c == 0 and g == 0:
                    pe.wait_ge(w_split, pair * 2 + p + 2)
                pe.wait_ge(full_done, step * NC + c + 1)
                for u in range(NU):
                    mm = split_product(pe, up[:, c % 2 * 2 + u, :], [w[:, c * P:(c + 1) * P] for w in w_up[p][u]],
                                       [x[:, g * GROUP:(g + 1) * GROUP] for x in xn])
                mm.then_inc(up_done, 1)

            def down_product(pair, p, g, c):
                step = (pair * 2 + p) * GROUPS + g
                if c == 0:
                    pe.wait_ge(scaled_done, step + 1)
                pe.wait_ge(hidden_done, step * NC + c + 3)
                mm = split_product(pe, down[:, g % 2, :], [w[:, c, :] for w in w_down[p]],
                                   [h[:, (g * NC + c) % HB, :] for h in hidden], first=(c == 0), last=(c == NC - 1))
                mm.then_inc(down_done, 1)

            def expert(pair, p, last):
                for g in range(GROUPS):
                    for c in range(NC):
                        if not (last and g == GROUPS - 1 and c >= NC - 2):
                            ups(*later(pair, p, g, c, 2))
                        down_product(pair, p, g, c)

            route_logits(pe)
            pe.wait_ge(x_split, GROUPS)
            ups(0, 0, 0, 0)
            ups(0, 0, 0, 1)
            route_turn(pe)
            all_experts(pe, expert)

        @block.scalar
        def _(act):
            func = ACT.Silu if gated else ACT.Gelu
            for g in range(GROUPS):
                cols = slice(g * GROUP, (g + 1) * GROUP)
                act.copy(xn[0][:, cols], chip.xnT[:, cols]).then_inc(x_high, 1)
            route_scalar(act)
            with act.Fori(0, E) as e:
                for j in range(GROUPS * NC):
                    k, c = e * (GROUPS * NC) + j, j % NC
                    act.wait_ge(up_done, k + 1)
                    if gated:
                        act.wait_ge(full_done, k + 1)
                        act.activation(silu[:, c % 2, :], up[:, c % 2 * 2, :], func).then_inc(silu_done, 1)
                    else:
                        act.wait_ge(hidden_done, k + 1)
                        act.activation(full[:, c % 2, :], up[:, c % 2 * 2, :], func).then_inc(full_done, 1)

        @block.vector
        def _(dve):
            route_vector(dve)

            def make_hidden(pair, p, g, c):
                k = ((pair * 2 + p) * GROUPS + g) * NC + c
                if gated:
                    dve.wait_ge(silu_done, k + 1)
                    dve.wait_ge(hidden_done, k + 1)
                    dve.tensor_tensor(full[:, c % 2, :], silu[:, c % 2, :], up[:, c % 2 * 2 + 1, :],
                                      ALU.mult).then_inc(full_done, 1)
                dve.wait_ge(full_done, k + 3)
                dve.wait_ge(down_done, k + 1)
                high, low = (h[:, (g * NC + c) % HB, :] for h in hidden)
                dve.tensor_copy(high, full[:, c % 2, :]).then_inc(high_done, 1)
                dve.wait_ge(high_done, k + 1)
                dve.tensor_tensor(low, full[:, c % 2, :], high.bitcast(F32), ALU.subtract).then_inc(hidden_done, 1)

            def expert(pair, p, last):
                for g in range(GROUPS):
                    step = (pair * 2 + p) * GROUPS + g
                    for c in range(NC):
                        if not (last and g == GROUPS - 1 and c >= NC - 2):
                            make_hidden(*later(pair, p, g, c, 2))
                    if g == 0:
                        dve.wait_ge(weight_loaded[p], (pair + 1) * 16)
                    dve.wait_ge(down_done, HB + (step + 1) * NC)
                    dve.wait_ge(added, step + 1)
                    dve.tensor_tensor(scaled[:, g % 2, :], down[:, g % 2, :], weight[p][:, g * GROUP:(g + 1) * GROUP],
                                      ALU.mult).then_inc(scaled_done, 1)

            make_hidden(0, 0, 0, 0)
            make_hidden(0, 0, 0, 1)
            all_experts(dve, expert)

        @block.gpsimd
        def _(pool):
            def split_weights(e, p):
                pool.wait_ge(loaded, (e + 1) * LOADS)
                pairs = [(raw_up[u][:, :], [w[:, :] for w in w_up[p][u]]) for u in range(NU)]
                pairs.append((raw_down[:, :, :], [w[:, :, :] for w in w_down[p]]))
                for raw, (high, _) in pairs:
                    one = ones[:, :] if len(raw.shape) == 2 else ones[:, :].unsqueeze(2)
                    last = pool.tensor_tensor(high, raw, one.to_broadcast(list(raw.shape)), ALU.mult)
                last.then_inc(w_high, 1)
                pool.wait_ge(w_high, e + 1)
                for raw, (high, low) in pairs:
                    last = pool.tensor_tensor(low, raw, high.bitcast(F32), ALU.subtract)
                last.then_inc(w_split, 1)

            def add(step, g):
                y = chip.yT[:, g * GROUP:(g + 1) * GROUP]
                pool.wait_ge(scaled_done, step + 3)
                pool.tensor_tensor(y, y, scaled[:, g % 2, :], ALU.add).then_inc(added, 1)

            pool.memset(ones[:, :], 1.0).then_inc(ones_done, 1)
            pool.wait_ge(ones_done, 1)
            for g in range(GROUPS):
                cols = slice(g * GROUP, (g + 1) * GROUP)
                pool.wait_ge(x_high, g + 1)
                pool.tensor_tensor(xn[1][:, cols], chip.xnT[:, cols], xn[0][:, cols].bitcast(F32),
                                   ALU.subtract).then_inc(x_split, 1)
            split_weights(0, 0)
            pool.memset(chip.yT[:, :], 0.0).then_inc(added, 2)
            pool.wait_ge(added, 2)
            split_weights(1, 1)
            with pool.Fori(0, E // 2 - 1) as pair:
                for p in range(2):
                    e = pair * 2 + p
                    for g in range(GROUPS):
                        add(e * GROUPS + g, g)
                    split_weights(e + 2, p)
            with pool.Fori(E - 2, E) as e:
                for g in range(GROUPS):
                    add(e * GROUPS + g, g)


PARTS = ("high", "low")


def split_product(pe, out, weights, moving, first=True, last=True):
    (w_high, w_low), (x_high, x_low) = weights, moving
    pe.matmul(out, w_high, x_high, start=first, stop=False)
    pe.matmul(out, w_high, x_low, start=False, stop=False)
    return pe.matmul(out, w_low, x_high, start=False, stop=last)


def project_stage(chip, name, w, features, tokens, bias=None, bias_row=None):
    nf = len(features)
    with Stage(chip, name) as st:
        products = st.sem("products")
        read = st.sem("banks_read", ahead=8)
        block = st.block()
        nt = len(tokens)

        jobs = [("features", n, g) for g in range(GROUPS) for n in range(nf)] + [("tokens", 0, q) for q in range(TILES // 2)]

        @block.tensor
        def _(pe):
            for k, (kind, n, q) in enumerate(jobs):
                pe.wait_ge(read, k + 1)
                if kind == "features":
                    mm = pe.matmul(chip.psum[:, k % 8, :], w[:, n, :], chip.xnT[:, q * GROUP:(q + 1) * GROUP],
                                   start=True, stop=True)
                else:
                    for half in range(2):
                        t = 2 * q + half
                        mm = pe.matmul(chip.psum[:, k % 8, half * nt * P:(half + 1) * nt * P], chip.xnT[:, t * P:(t + 1) * P],
                                       w[:, nf:, :].rearrange("p a d -> p (a d)"), start=True, stop=True)
                mm.then_inc(products, 1)

        def copy(eng, k, kind, n, q):
            bank = chip.psum[:, k % 8, :]
            eng.wait_ge(products, k + 1)
            if kind == "features":
                dst = features[n][:, q * GROUP:(q + 1) * GROUP]
                if bias is not None:
                    return eng.tensor_scalar(dst, bank, bias[:, n:n + 1], None, ALU.add)
                return eng.tensor_copy(dst, bank)
            view = bank[:, 0:2 * nt * P].rearrange("p (t a d) -> p t a d", t=2, a=nt)
            for a in range(nt):
                dst = tokens[a][:, 2 * q:2 * q + 2, :]
                if bias is not None:
                    last = eng.tensor_tensor(dst, view[:, :, a], bias_row[:, a, :].unsqueeze(1).to_broadcast([P, 2, P]),
                                             ALU.add)
                else:
                    last = eng.tensor_copy(dst, view[:, :, a])
            return last

        @block.vector
        def _(dve):
            for k, job in enumerate(jobs):
                copy(dve, k, *job).then_inc(read, 1)


def output_stage(chip, name, features, w, bias):
    with Stage(chip, name) as st:
        out_done = st.sem("out_done")
        block = st.block()

        @block.tensor
        def _(pe):
            for g in range(GROUPS):
                pe.matmul(chip.psum[:, g, :], w[:, :], features[:, g * GROUP:(g + 1) * GROUP],
                          start=True, stop=True).then_inc(out_done, 1)

        @block.vector
        def _(dve):
            for g in range(GROUPS):
                dve.wait_ge(out_done, g + 1)
                dve.tensor_scalar(chip.yT[:, g * GROUP:(g + 1) * GROUP], chip.psum[:, g, :], bias[:, 0:1], None, ALU.add)


DH0 = D // H
SLOTS = 32 // DH0
ROWS = H // SLOTS


def retention_attention(chip, norm):
    with Stage(chip, "retention") as outer:
        qT, kT = outer.sb("qT", [P, TOK]), outer.sb("kT", [P, TOK])
        k_tok, v_tok = outer.sb("k_tok", [P, TILES, P]), outer.sb("v_tok", [P, TILES, P])
        retained = outer.sb("retained", [P, TOK])
        w = outer.sb("w", [P, 4, P])
        wo = outer.sb("wo", [P, P])
        affine = outer.sb("affine", [P, 2])
        head_mean = outer.sb("head_mean", [P, P])
        consts = RetentionConstants(outer)
        norm([(w[:, n, :], chip.dram[nm]) for n, nm in enumerate(("ret_wq", "ret_wk", "ret_wk", "ret_wv"))]
             + [(wo[:, :], chip.dram["ret_wo"]), (affine[:, :], chip.dram["ret_affine"]),
                (head_mean[:, :], chip.dram["head_mean"])] + consts.loads(chip))
        project_stage(chip, "retention_in", w, (qT, kT), (k_tok, v_tok))
        retention_chunks(chip, consts, qT, kT, k_tok, v_tok, retained)
        group_norm_stage(chip, retained, wo, affine, head_mean)


class RetentionConstants:

    def __init__(self, st):
        self.decay = st.sb("decay", [P, H, P])
        self.q_decay = st.sb("q_decay", [P, P])
        self.k_decay = st.sb("k_decay", [P, P])
        self.chunk_decay = st.sb("chunk_decay", [P, 1])
        self.same_head = st.sb("same_head", [P, P])
        self.slot = st.sb("slot", [P, SLOTS])
        self.slot_cols = st.sb("slot_cols", [P, SLOTS, P])

    def loads(self, chip):
        dram = chip.dram
        return [(self.decay[:, :, :], dram["ret_decay"]), (self.q_decay[:, :], dram["ret_q_decay"]),
                (self.k_decay[:, :], dram["ret_k_decay"]), (self.chunk_decay[:, :], dram["ret_chunk_decay"]),
                (self.same_head[:, :], dram["same_head"]), (self.slot[:, :], dram["slot"]),
                (self.slot_cols[:, :, :], dram["slot_cols"])]


def retention_chunks(chip, consts, qT, kT, k_tok, v_tok, retained):
    with Stage(chip, "retention_chunks") as st:
        decay, q_decay, k_decay, chunk_decay = consts.decay, consts.q_decay, consts.k_decay, consts.chunk_decay
        same_head, slot, slot_cols = consts.same_head, consts.slot, consts.slot_cols
        vals = [st.sb(f"vals{p}", [P, SLOTS, P]) for p in range(2)]
        kc = [st.sb(f"kc{p}", [P, P]) for p in range(2)]
        qm = [st.sb(f"qm{p}", [P, SLOTS, P]) for p in range(2)]
        qd = [st.sb(f"qd{p}", [P, P]) for p in range(2)]
        kd = [st.sb(f"kd{p}", [P, P]) for p in range(2)]
        probs = st.sb("probs", [P, H, P])
        state = st.sb("state", [P, P])
        fresh = st.sb("fresh", [P, P])
        prepared = st.sem("prepared")
        scores_done = st.sem("scores_done")
        probs_done = st.sem("probs_done")
        update_done = st.sem("update_done")
        inter_done = st.sem("inter_done", ahead=1)
        fresh_done = st.sem("fresh_done", ahead=1)
        state_done = st.sem("state_done", ahead=1)
        y_done = st.sem("y_done")
        y_copied = st.sem("y_copied", ahead=2)
        block = st.block()
        scores, y, update = chip.psum[:, 0:4, :], chip.psum[:, 4:6, 0:P], chip.psum[:, 6, 0:P]

        @block.gpsimd
        def _(pool):
            with pool.Fori(0, TILES // 2) as pair:
                for p in range(2):
                    n = pair * 2 + p
                    pool.wait_ge(y_copied, n + 1)
                    cols = bass.ts(n, P)
                    pool.tensor_copy(kc[p][:, :], kT[:, cols])
                    pool.tensor_tensor(qm[p][:, :, :], qT[:, cols].unsqueeze(1).to_broadcast([P, SLOTS, P]),
                                       slot[:, :].unsqueeze(2).to_broadcast([P, SLOTS, P]), ALU.mult)
                    pool.tensor_tensor(vals[p][:, :, :], v_tok[:, bass.ds(n, 1), :].to_broadcast([P, SLOTS, P]),
                                       slot_cols[:, :, :], ALU.mult)
                    pool.tensor_tensor(qd[p][:, :], qT[:, cols], q_decay[:, :], ALU.mult)
                    pool.tensor_tensor(kd[p][:, :], k_tok[:, bass.ds(n, 1), :].rearrange("p a d -> p (a d)"), k_decay[:, :],
                                       ALU.mult).then_inc(prepared, 1)

        @block.tensor
        def _(pe):
            def score(n, p, r):
                if r == 0:
                    pe.wait_ge(prepared, n + 1)
                rows = slice(32 * r, 32 * r + 32)
                pe.matmul(scores[:, r, :], kc[p][rows, :], qm[p][rows, :, :].rearrange("p s i -> p (s i)"),
                          start=True, stop=True).then_inc(scores_done, 1)

            def chunk(b, n, p, last):
                v = v_tok[:, bass.ds(n, 1), :].rearrange("p a d -> p (a d)")
                pe.wait_ge(fresh_done, n + 1)
                pe.matmul(update, kd[p][:, :], v, start=True, stop=True).then_inc(update_done, 1)
                pe.wait_ge(state_done, n + b + 2)
                pe.wait_ge(y_copied, n + 1)
                pe.matmul(y[:, p, :], state[:, :], qd[p][:, :], start=True, stop=False,
                          skip_group_check=True).then_inc(inter_done, 1)
                for r in range(ROWS):
                    pe.wait_ge(probs_done, n * ROWS + r + 1)
                    rows = slice(32 * r, 32 * r + 32)
                    for s in range(SLOTS):
                        h = r * SLOTS + s
                        mm = pe.matmul(y[rows, p, :], vals[p][:, s, rows], probs[:, h, :],
                                       start=False, stop=(h == H - 1), skip_group_check=True)
                    if r == ROWS - 1:
                        mm.then_inc(y_done, 1)
                    if not last:
                        score(n + 1, 1 - p, r)

            with pe.Fori(0, B) as b:
                for r in range(ROWS):
                    score(b * PER_B, 0, r)
                with pe.Fori(0, PER_B // 2 - 1) as pair:
                    for p in range(2):
                        chunk(b, b * PER_B + pair * 2 + p, p, False)
                for p in range(2):
                    chunk(b, b * PER_B + PER_B - 2 + p, p, p == 1)

        @block.vector
        def _(dve):
            with dve.Fori(0, B) as b:
                dve.wait_ge(inter_done, b * PER_B + 1)
                dve.wait_ge(state_done, b * (PER_B + 1) + 1)
                dve.memset(state[:, :], 0.0).then_inc(state_done, 1)
                with dve.Fori(0, PER_B) as c:
                    n = b * PER_B + c
                    for r in range(ROWS):
                        dve.wait_ge(scores_done, n * ROWS + r + 1)
                        heads = slice(r * SLOTS, (r + 1) * SLOTS)
                        dve.tensor_tensor(probs[:, heads, :].rearrange("p s i -> p (s i)"), scores[:, r, :],
                                          decay[:, heads, :].rearrange("p s i -> p (s i)"), ALU.mult).then_inc(probs_done, 1)
                    dve.wait_ge(update_done, n + 1)
                    dve.wait_ge(state_done, n + b + 2)
                    dve.tensor_tensor(fresh[:, :], update, same_head[:, :], ALU.mult).then_inc(fresh_done, 1)
                    dve.wait_ge(fresh_done, n + 2)
                    dve.wait_ge(inter_done, n + 2)
                    dve.scalar_tensor_tensor(state[:, :], state[:, :], chunk_decay[:, 0:1], fresh[:, :], ALU.mult,
                                             ALU.add).then_inc(state_done, 1)

        @block.scalar
        def _(act):
            with act.Fori(0, TILES // 2) as pair:
                for p in range(2):
                    n = pair * 2 + p
                    act.wait_ge(y_done, n + 1)
                    act.copy(retained[:, bass.ts(n, P)], y[:, p, :]).then_inc(y_copied, 1)


def group_norm_stage(chip, retained, w, affine, head_mean):
    with Stage(chip, "group_norm") as st:
        y = st.sb("y", [P, TOK])
        stats = st.sb("stats", [P, GROUPS, 6])
        moments = st.sb("moments", [P, B, 2])
        mean_of = st.sb("mean_of", [P, B])
        off = st.sb("off", [P, B])
        var_of = st.sb("var_of", [P, B])
        scale, shift = st.sb("scale", [P, B]), st.sb("shift", [P, B])
        own = st.sem("dve_steps")
        asked = st.sem("asked")
        averaged = st.sem("averaged")
        var_done, std_done = st.sem("var_done"), st.sem("std_done")
        normed, out_done = st.sem("normed"), st.sem("out_done")
        block = st.block()
        psum = chip.psum

        @block.tensor
        def _(pe):
            for k, v in enumerate((moments[:, :, 0], off[:, :])):
                pe.wait_ge(asked, k + 1)
                pe.matmul(psum[:, 4, k * B:(k + 1) * B], head_mean[:, :], v, start=True, stop=True).then_inc(averaged, 1)
            for g in range(GROUPS):
                pe.wait_ge(normed, g + 1)
                pe.matmul(psum[:, g, :], w[:, :], y[:, g * GROUP:(g + 1) * GROUP], start=True,
                          stop=True).then_inc(out_done, 1)

        @block.vector
        def _(dve):
            done = Chain(dve, own).done
            for g in range(GROUPS):
                last = dve.bn_stats(stats[:, g, :], retained[:, g * GROUP:(g + 1) * GROUP])
            done(last)
            for b in range(B):
                last = dve.bn_aggr(moments[:, b, :], stats[:, 2 * b:2 * b + 2, :].rearrange("p a s -> p (a s)"))
            last.then_inc(asked, 1)
            dve.wait_ge(averaged, 1)
            done(dve.tensor_copy(mean_of[:, :], psum[:, 4, 0:B]))
            done(dve.tensor_tensor(off[:, :], moments[:, :, 0], mean_of[:, :], ALU.subtract))
            done(dve.tensor_tensor(off[:, :], off[:, :], off[:, :], ALU.mult))
            dve.tensor_tensor(off[:, :], off[:, :], moments[:, :, 1], ALU.add).then_inc(asked, 1)
            dve.wait_ge(averaged, 2)
            dve.tensor_scalar(var_of[:, :], psum[:, 4, B:2 * B], EPS, None, ALU.add).then_inc(var_done, 1)
            dve.wait_ge(std_done, 1)
            done(dve.reciprocal(scale[:, :], var_of[:, :]))
            done(dve.tensor_scalar(scale[:, :], scale[:, :], affine[:, 0:1], None, ALU.mult))
            done(dve.tensor_tensor(shift[:, :], mean_of[:, :], scale[:, :], ALU.mult))
            done(dve.tensor_scalar(shift[:, :], shift[:, :], -1.0, affine[:, 1:2], ALU.mult, ALU.add))
            for g in range(GROUPS):
                b = g // (GROUPS // B)
                dve.tensor_scalar(y[:, g * GROUP:(g + 1) * GROUP], retained[:, g * GROUP:(g + 1) * GROUP], scale[:, b:b + 1], shift[:, b:b + 1],
                                  ALU.mult, ALU.add).then_inc(normed, 1)
            for g in range(GROUPS):
                dve.wait_ge(out_done, g + 1)
                dve.tensor_copy(chip.yT[:, g * GROUP:(g + 1) * GROUP], psum[:, g, :])

        @block.scalar
        def _(act):
            act.wait_ge(var_done, 1)
            act.activation(var_of[:, :], var_of[:, :], ACT.Sqrt).then_inc(std_done, 1)


def window_attention(chip, norm):
    with Stage(chip, "window") as outer:
        qT, kT = outer.sb("qT", [P, TOK]), outer.sb("kT", [P, TOK])
        v_tok = outer.sb("v_tok", [P, TILES, P])
        attended = outer.sb("attended", [P, TOK])
        w, wo = outer.sb("w", [P, 3, P]), outer.sb("wo", [P, P])
        bias, bias_row, bo = outer.sb("bias", [P, 2]), outer.sb("bias_row", [P, 1, P]), outer.sb("bo", [P, 1])
        slope = outer.sb("slope", [P, ROWS, 2, SLOTS, P])
        slot = outer.sb("slot", [P, SLOTS])
        slot_cols = outer.sb("slot_cols", [P, SLOTS, P])
        norm([(w[:, n, :], chip.dram[nm]) for n, nm in enumerate(("win_wq", "win_wk", "win_wv"))]
             + [(bias[:, :], chip.dram["win_bias_qk"]), (bias_row[:, 0, :], chip.dram["win_bias_v"]),
                (wo[:, :], chip.dram["win_wo"]), (bo[:, :], chip.dram["win_bo"]), (slot[:, :], chip.dram["slot"]),
                (slot_cols[:, :, :], chip.dram["slot_cols"]),
                (slope[:, :, :, :, :].rearrange("p r a s j -> p (r a s j)"), chip.dram["win_slope"])])
        project_stage(chip, "window_in", w, (qT, kT), (v_tok,), bias, bias_row)
        window_chunks(chip, qT, kT, v_tok, attended, slope, slot, slot_cols)
        output_stage(chip, "window_out", attended, wo, bo)


def window_chunks(chip, qT, kT, v_tok, attended, slope, slot, slot_cols):
    with Stage(chip, "window_chunks") as st:
        keys = [st.sb(f"keys{p}", [P, 2, SLOTS, P]) for p in range(2)]
        qc = [st.sb(f"qc{p}", [P, P]) for p in range(2)]
        vals = [st.sb(f"vals{p}", [P, 2, SLOTS, P]) for p in range(2)]
        biased = [st.sb(f"biased{p}", [P, 2, SLOTS, P]) for p in range(2)]
        expd = [st.sb(f"expd{p}", [P, 2, SLOTS, P]) for p in range(2)]
        probsT = [st.sb(f"probsT{p}", [P, 2, SLOTS, P]) for p in range(2)]
        low = st.sb("low", [P, 2, SLOTS])
        sums = st.sb("sums", [P, 2, H])
        inverse = st.sb("inverse", [P, H])
        spread_inv = [st.sb(f"spread_inv{p}", [P, H, DH0]) for p in range(2)]
        inverseT = st.sb("inverseT", [P, 2, P])
        prepared, prepared_v = st.sem("prepared"), st.sem("prepared_v")
        scores_done = st.sem("scores_done", ahead=2 * ROWS)
        biased_done = st.sem("biased_done", ahead=2)
        max_done = st.sem("max_done")
        exp_done = st.sem("exp_done", ahead=2 * SLOTS)
        turned = st.sem("turned", ahead=2)
        own_ready = st.sem("own_ready", ahead=1)
        other_ready = st.sem("other_ready", ahead=1)
        used = st.sem("used", ahead=2 * ROWS)
        inverse_done, spread_done = st.sem("inverse_done"), st.sem("spread_done", ahead=1)
        inverse_turned, inverse_copied = st.sem("inverse_turned", ahead=2), st.sem("inverse_copied")
        y_done = st.sem("y_done", ahead=2)
        block = st.block()
        psum = chip.psum

        def tile_loop(eng, body):
            with eng.Fori(0, B) as b:
                body(b, 0, 0, True, False, False)
                body(b, 1, 1, False, True, False)
                with eng.Fori(1, PER_B // 2 - 1) as pair:
                    body(b, pair * 2, 0, False, False, False)
                    body(b, pair * 2 + 1, 1, False, False, False)
                body(b, PER_B - 2, 0, False, False, False)
                body(b, PER_B - 1, 1, False, False, True)

        def later(b, c, p, r, first, last, steps):
            if r + steps < ROWS:
                return b, c, p, r + steps, first
            return None if last else (b, c + 1, 1 - p, r + steps - ROWS, False)

        def place(first, a, h):
            return (h // 2, h % 2) if first else (a, h)

        def half_of(buf, first, half):
            return buf[:, half, 0:2 if first else SLOTS, :].rearrange("p s i -> p (s i)")

        def half_of_bank(first, half):
            return psum[:, 4 + half, 0:2 * P if first else SLOTS * P]

        @block.gpsimd
        def _(pool):
            def prepare(b, c, p, first):
                n = b * PER_B + c
                cols = bass.ts(n, P)
                pool.wait_ge(scores_done, (n + 1) * ROWS)
                pool.tensor_copy(qc[p][:, :], qT[:, cols])
                for a in range(1 if first else 2):
                    last = pool.tensor_tensor(keys[p][:, a, :, :], kT[:, bass.ts(n - a, P)].unsqueeze(1).to_broadcast([P, SLOTS, P]),
                                              slot[:, :].unsqueeze(2).to_broadcast([P, SLOTS, P]), ALU.mult)
                last.then_inc(prepared, 1)
                pool.wait_ge(used, (n + 1) * ROWS)
                for a in range(1 if first else 2):
                    last = pool.tensor_tensor(vals[p][:, a, :, :], v_tok[:, bass.ds(n - a, 1), :].to_broadcast([P, SLOTS, P]),
                                              slot_cols[:, :, :], ALU.mult)
                last.then_inc(prepared_v, 1)

            tile_loop(pool, lambda b, c, p, first, second, last: prepare(b, c, p, first))

        @block.tensor
        def _(pe):
            def scores(b, c, p, r, first):
                n = b * PER_B + c
                s = n * ROWS + r
                if r == 0:
                    pe.wait_ge(prepared, n + 1)
                pe.wait_ge(biased_done, s + 1)
                rows = slice(32 * r, 32 * r + 32)
                for a in range(1 if first else 2):
                    mm = pe.matmul(psum[:, r % 2 * 2 + a, :], qc[p][rows, :],
                                   keys[p][rows, a, :, :].rearrange("p s j -> p (s j)"), start=True, stop=True)
                mm.then_inc(scores_done, 1)

            def turn(b, c, p, r, first):
                s = (b * PER_B + c) * ROWS + r
                pe.wait_ge(exp_done, (s + 3) * SLOTS)
                pe.wait_ge(own_ready, s + 1)
                pe.wait_ge(other_ready, s + 1)
                for a in range(1 if first else 2):
                    for h in range(SLOTS):
                        bank, col = place(first, a, h)
                        mm = nc_t(pe, psum[:, 4 + bank, col * P:(col + 1) * P], expd[r % 2][:, a, h, :], chip)
                mm.then_inc(turned, 1)

            def times_v(b, c, p, r, first):
                n = b * PER_B + c
                s = n * ROWS + r
                if r == 0:
                    pe.wait_ge(prepared_v, n + 1)
                    pe.wait_ge(y_done, n + 1)
                pe.wait_ge(own_ready, s + 2)
                pe.wait_ge(other_ready, s + 2)
                rows = slice(32 * r, 32 * r + 32)
                blocks = 1 if first else 2
                for a in range(blocks):
                    for h in range(SLOTS):
                        half, col = place(first, a, h)
                        mm = pe.matmul(psum[rows, 6 + p, 0:P], vals[p][:, a, h, rows], probsT[r % 2][:, half, col, :],
                                       start=(a == 0 and h == 0), stop=(a == blocks - 1 and h == SLOTS - 1))
                mm.then_inc(used, 1)

            def finish(b, c, p, first):
                n = b * PER_B + c
                times_v(b, c, p, ROWS - 1, first)
                pe.wait_ge(spread_done, n + 2)
                nc_t(pe, psum[:, 6 + p, P:2 * P], spread_inv[p][:, :, :].rearrange("p h e -> p (h e)"),
                     chip).then_inc(inverse_turned, 1)

            def tile(b, c, p, first, second, last):
                if first:
                    scores(b, c, p, 0, True)
                    scores(b, c, p, 1, True)
                for r in range(ROWS):
                    ahead = later(b, c, p, r, first, last, 2)
                    if ahead:
                        scores(*ahead)
                    turn(b, c, p, r, first)
                    if r > 0:
                        times_v(b, c, p, r - 1, first)
                    elif not first:
                        finish(b, c - 1, 1 - p, second)
                if last:
                    finish(b, c, p, False)

            tile_loop(pe, tile)

        @block.vector
        def _(dve):
            def bias_and_max(b, c, p, r, first):
                s = (b * PER_B + c) * ROWS + r
                dve.wait_ge(scores_done, s + 1 + 2 * ROWS)
                dve.wait_ge(exp_done, (s + 1) * SLOTS)
                blocks = 1 if first else 2
                for a in range(blocks):
                    last = dve.scalar_tensor_tensor(
                        biased[r % 2][:, a, :, :].rearrange("p s j -> p (s j)"), psum[:, r % 2 * 2 + a, :], float(DH0) ** -0.5,
                        slope[:, r, a, :, :].rearrange("p s j -> p (s j)"), ALU.mult, ALU.add)
                last.then_inc(biased_done, 1)
                dve.wait_ge(biased_done, s + 3)
                dve.tensor_reduce(low[:, r % 2, :], biased[r % 2][:, 0:blocks, :, :].rearrange("p a s j -> p s a j"),
                                  mybir.AxisListType.XY, ALU.max, negate=True).then_inc(max_done, 1)

            def copy_turned(b, c, p, r, first):
                s = (b * PER_B + c) * ROWS + r
                dve.wait_ge(turned, s + 3)
                dve.wait_ge(used, s + 7)
                dve.tensor_copy(half_of(probsT[r % 2], first, 0), half_of_bank(first, 0)).then_inc(own_ready, 1)

            def invert(b, c, p):
                n = b * PER_B + c
                dve.wait_ge(exp_done, (n + 1) * ROWS * SLOTS + 2 * SLOTS)
                dve.wait_ge(spread_done, n + 1)
                dve.reciprocal(inverse[:, :], sums[:, p, :]).then_inc(inverse_done, 1)
                dve.wait_ge(inverse_done, n + 1)
                dve.wait_ge(inverse_turned, n + 1)
                dve.tensor_copy(spread_inv[p][:, :, :], inverse[:, :].unsqueeze(2).to_broadcast([P, H, DH0])).then_inc(
                    spread_done, 1)

            def finish(b, c, p):
                n = b * PER_B + c
                dve.wait_ge(used, (n + 3) * ROWS)
                dve.wait_ge(inverse_copied, n + 1)
                dve.tensor_tensor(attended[:, bass.ts(n, P)], psum[:, 6 + p, 0:P], inverseT[:, p, :],
                                  ALU.mult).then_inc(y_done, 1)

            def tile(b, c, p, first, second, last):
                if first:
                    bias_and_max(b, c, p, 0, True)
                    bias_and_max(b, c, p, 1, True)
                for r in range(ROWS):
                    ahead = later(b, c, p, r, first, last, 2)
                    if ahead:
                        bias_and_max(*ahead)
                    copy_turned(b, c, p, r, first)
                    if r == 1 and not first:
                        finish(b, c - 1, 1 - p)
                invert(b, c, p)
                if last:
                    finish(b, c, p)

            tile_loop(dve, tile)

        @block.scalar
        def _(act):
            def exponentials(b, c, p, r, first):
                s = (b * PER_B + c) * ROWS + r
                act.wait_ge(max_done, s + 1)
                act.wait_ge(turned, s + 1)
                for h in range(SLOTS):
                    act.activation(expd[r % 2][:, 0:1 if first else 2, h, :], biased[r % 2][:, 0:1 if first else 2, h, :], ACT.Exp,
                                   bias=low[:, r % 2, h:h + 1],
                                   accum_out=sums[:, p, r * SLOTS + h:r * SLOTS + h + 1]).then_inc(exp_done, 1)

            def copy_turned(b, c, p, r, first):
                s = (b * PER_B + c) * ROWS + r
                act.wait_ge(turned, s + 3)
                act.wait_ge(used, s + 7)
                act.copy(half_of(probsT[r % 2], first, 1), half_of_bank(first, 1)).then_inc(other_ready, 1)

            def copy_inverse(b, c, p):
                n = b * PER_B + c
                act.wait_ge(inverse_turned, n + 3)
                act.wait_ge(y_done, n + 1)
                act.copy(inverseT[:, p, :], psum[:, 6 + p, P:2 * P]).then_inc(inverse_copied, 1)

            def tile(b, c, p, first, second, last):
                if first:
                    exponentials(b, c, p, 0, True)
                for r in range(ROWS):
                    ahead = later(b, c, p, r, first, last, 1)
                    if ahead:
                        exponentials(*ahead)
                    copy_turned(b, c, p, r, first)
                    if r == 0 and not first:
                        copy_inverse(b, c - 1, 1 - p)
                if last:
                    copy_inverse(b, c, p)

            tile_loop(act, tile)


WIDE = 64
HID = H * WIDE
BLOCKS = HID // P
RMS_EPS = 2.0 ** -23


def gated_attention(chip, norm):
    with Stage(chip, "gla") as outer:
        reach = outer.sb("reach", [P, TILES, H])
        left = outer.sb("left", [P, TILES, H])
        whole = outer.sb("whole", [P, TILES, BLOCKS])
        reach_rows = chip.nc.dram_tensor("reach_rows", (H, TOK), F32).ap()
        gained_rows = chip.nc.dram_tensor("gained_rows", (H, TOK), F32).ap()
        wd, bd = outer.sb("wd", [P, H]), outer.sb("bd", [P, H])
        sums = outer.sb("sums", [P, 3, P])
        w = GatedWeights(outer)
        norm([(wd[:, :], chip.dram["gla_wd"]), (bd[:, :], chip.dram["gla_bd"]), (sums[:, :, :], chip.dram["gla_sums"])]
             + w.loads(chip))
        decay_stage(chip, wd, bd, sums, reach, left, whole, reach_rows, gained_rows)
        gated_chunks(chip, w, reach, left, whole, reach_rows, gained_rows)


class GatedWeights:

    def __init__(self, st):
        self.w_tok = st.sb("w_tok", [P, 3, HID])
        self.wq, self.wog = st.sb("wq", [P, HID]), st.sb("wog", [P, HID])
        self.wo = st.sb("wo", [P, BLOCKS, D])
        self.norm_w = st.sb("norm_w", [P, BLOCKS])
        self.causal = st.sb("causal", [P, P])

    def loads(self, chip):
        pairs = [(self.w_tok[:, k, :], chip.dram[nm]) for k, nm in enumerate(("gla_wk", "gla_wg", "gla_wv"))]
        return pairs + [(self.wq[:, :], chip.dram["gla_wq"]), (self.wog[:, :], chip.dram["gla_wog"]),
                        (self.wo[:, :, :], chip.dram["gla_wo"]), (self.norm_w[:, :], chip.dram["gla_norm_w"]),
                        (self.causal[:, :], chip.dram["causal"])]


def decay_stage(chip, wd, bd, sums, reach, left, whole, reach_rows, gained_rows):
    N = TILES * H
    with Stage(chip, "decay") as st:
        z, size, log1p, g = (st.sb(n, [P, TILES, H]) for n in ("z", "size", "log1p", "g"))
        reachT, gainedT = st.sb("reachT", [H, TOK]), st.sb("gainedT", [H, TOK])
        logits_done, own = st.sem("logits_done"), st.sem("dve_steps")
        asked, answered = st.sem("asked"), st.sem("answered")
        g_done, sums_done, copied = st.sem("g_done"), st.sem("sums_done"), st.sem("copied")
        turned, stored, rows_copied = st.sem("turned"), st.sem("stored"), st.sem("rows_copied")
        gained_done = st.sem("gained_done")
        block = st.block()
        psum = chip.psum
        logits = psum[:, 0, 0:N].rearrange("p (t h) -> p t h", h=H)

        @block.sync
        def _(sp):
            sp.wait_ge(rows_copied, 4)
            sp.dma_start(reach_rows, reachT[:, :]).then_inc(stored, 16)
            sp.wait_ge(gained_done, 1)
            sp.dma_start(gained_rows, gainedT[:, :]).then_inc(stored, 16)
            sp.wait_ge(stored, 32)

        @block.tensor
        def _(pe):
            for t in range(TILES):
                mm = pe.matmul(logits[:, t, :], chip.xnT[:, t * P:(t + 1) * P], wd[:, :], start=True, stop=True)
            mm.then_inc(logits_done, 1)
            pe.wait_ge(g_done, 1)
            for k in range(3):
                mm = pe.matmul(psum[:, 1 + k, 0:N], sums[:, k, :], g[:, :, :].rearrange("p t h -> p (t h)"), start=True, stop=True)
            mm.then_inc(sums_done, 1)
            pe.wait_ge(copied, 1)
            for t in range(TILES):
                turn = nc_t(pe, psum[0:H, 4 + t // 4, t % 4 * P:(t % 4 + 1) * P], reach[:, t, :], chip)
                if t % 4 == 3:
                    turn.then_inc(turned, 1)

        @block.vector
        def _(dve):
            done = Chain(dve, own).done
            dve.wait_ge(logits_done, 1)
            done(dve.tensor_tensor(z[:, :, :], logits, bd[:, :].unsqueeze(1).to_broadcast([P, TILES, H]), ALU.add))
            done(dve.tensor_scalar(size[:, :, :], z[:, :, :], -1.0, None, ALU.mult))
            dve.tensor_tensor(size[:, :, :], size[:, :, :], z[:, :, :], ALU.min).then_inc(asked, 1)
            dve.wait_ge(answered, 1)
            dve.tensor_scalar(log1p[:, :, :], log1p[:, :, :], 1.0, None, ALU.add).then_inc(asked, 1)
            dve.wait_ge(answered, 2)
            done(dve.scalar_tensor_tensor(g[:, :, :], z[:, :, :], 0.0, log1p[:, :, :], ALU.max, ALU.add))
            dve.tensor_scalar(g[:, :, :], g[:, :, :], -1.0, None, ALU.mult).then_inc(g_done, 1)
            dve.wait_ge(sums_done, 1)
            dve.tensor_copy(reach[:, :, :].rearrange("p t h -> p (t h)"), psum[:, 1, 0:N]).then_inc(copied, 1)
            for q in range(4):
                dve.wait_ge(turned, q + 1)
                dve.tensor_copy(reachT[:, q * GROUP:(q + 1) * GROUP], psum[0:H, 4 + q, :]).then_inc(rows_copied, 1)

        @block.scalar
        def _(act):
            act.wait_ge(asked, 1)
            act.activation(log1p[:, :, :], size[:, :, :], ACT.Exp).then_inc(answered, 1)
            act.wait_ge(asked, 2)
            act.activation(log1p[:, :, :], log1p[:, :, :], ACT.Ln).then_inc(answered, 1)
            act.wait_ge(sums_done, 1)
            act.activation(left[:, :, :].rearrange("p t h -> p (t h)"), psum[:, 2, 0:N], ACT.Exp)
            pairs = psum[:, 3, 0:N].rearrange("p (t m two) -> p t m two", m=BLOCKS, two=2)
            for half in range(2):
                rows = slice(half * WIDE, (half + 1) * WIDE)
                act.activation(whole[rows, :, :], pairs[rows, :, :, half], ACT.Exp)
            act.wait_ge(rows_copied, 4)
            act.activation(gainedT[:, :], reachT[:, :], ACT.Exp).then_inc(gained_done, 1)


def rows_of_chunks(eng, start, chunk):
    with eng.Fori(0, B) as b:
        start(b)
        with eng.Fori(0, PER_B // 2 - 1) as pair:
            for p in range(2):
                chunk(b, b * PER_B + pair * 2 + p, p, False)
        for p in range(2):
            chunk(b, b * PER_B + PER_B - 2 + p, p, p == 1)


def by_head(buf, width=WIDE):
    return buf[:, :].rearrange("p (h e) -> p h e", e=width)


def spread(v, width=WIDE):
    return v[:, :].unsqueeze(2).to_broadcast([P, v.shape[1], width])


def head_of(k):
    return k // 8 * 8 + k % 4 * 2 + k // 4 % 2


def gated_chunks(chip, w, reach, left, whole, reach_rows, gained_rows):
    with Stage(chip, "gla_chunks") as st:
        def count(name, ahead=1):
            return st.sem(name, ahead=ahead)

        w_tok, wq, wog, wo, norm_w, causal = w.w_tok, w.wq, w.wog, w.wo, w.norm_w, w.causal
        ones = st.sb("ones", [P, P])
        xc = [st.sb(f"xc{p}", [P, P]) for p in range(2)]
        reach_bc = st.sb("reach_bc", [P, H, P])
        gained_bc = st.sb("gained_bc", [P, BLOCKS, P])
        k_tok, v_tok = ([st.sb(f"{n}{p}", [P, HID]) for p in range(2)] for n in ("k_tok", "v_tok"))
        gate, v_left = st.sb("gate", [P, HID]), st.sb("v_left", [P, HID])
        og, z, square, qT, qd, kT = (st.sb(n, [P, BLOCKS, P]) for n in ("og", "z", "square", "qT", "qd", "kT"))
        decay, probs = st.sb("decay", [P, H, P]), st.sb("probs", [P, H, P])
        rstd = st.sb("rstd", [P, P])
        state = st.sb("state", [P, BLOCKS, P])
        ones_done, wo_ready = st.sem("ones_done"), st.sem("wo_ready")
        x_in = count("x_in")
        rows_in, gained_in = st.sem("rows_in"), st.sem("gained_in")
        k_done, gate_done, v_done, og_done, q_done = (count(n + "_done") for n in ("k", "gate", "v", "og", "q"))
        gate_ready, k_ready, v_ready, og_ready, q_ready = (count(n + "_ready") for n in ("gate", "k", "v", "og", "q"))
        kt_done, kt_ready = count("kt_done"), count("kt_ready")
        arg_done, decay_done = count("arg_done"), count("decay_done")
        score_done, probs_done = count("score_done"), count("probs_done")
        v_left_done, qd_done, past_done = count("v_left_done"), count("qd_done"), count("past_done")
        intra_done, z_ready, square_done = count("intra_done"), count("z_ready"), count("square_done")
        update_done, decayed = count("update_done"), count("decayed")
        state_done = count("state_done")
        y_done, power_done, shifted, std_done, rstd_done = (
            count(n) for n in ("y_done", "power_done", "shifted", "std_done", "rstd_done"))
        y_read = count("y_read", ahead=2)
        block = st.block()
        psum = chip.psum
        R, PLACES = 4, 4

        def two(n):
            return psum[:, n:n + 2, :].rearrange("p a f -> p (a f)")

        gate_ps, v_ps, kT_ps = two(0), two(0), two(0)
        k_ps, q_ps, og_ps = two(2), two(2), two(2)
        update_ps, out_ps = two(4).rearrange("p (m f) -> p m f", f=P), two(6)
        y_ps, power_ps = psum[:, 0, 0:P], psum[:, 0, P:2 * P]

        def flat(buf):
            return buf[:, :, :].rearrange("p m i -> p (m i)")

        halves = [slice(0, WIDE), slice(WIDE, P)]

        def rows_of(h):
            return slice(h % 2 * WIDE, h % 2 * WIDE + WIDE)

        @block.sync
        def _(sp):
            with sp.Fori(0, TILES) as n:
                sp.wait_ge(arg_done, n + 1)
                sp.dma_start(reach_bc[:, :, :], reach_rows[:, bass.ts(n, P)].unsqueeze(0).to_broadcast([P, H, P])).then_inc(rows_in, 16)
                sp.wait_ge(qd_done, n + 1)
                for half in range(2):
                    rows = gained_rows.rearrange("(m two) t -> two m t", two=2)[half, :, bass.ts(n, P)]
                    sp.dma_start(gained_bc[half * WIDE:(half + 1) * WIDE, :, :],
                                 rows.unsqueeze(0).to_broadcast([WIDE, BLOCKS, P])).then_inc(gained_in, 16)

        @block.gpsimd
        def _(pool):
            pool.memset(ones[:, :], 1.0).then_inc(ones_done, 1)
            with pool.Fori(0, TILES // 2) as pair:
                for p in range(2):
                    n = pair * 2 + p
                    pool.wait_ge(og_done, n + 1)
                    pool.tensor_copy(xc[p][:, :], chip.xnT[:, bass.ts(n, P)]).then_inc(x_in, 1)
                    pool.wait_ge(v_ready, n + 2)
                    pool.wait_ge(update_done, n + 1)
                    pool.tensor_tensor(by_head(v_left), by_head(v_tok[p]), left[:, bass.ds(n, 1), :].rearrange(
                        "p a h -> p (a h)").unsqueeze(2).to_broadcast([P, H, WIDE]), ALU.mult).then_inc(v_left_done, 1)
                    pool.wait_ge(q_ready, n + 2)
                    pool.wait_ge(gained_in, (n + 1) * 32)
                    pool.wait_ge(past_done, n + 1)
                    pool.tensor_tensor(qd[:, :, :], qT[:, :, :], gained_bc[:, :, :], ALU.mult).then_inc(qd_done, 1)

        @block.tensor
        def _(pe):
            pe.wait_ge(ones_done, 1)
            pe.wait_ge(wo_ready, 1)

            def token_major(out, which, p):
                for half in range(2):
                    cols = slice(half * GROUP, (half + 1) * GROUP)
                    mm = pe.matmul(out[:, cols], xc[p][:, :], w_tok[:, which, cols], start=True, stop=True)
                return mm

            def feature_major(out, weights, p):
                for m in range(BLOCKS):
                    cols = slice(m * P, (m + 1) * P)
                    mm = pe.matmul(out[:, cols], weights[:, cols], xc[p][:, :], start=True, stop=True)
                return mm

            def gates(n, p):
                pe.wait_ge(x_in, n + 2)
                token_major(gate_ps, 1, p).then_inc(gate_done, 1)

            def keys(n, p):
                pe.wait_ge(og_ready, n + 1)
                token_major(k_ps, 0, p).then_inc(k_done, 1)

            def values(n, p):
                pe.wait_ge(gate_ready, n + 2)
                token_major(v_ps, 2, p).then_inc(v_done, 1)

            def queries(n, p):
                pe.wait_ge(k_ready, n + 2)
                feature_major(q_ps, wq, p).then_inc(q_done, 1)

            def turned_keys(n, p):
                pe.wait_ge(v_ready, n + 2)
                for m in range(BLOCKS):
                    mm = nc_t(pe, kT_ps[:, m * P:(m + 1) * P], k_tok[p][:, m * P:(m + 1) * P], chip)
                mm.then_inc(kt_done, 1)

            def output_gates(n, p):
                pe.wait_ge(q_ready, n + 2)
                feature_major(og_ps, wog, p).then_inc(og_done, 1)

            def score_rounds(n, rounds):
                for s in range(PLACES):
                    for r in rounds:
                        h = head_of(r * PLACES + s)
                        mm = pe.matmul(psum[:, 4 + r % 2, s * P:(s + 1) * P], kT[rows_of(h), h // 2, :],
                                       qT[rows_of(h), h // 2, :], start=True, stop=True)
                        if s == PLACES - 1:
                            mm.then_inc(score_done, 1)

            def intra(n, p, r):
                pe.wait_ge(probs_done, n * R + r + 2)
                for k in range(r * PLACES, (r + 1) * PLACES):
                    h = head_of(k)
                    mm = pe.matmul(out_ps[rows_of(h), h // 2 * P:(h // 2 + 1) * P], v_tok[p][:, h * WIDE:(h + 1) * WIDE],
                                   probs[:, k, :], start=False, stop=(k % PLACES == PLACES - 1), skip_group_check=True)
                if r == R - 1:
                    mm.then_inc(intra_done, 1)

            def start(b):
                n = b * PER_B
                pe.wait_ge(y_read, n + 2)
                gates(n, 0)
                keys(n, 0)
                values(n, 0)
                queries(n, 0)
                turned_keys(n, 0)
                output_gates(n, 0)

            def chunk(b, n, p, last):
                pe.wait_ge(state_done, n + b + 2)
                pe.wait_ge(kt_ready, n + 2)
                score_rounds(n, (0, 1))
                pe.wait_ge(qd_done, n + 2)
                pe.wait_ge(square_done, n + 1)
                for m in range(BLOCKS):
                    mm = pe.matmul(out_ps[:, m * P:(m + 1) * P], state[:, m, :], qd[:, m, :], start=(m % (BLOCKS // 2) == 0),
                                   stop=False, skip_group_check=True)
                mm.then_inc(past_done, 1)
                if not last:
                    pe.wait_ge(y_read, n + 2)
                    gates(n + 1, 1 - p)
                pe.wait_ge(probs_done, n * R + 3)
                score_rounds(n, (2, 3))
                if not last:
                    keys(n + 1, 1 - p)
                intra(n, p, 0)
                intra(n, p, 1)
                if not last:
                    values(n + 1, 1 - p)
                intra(n, p, 2)
                intra(n, p, 3)
                pe.wait_ge(v_left_done, n + 2)
                for m in range(BLOCKS):
                    cols = slice(m * P, (m + 1) * P)
                    mm = pe.matmul(update_ps[:, m, :], k_tok[p][:, cols], v_left[:, cols], start=True, stop=True)
                mm.then_inc(update_done, 1)
                if not last:
                    queries(n + 1, 1 - p)
                    turned_keys(n + 1, 1 - p)
                    output_gates(n + 1, 1 - p)
                    pe.wait_ge(kt_ready, n + 3)
                pe.wait_ge(z_ready, n + 2)
                for m in range(BLOCKS):
                    mm = pe.matmul(y_ps, wo[:, m, :], z[:, m, :], start=(m == 0), stop=(m == BLOCKS - 1))
                mm.then_inc(y_done, 1)
                pe.wait_ge(square_done, n + 2)
                for m in range(BLOCKS):
                    mm = pe.matmul(power_ps, ones[:, :], square[:, m, :], start=(m == 0), stop=(m == BLOCKS - 1))
                mm.then_inc(power_done, 1)

            rows_of_chunks(pe, start, chunk)

        @block.vector
        def _(dve):
            dve.tensor_tensor(wo[:, :, :], wo[:, :, :], spread(norm_w, D), ALU.mult).then_inc(wo_ready, 1)

            def take_k(n, p):
                dve.wait_ge(gate_ready, n + 2)
                dve.wait_ge(k_done, n + 2)
                dve.wait_ge(update_done, n + 1 if p is None else n)
                dve.tensor_tensor(k_tok[p or 0][:, :], gate[:, :], k_ps, ALU.mult).then_inc(k_ready, 1)

            def decay_args(n):
                dve.wait_ge(rows_in, (n + 1) * 16)
                dve.wait_ge(probs_done, n * R + 1)
                for k in range(H):
                    h = head_of(k)
                    last = dve.scalar_tensor_tensor(decay[:, k, :], reach_bc[:, h, :], reach[:, bass.ds(n, 1), h:h + 1].rearrange(
                        "p a h -> p (a h)"), causal[:, :], ALU.subtract, ALU.add)
                last.then_inc(arg_done, 1)

            def take_kt(n):
                dve.wait_ge(kt_done, n + 2)
                dve.wait_ge(score_done, n * R + 1)
                dve.tensor_copy(flat(kT), kT_ps).then_inc(kt_ready, 1)

            def start(b):
                n = b * PER_B
                dve.wait_ge(past_done, n + 1)
                dve.wait_ge(state_done, b * (PER_B + 1) + 1)
                dve.memset(state[:, :, :], 0.0).then_inc(state_done, 1)
                take_k(n, None)
                decay_args(n)
                take_kt(n)

            def chunk(b, n, p, last):
                dve.wait_ge(decay_done, n + 2)
                for r in range(R):
                    dve.wait_ge(score_done, n * R + r + 2)
                    dve.wait_ge(intra_done, n + 1)
                    heads = slice(r * PLACES, (r + 1) * PLACES)
                    dve.tensor_tensor(probs[:, heads, :].rearrange("p s i -> p (s i)"), psum[:, 4 + r % 2, :],
                                      decay[:, heads, :].rearrange("p s i -> p (s i)"), ALU.mult).then_inc(probs_done, 1)
                if not last:
                    take_k(n + 1, 1 - p)
                    decay_args(n + 1)
                dve.wait_ge(past_done, n + 2)
                dve.wait_ge(state_done, n + b + 2)
                for rows in halves:
                    mult = dve.tensor_tensor(state[rows, :, rows], state[rows, :, rows], whole[rows, bass.ds(n, 1), :].rearrange(
                        "p a m -> p (a m)").unsqueeze(2).to_broadcast([WIDE, BLOCKS, WIDE]), ALU.mult)
                mult.then_inc(decayed, 1)
                dve.wait_ge(intra_done, n + 2)
                dve.wait_ge(og_ready, n + 2)
                dve.wait_ge(y_done, n + 1)
                dve.tensor_tensor(flat(z), out_ps, flat(og), ALU.mult).then_inc(z_ready, 1)
                dve.wait_ge(update_done, n + 2)
                dve.wait_ge(decayed, n + 2)
                for rows in halves:
                    add = dve.tensor_tensor(state[rows, :, rows], state[rows, :, rows], update_ps[rows, :, rows], ALU.add)
                add.then_inc(state_done, 1)
                if not last:
                    take_kt(n + 1)
                dve.wait_ge(power_done, n + 2)
                dve.tensor_scalar(rstd[:, :], power_ps, 1.0 / HID, RMS_EPS, ALU.mult, ALU.add).then_inc(shifted, 1)
                dve.wait_ge(std_done, n + 2)
                dve.reciprocal(rstd[:, :], rstd[:, :]).then_inc(rstd_done, 1)
                dve.wait_ge(rstd_done, n + 2)
                dve.wait_ge(y_done, n + 2)
                dve.tensor_tensor(chip.yT[:, bass.ts(n, P)], y_ps, rstd[:, :], ALU.mult).then_inc(y_read, 1)

            rows_of_chunks(dve, start, chunk)

        @block.scalar
        def _(act):
            def take_gate(n):
                act.wait_ge(gate_done, n + 2)
                act.wait_ge(k_ready, n + 1)
                act.activation(gate[:, :], gate_ps, ACT.Sigmoid).then_inc(gate_ready, 1)

            def take_v(n, p):
                act.wait_ge(v_done, n + 2)
                act.wait_ge(intra_done, n)
                act.wait_ge(v_left_done, n)
                act.copy(v_tok[p][:, :], v_ps).then_inc(v_ready, 1)

            def take_decay(n):
                act.wait_ge(arg_done, n + 2)
                act.activation(decay[:, :, :], decay[:, :, :], ACT.Exp).then_inc(decay_done, 1)

            def take_q(n):
                act.wait_ge(q_done, n + 2)
                act.wait_ge(score_done, n * R + 1)
                act.wait_ge(qd_done, n + 1)
                act.copy(flat(qT), q_ps).then_inc(q_ready, 1)

            def take_og(n):
                act.wait_ge(og_done, n + 2)
                act.wait_ge(z_ready, n + 1)
                act.activation(flat(og), og_ps, ACT.Sigmoid).then_inc(og_ready, 1)

            def start(b):
                n = b * PER_B
                take_gate(n)
                act.wait_ge(intra_done, n + 1)
                act.wait_ge(v_left_done, n + 1)
                act.wait_ge(v_done, n + 2)
                act.copy(v_tok[0][:, :], v_ps).then_inc(v_ready, 1)
                take_decay(n)
                take_q(n)
                take_og(n)

            def chunk(b, n, p, last):
                if not last:
                    take_gate(n + 1)
                    take_v(n + 1, 1 - p)
                    take_decay(n + 1)
                act.wait_ge(z_ready, n + 2)
                act.wait_ge(power_done, n + 1)
                act.activation(flat(square), out_ps, ACT.Square).then_inc(square_done, 1)
                if not last:
                    take_q(n + 1)
                    take_og(n + 1)
                act.wait_ge(shifted, n + 2)
                act.activation(rstd[:, :], rstd[:, :], ACT.Sqrt).then_inc(std_done, 1)

            rows_of_chunks(act, start, chunk)


FINITE = 3e38
R_BANKS, R_HEADS = 4, 4


def feature_attention(chip, norm):
    W1 = WIDE + 1
    with Stage(chip, "features") as st:
        def count(name):
            return st.sem(name, ahead=1)

        wq, wk, wv = (st.sb(n, [P, HID]) for n in ("wq", "wk", "wv"))
        wo = st.sb("wo", [P, BLOCKS, D])
        bo = st.sb("bo", [P, 1])
        omega = st.sb("omega", [P, P])
        half_norm = st.sb("half_norm", [P, P])
        allowed = st.sb("allowed", [P, P])
        xc = [st.sb(f"xc{p}", [P, P]) for p in range(2)]
        qT, kT, q2, k2, phi_q, phi_k, oT = (st.sb(n, [P, BLOCKS, P]) for n in ("qT", "kT", "q2", "k2", "phi_q", "phi_k", "oT"))
        k_tok, o = st.sb("k_tok", [P, HID]), st.sb("o", [P, H, WIDE])
        v_tok = st.sb("v_tok", [P, H, W1])
        probs = st.sb("probs", [P, H, P])
        z = st.sb("z", [P, R_BANKS, R_HEADS])
        state = st.sb("state", [P, BLOCKS, W1])
        norm([(wq[:, :], chip.dram["fea_wq"]), (wk[:, :], chip.dram["fea_wk"]), (wv[:, :], chip.dram["fea_wv"]),
              (wo[:, :, :], chip.dram["fea_wo"]), (bo[:, :], chip.dram["fea_bo"]), (omega[:, :], chip.dram["fea_omega"]),
              (half_norm[:, :], chip.dram["fea_half_norm"]), (allowed[:, :], chip.dram["allowed"])])
        ones_done, x_in = st.sem("ones_done"), count("x_in")
        q_done, k_done, v_done = count("q_done"), count("k_done"), count("v_done")
        q_ready, k_ready, v_ready = count("q_ready"), count("k_ready"), count("v_ready")
        squares = count("squares")
        arg_done, phi_ready = count("arg_done"), count("phi_ready")
        kt_done, kt_ready = count("kt_done"), count("kt_ready")
        score_done, probs_done = count("score_done"), count("probs_done")
        past_done, update_done = count("past_done"), count("update_done")
        state_done = count("state_done")
        out_done, z_steps, o_ready = count("out_done"), count("z_steps"), count("o_ready")
        ot_done, ot_ready, y_done, y_read = count("ot_done"), count("ot_ready"), count("y_done"), count("y_read")
        block = st.block()
        psum = chip.psum
        R = R_BANKS

        def two(n):
            return psum[:, n:n + 2, :].rearrange("p a f -> p (a f)")

        q_ps, k_ps, v_ps, kt_ps, oT_ps = two(0), two(2), two(4), two(6), two(6)
        out_ps = psum[:, 4:8, 0:R_HEADS * W1].rearrange("p r (s w) -> p r s w", w=W1)
        update_ps = psum[:, 0:2, 0:R_HEADS * W1].rearrange("p a (m w) -> p a m w", w=W1)
        y_ps = psum[:, 6, 0:P]

        def flat(buf):
            return buf[:, :, :].rearrange("p m i -> p (m i)")

        @block.gpsimd
        def _(pool):
            pool.memset(v_tok[:, :, :], 1.0).then_inc(ones_done, 1)
            with pool.Fori(0, TILES // 2) as pair:
                for p in range(2):
                    n = pair * 2 + p
                    pool.wait_ge(v_done, n + 1)
                    pool.tensor_copy(xc[p][:, :], chip.xnT[:, bass.ts(n, P)]).then_inc(x_in, 1)
                    for k, (ready, src, dst) in enumerate(((q_ready, qT, q2), (k_ready, kT, k2))):
                        pool.wait_ge(ready, n + 2)
                        pool.wait_ge(arg_done, 2 * n + 1)
                        pool.tensor_tensor(dst[:, :, :], src[:, :, :], src[:, :, :], ALU.mult).then_inc(squares, 1)

        @block.tensor
        def _(pe):

            def ahead(b, n, p):
                pe.wait_ge(x_in, n + 2)
                pe.wait_ge(state_done, n + b + 2)
                pe.wait_ge(probs_done, n * R + 1)
                for ps, w, sem in ((q_ps, wq, q_done), (k_ps, wk, k_done)):
                    for m in range(BLOCKS):
                        mm = pe.matmul(ps[:, m * P:(m + 1) * P], w[:, m * P:(m + 1) * P], xc[p][:, :], start=True, stop=True)
                    mm.then_inc(sem, 1)
                pe.wait_ge(o_ready, n + 1)
                for half in range(2):
                    cols = slice(half * GROUP, (half + 1) * GROUP)
                    mm = pe.matmul(v_ps[:, cols], xc[p][:, :], wv[:, cols], start=True, stop=True)
                mm.then_inc(v_done, 1)

            def chunk(b, n, p, last):
                for k, (ps, raw, sq) in enumerate(((q_ps, qT, q2), (k_ps, kT, k2))):
                    pe.wait_ge(squares, 2 * n + k + 2)
                    for half in range(2):
                        cols = slice(half * GROUP, (half + 1) * GROUP)
                        pe.matmul(ps[:, cols], omega[:, :], flat(raw)[:, cols], start=True, stop=False)
                        mm = pe.matmul(ps[:, cols], half_norm[:, :], flat(sq)[:, cols], start=False, stop=True)
                    mm.then_inc(arg_done, 1)
                pe.wait_ge(phi_ready, 2 * n + 3)
                pe.wait_ge(y_read, n + 1)
                for m in range(BLOCKS):
                    mm = nc_t(pe, kt_ps[:, m * P:(m + 1) * P], phi_k[:, m, :], chip)
                mm.then_inc(kt_done, 1)
                for k in range(H):
                    r, s = k // (2 * R_HEADS) * 2 + k % 2, k // 2 % R_HEADS
                    h = head_of(r * R_HEADS + s)
                    rows = slice(h % 2 * WIDE, h % 2 * WIDE + WIDE)
                    mm = pe.matmul(psum[:, r, s * P:(s + 1) * P], phi_k[rows, h // 2, :], phi_q[rows, h // 2, :],
                                   start=True, stop=True)
                    if s == R_HEADS - 1:
                        mm.then_inc(score_done, 1)
                pe.wait_ge(v_ready, n + 2)
                pe.wait_ge(kt_ready, n + 2)
                pe.wait_ge(state_done, n + b + 2)
                for k in range(H):
                    r, s = k // (2 * R_HEADS) * 2 + k % 2, k // 2 % R_HEADS
                    h = head_of(r * R_HEADS + s)
                    rows = slice(h % 2 * WIDE, h % 2 * WIDE + WIDE)
                    mm = pe.matmul(out_ps[:, r, s, :], phi_q[rows, h // 2, :], state[rows, h // 2, :],
                                   start=(s == 0), stop=False, skip_group_check=True)
                mm.then_inc(past_done, 1)
                pe.wait_ge(probs_done, n * R + 3)
                for h in range(H):
                    rows = slice(h % 2 * WIDE, h % 2 * WIDE + WIDE)
                    m = h // 2
                    mm = pe.matmul(update_ps[rows, m // R_HEADS, m % R_HEADS, :], k_tok[:, h * WIDE:(h + 1) * WIDE],
                                   v_tok[:, h, :], start=True, stop=True)
                mm.then_inc(update_done, 1)
                for k in range(H):
                    if k % R_HEADS == 0:
                        pe.wait_ge(probs_done, n * R + k // R_HEADS + 2)
                    mm = pe.matmul(out_ps[:, k // R_HEADS, k % R_HEADS, :], probs[:, k, :], v_tok[:, head_of(k), :],
                                   start=False, stop=(k % R_HEADS == R_HEADS - 1), skip_group_check=True)
                mm.then_inc(out_done, 1)
                if not last:
                    ahead(b, n + 1, 1 - p)
                pe.wait_ge(o_ready, n + 2)
                for m in range(BLOCKS):
                    mm = nc_t(pe, oT_ps[:, m * P:(m + 1) * P], o[:, 2 * m:2 * m + 2, :].rearrange("p a e -> p (a e)"), chip)
                mm.then_inc(ot_done, 1)
                pe.wait_ge(ot_ready, n + 2)
                for m in range(BLOCKS):
                    mm = pe.matmul(y_ps, wo[:, m, :], oT[:, m, :], start=(m == 0), stop=(m == BLOCKS - 1))
                mm.then_inc(y_done, 1)

            rows_of_chunks(pe, lambda b: ahead(b, b * PER_B, 0), chunk)

        @block.vector
        def _(dve):
            dve.wait_ge(ones_done, 1)

            def take_qk(n):
                for done, ready, ps, dst in ((q_done, q_ready, q_ps, qT), (k_done, k_ready, k_ps, kT)):
                    dve.wait_ge(done, n + 2)
                    dve.wait_ge(squares, 2 * n + 1)
                    dve.wait_ge(arg_done, 2 * n + 1)
                    dve.tensor_copy(flat(dst), ps).then_inc(ready, 1)

            def start(b):
                dve.wait_ge(past_done, b * PER_B + 1)
                dve.wait_ge(state_done, b * (PER_B + 1) + 1)
                dve.memset(state[:, :, :], 0.0).then_inc(state_done, 1)
                take_qk(b * PER_B)

            def chunk(b, n, p, last):
                dve.wait_ge(kt_done, n + 2)
                dve.wait_ge(update_done, n + 1)
                dve.tensor_copy(k_tok[:, :], kt_ps).then_inc(kt_ready, 1)
                for r in range(R):
                    dve.wait_ge(score_done, n * R + r + 2)
                    dve.wait_ge(out_done, n + 1)
                    heads = slice(r * R_HEADS, (r + 1) * R_HEADS)
                    dve.scalar_tensor_tensor(probs[:, heads, :], psum[:, r, :].rearrange("p (s i) -> p s i", i=P), FINITE,
                                             allowed[:, :].unsqueeze(1).to_broadcast([P, R_HEADS, P]), ALU.min,
                                             ALU.mult).then_inc(probs_done, 1)
                dve.wait_ge(update_done, n + 2)
                dve.wait_ge(past_done, n + 2)
                dve.wait_ge(state_done, n + b + 2)
                halves = state[:, :, :].rearrange("p (a m) w -> p a m w", a=2)
                dve.tensor_tensor(halves, halves, update_ps, ALU.add).then_inc(state_done, 1)
                dve.wait_ge(out_done, n + 2)
                dve.wait_ge(o_ready, n + 1)
                dve.tensor_scalar(z[:, :, :], out_ps[:, :, :, WIDE], WIDE * 1e-6, None, ALU.add).then_inc(z_steps, 1)
                dve.wait_ge(z_steps, 2 * n + 2)
                dve.reciprocal(z[:, :, :], z[:, :, :]).then_inc(z_steps, 1)
                dve.wait_ge(z_steps, 2 * n + 3)
                dve.wait_ge(ot_done, n + 1)
                dve.tensor_tensor(o[:, :, :].rearrange("p (r s) e -> p r s e", s=R_HEADS), out_ps[:, :, :, 0:WIDE],
                                  z[:, :, :].unsqueeze(3).to_broadcast([P, R, R_HEADS, WIDE]), ALU.mult).then_inc(o_ready, 1)
                if not last:
                    take_qk(n + 1)

            rows_of_chunks(dve, start, chunk)

        @block.scalar
        def _(act):
            act.wait_ge(ones_done, 1)

            def chunk(b, n, p, last):
                act.wait_ge(v_done, n + 2)
                act.wait_ge(out_done, n + 1)
                act.copy(v_tok[:, :, 0:WIDE], v_ps.rearrange("p (h e) -> p h e", e=WIDE)).then_inc(v_ready, 1)
                for k, (ps, dst) in enumerate(((q_ps, phi_q), (k_ps, phi_k))):
                    act.wait_ge(arg_done, 2 * n + k + 2)
                    act.wait_ge(past_done, n + 1)
                    act.wait_ge(score_done, n * R + 1)
                    act.activation(flat(dst), ps, ACT.Exp).then_inc(phi_ready, 1)
                act.wait_ge(ot_done, n + 2)
                act.wait_ge(y_done, n + 1)
                act.copy(flat(oT), oT_ps).then_inc(ot_ready, 1)
                act.wait_ge(y_done, n + 2)
                act.activation(chip.yT[:, bass.ts(n, P)], y_ps, ACT.Identity, bias=bo[:, 0:1]).then_inc(y_read, 1)

            rows_of_chunks(act, lambda b: None, chunk)


def program(nc, dram, out, layers=None):
    with ExitStack() as ctx:
        chip = Chip(nc, dram, out, ctx)
        load_stage(chip)
        steps = [
            lambda norm: ffn_stage(chip, "ffn_a", norm), lambda norm: retention_attention(chip, norm),
            lambda norm: ffn_stage(chip, "ffn_b", norm),
            lambda norm: moe1(chip, "moe1_a", norm), lambda norm: window_attention(chip, norm),
            lambda norm: moe1(chip, "moe1_b", norm),
            lambda norm: moe2(chip, "moe2_a", norm), lambda norm: gated_attention(chip, norm),
            lambda norm: moe2(chip, "moe2_b", norm),
            lambda norm: choice(chip, "moe3_a", norm), lambda norm: feature_attention(chip, norm),
            lambda norm: choice(chip, "moe3_b", norm),
        ]
        scale = None
        for n, step in enumerate(steps):
            if layers is not None and n not in layers:
                continue
            step(lambda loads, n=n, scale=scale: norm_stage(chip, f"norm{n}", scale, loads))
            scale = 1.0 if n % 3 == 1 else 0.5
        store_stage(chip, scale)


def moe1(chip, name, norm):
    experts_stage(chip, name, norm, "sum", "moe1_router", 512, True, ("moe1_gate", "moe1_up"), "moe1_down")


def moe2(chip, name, norm):
    experts_stage(chip, name, norm, "softmax", "moe2_router", 256, True, ("moe2_gate", "moe2_up"), "moe2_down")


def choice(chip, name, norm):
    experts_stage(chip, name, norm, "choice", "moe3_router", 512, False, ("moe3_up",), "moe3_down")


def _arrays(i):
    import numpy as np

    f = np.float32

    def chunked(w):
        return np.swapaxes(w.reshape(*w.shape[:-2], -1, P, w.shape[-1]), -3, -2)

    def column(v):
        return v.reshape(-1, P).T

    head = np.arange(D) // DH0
    gamma = 1.0 - 2.0 ** (-5.0 - np.arange(H))
    pos = np.arange(P)
    ahead = pos[None, :] - pos[:, None]
    root = np.sqrt(DH0)
    decay = np.where(ahead >= 0, gamma[:, None, None] ** np.maximum(ahead, 0), 0.0) / root
    same_head = (head[:, None] == head[None, :]).astype(f)
    start = 2.0 ** -(2.0 ** -(np.log2(H) - 3))
    slopes = np.array([start * start ** h for h in range(H)])
    FAR = -1e30
    back = pos[:, None] - pos[None, :]
    slope = np.stack([np.where(back >= 0, -back * slopes[:, None, None], FAR),
                      np.where(back < 0, -(back + P) * slopes[:, None, None], FAR)])
    slope = slope.reshape(2, ROWS, SLOTS, P, P).transpose(3, 1, 0, 2, 4).reshape(P, -1)
    upto = (ahead >= 0).astype(f)
    two = np.kron(np.eye(2, dtype=f), np.ones((WIDE, WIDE), f))
    omega = np.zeros((P, P), f)
    for k in range(2):
        omega[k * WIDE:(k + 1) * WIDE, k * WIDE:(k + 1) * WIDE] = i["L3_attn_omega"].T
    places = [head_of(k) for k in range(H)]
    wo3 = i["L3_attn_wo"].T.reshape(H, WIDE, D)[places].reshape(HID, D)
    return {
        "fea_wq": i["L3_attn_wq"].T, "fea_wk": i["L3_attn_wk"].T, "fea_wv": i["L3_attn_wv"].T, "fea_wo": chunked(wo3),
        "fea_bo": column(i["L3_attn_bo"]), "fea_omega": omega, "fea_half_norm": f(-0.5) * two, "allowed": upto,
        "gla_wd": i["L2_attn_Wd"].T, "gla_bd": np.tile(i["L2_attn_bd"], (P, 1)),
        "gla_sums": np.stack([upto, 1 - upto, np.ones_like(upto)], 1),
        "gla_wk": i["L2_attn_Wk"].T, "gla_wg": i["L2_attn_Wg"].T, "gla_wv": i["L2_attn_Wv"].T, "gla_wog": i["L2_attn_Wog"].T,
        "gla_wq": i["L2_attn_Wq"].T, "gla_wo": chunked(i["L2_attn_Wo"].T), "gla_norm_w": column(i["L2_attn_norm_w"]),
        "causal": np.where(ahead >= 0, 0.0, FAR).astype(f),
        "win_slope": slope.astype(f),
        "win_wq": i["L1_attn_wq"].T, "win_wk": i["L1_attn_wk"].T, "win_wv": i["L1_attn_wv"].T, "win_wo": i["L1_attn_wo"].T,
        "win_bias_qk": np.stack([i["L1_attn_bq"], i["L1_attn_bk"]], 1), "win_bias_v": np.tile(i["L1_attn_bv"], (P, 1)),
        "win_bo": column(i["L1_attn_bo"]),
        "same_head": same_head, "head_mean": same_head / f(DH0),
        "slot": (head[:, None] % SLOTS == np.arange(SLOTS)).astype(f),
        "slot_cols": np.tile((head[None, :] % SLOTS == np.arange(SLOTS)[:, None]).astype(f), (P, 1, 1)),
        "ret_decay": decay.transpose(1, 0, 2).astype(f),
        "ret_q_decay": (gamma[head][:, None] ** (pos + 1) / root).astype(f),
        "ret_k_decay": (gamma[head][None, :] ** (P - 1 - pos[:, None])).astype(f),
        "ret_chunk_decay": (gamma[head][:, None] ** P).astype(f),
        "ret_wq": i["L0_attn_W_q"].T, "ret_wk": i["L0_attn_W_k"].T, "ret_wv": i["L0_attn_W_v"].T, "ret_wo": i["L0_attn_W_o"].T,
        "ret_affine": np.stack([i["L0_attn_gn_weight"], i["L0_attn_gn_bias"]], 1),
        "x": i["L0_attn_x"],
        "ident": np.eye(P, dtype=f),
        "descending": np.tile(np.arange(E, 0, -1).astype(f), (P, 1)),
        "place": np.tile(np.array([2.0 ** (3 * (ROUNDS - 1 - n)) for n in range(ROUNDS)], f), (P, 1)),
        "trials": np.array([[r << 3 * (ROUNDS - 1 - n) for n in range(ROUNDS)] for r in range(TRIAL_COUNT)
                            for _ in range(B * E)], np.int32),
        "same_row": np.array([[i // (B * E) > 0 and (i - j) % (B * E) == 0 for j in range(P)] for i in range(P)], f),
        "ffn_w1": i["L0_ffn_W1"], "ffn_b1": column(i["L0_ffn_b1"]), "ffn_w2": chunked(i["L0_ffn_W2"]), "ffn_b2": column(i["L0_ffn_b2"]),
        "moe1_router": i["L1_ffn_Wr"], "moe1_gate": i["L1_ffn_Wg"], "moe1_up": i["L1_ffn_Wu"], "moe1_down": chunked(i["L1_ffn_Wd"]),
        "moe2_router": i["L2_ffn_router_kernel_DE"], "moe2_gate": i["L2_ffn_kernel_gating_EDF"],
        "moe2_up": i["L2_ffn_kernel_up_EDF"], "moe2_down": chunked(i["L2_ffn_kernel_down_EFD"]),
        "moe3_router": i["L3_ffn_gate_w"].T, "moe3_up": i["L3_ffn_w1"], "moe3_down": chunked(i["L3_ffn_w2"]),
    }


def kernel(**inputs):
    import numpy as np
    import concourse.bacc as bacc
    from concourse.bass_utils import run_bass_kernel_spmd

    nc = bacc.Bacc("TRN2", target_bir_lowering=False, num_devices=1)
    arrays, dram = {}, {}
    for name, a in _arrays({k: np.asarray(v) for k, v in inputs.items()}).items():
        arrays["in_" + name] = np.ascontiguousarray(a)
        dram[name] = nc.dram_tensor("in_" + name, a.shape, mybir.dt.from_np(a.dtype), kind="ExternalInput").ap()
    out = nc.dram_tensor("out_x", (B, T, D), F32, kind="ExternalOutput").ap()
    program(nc, dram, out)
    r = run_bass_kernel_spmd(nc, [arrays], core_ids=[0])
    return r.results[0]["out_x"]
```

```python
from contextlib import ExitStack

import concourse.bass as bass
from concourse import mybir
from concourse.alu_op_type import AluOpType as ALU

ACT = mybir.ActivationFunctionType
F32 = mybir.dt.float32
I32 = mybir.dt.int32
F32R = mybir.dt.float32r
AX_X = mybir.AxisListType.X

P = 128
B, T, D = 2, 1024, 128
TOK = B * T
TILES = TOK // P
PER_B = T // P
GROUP = 512
GROUPS = TOK // GROUP
E = 8
H = 16
EPS = 1e-5
SEMAPHORES = 150
STAGE_SEMAPHORES = 62


class Chip:

    def __init__(self, nc, dram, out, ctx):
        self.nc, self.dram, self.out, self.ctx = nc, dram, out, ctx
        self.used_semaphores = []
        sb = self.sb
        self.x = sb("x_residual", [P, TILES, D])
        self.xnT = sb("xn_features", [P, TOK])
        self.yT = sb("y_features", [P, TOK])
        self.ident = sb("ident", [P, P])
        self.psum = ctx.enter_context(nc.psum_tensor("banks", [P, 8, GROUP], F32))
        self.weights_by_expert = nc.dram_tensor("weights_by_expert", (B * E, T), F32).ap()

    def sb(self, name, shape, dtype=F32):
        return self.ctx.enter_context(self.nc.sbuf_tensor(name, shape, dtype))


class Stage:

    def __init__(self, chip, name):
        self.chip, self.nc, self.name, self.ctx = chip, chip.nc, name, ExitStack()

    def __enter__(self):
        if len(self.chip.used_semaphores) > SEMAPHORES - STAGE_SEMAPHORES:
            self.nc.clear_and_free_semaphores(self.chip.used_semaphores)
            self.nc.all_engine_barrier()
            self.chip.used_semaphores = []
        return self

    def __exit__(self, *a):
        return self.ctx.__exit__(*a)

    def sb(self, name, shape, dtype=F32):
        return self.ctx.enter_context(self.nc.sbuf_tensor(f"{self.name}_{name}", shape, dtype))

    def sem(self, name, ahead=0):
        semaphore = self.nc.alloc_semaphore(f"{self.name}_{name}")
        self.chip.used_semaphores.append(semaphore)
        if ahead:
            self.nc.sync.sem_inc(semaphore, ahead)
        return semaphore

    def block(self):
        return self.ctx.enter_context(self.nc.Block())


class Chain:

    def __init__(self, engine, sem, start=0):
        self.engine, self.sem, self.n = engine, sem, start

    def done(self, instruction):
        instruction.then_inc(self.sem, 1)
        self.n = self.n + 1
        self.engine.wait_ge(self.sem, self.n)


def load_stage(chip):
    with Stage(chip, "load") as st:
        loaded = st.sem("loaded")
        block = st.block()

        @block.sync
        def _(sp):
            xs = chip.dram["x"].rearrange("b (t p) d -> p (b t) d", p=P)
            for q in range(4):
                tiles = slice(4 * q, 4 * q + 4)
                sp.dma_start(chip.x[:, tiles, :], xs[:, tiles, :]).then_inc(loaded, 16)
            sp.dma_start(chip.ident[:, :], chip.dram["ident"]).then_inc(loaded, 16)
            sp.wait_ge(loaded, 80)


def norm_stage(chip, name, scale, loads=()):
    Q = 4
    with Stage(chip, name) as st:
        xn = st.sb("xn", [P, TILES, D])
        stats = st.sb("stats", [P, TILES, 6])
        moments = st.sb("moments", [P, TILES, 2])
        rstd, var, shift = st.sb("rstd", [P, TILES]), st.sb("var", [P, TILES]), st.sb("shift", [P, TILES])
        preloaded = st.sem("preloaded")
        y_turned = st.sem("y_turned")
        x_added, stats_done, moments_done = st.sem("x_added"), st.sem("stats_done"), st.sem("moments_done")
        var_done, std_done, rstd_done = st.sem("var_done"), st.sem("std_done"), st.sem("rstd_done")
        affine_ready = st.sem("affine_ready")
        xn_ready = st.sem("xn_ready")
        xn_turned = st.sem("xn_turned")
        block = st.block()
        x, psum = chip.x, chip.psum

        @block.sync
        def _(sp):
            for buf, array in loads:
                sp.dma_start(buf, array).then_inc(preloaded, 16)
            if loads:
                sp.wait_ge(preloaded, 16 * len(loads))

        @block.tensor
        def _(pe):
            if scale is not None:
                for t in range(TILES):
                    turn = nc_t(pe, psum[:, t // 4, t % 4 * P:(t % 4 + 1) * P], chip.yT[:, t * P:(t + 1) * P], chip)
                    if t % 4 == 3:
                        turn.then_inc(y_turned, 1)
            for t in range(TILES):
                if t % 4 == 0:
                    pe.wait_ge(xn_ready, t // 4 + 1)
                turn = nc_t(pe, psum[:, 4 + t // 4, t % 4 * P:(t % 4 + 1) * P], xn[:, t, :], chip)
                if t % 4 == 3:
                    turn.then_inc(xn_turned, 1)

        @block.vector
        def _(dve):
            def moments_of(q):
                tiles = slice(4 * q, 4 * q + 4)
                if scale is not None:
                    dve.wait_ge(y_turned, q + 1)
                    flat = x[:, tiles, :].rearrange("p t d -> p (t d)")
                    dve.scalar_tensor_tensor(flat, psum[:, q, :], scale, flat, ALU.mult, ALU.add).then_inc(x_added, 1)
                    dve.wait_ge(x_added, q + 1)
                for t in range(4 * q, 4 * q + 4):
                    last = dve.bn_stats(stats[:, t, :], x[:, t, :])
                last.then_inc(stats_done, 1)
                dve.wait_ge(stats_done, q + 1)
                for t in range(4 * q, 4 * q + 4):
                    last = dve.bn_aggr(moments[:, t, :], stats[:, t, :])
                last.then_inc(moments_done, 1)
                dve.wait_ge(moments_done, q + 1)
                dve.tensor_scalar(var[:, tiles], moments[:, tiles, 1], EPS, None, ALU.add).then_inc(var_done, 1)

            def affine_of(q):
                tiles = slice(4 * q, 4 * q + 4)
                dve.wait_ge(std_done, q + 1)
                dve.reciprocal(rstd[:, tiles], var[:, tiles]).then_inc(rstd_done, 1)
                dve.wait_ge(rstd_done, q + 1)
                dve.scalar_tensor_tensor(shift[:, tiles], moments[:, tiles, 0], -1.0, rstd[:, tiles], ALU.mult,
                                         ALU.mult).then_inc(affine_ready, 1)

            moments_of(0)
            for q in range(1, Q):
                moments_of(q)
                affine_of(q - 1)
            affine_of(Q - 1)

        @block.scalar
        def _(act):
            def root(q):
                act.wait_ge(var_done, q + 1)
                act.activation(var[:, 4 * q:4 * q + 4], var[:, 4 * q:4 * q + 4], ACT.Sqrt).then_inc(std_done, 1)

            def normalise(q):
                act.wait_ge(affine_ready, q + 1)
                for t in range(4 * q, 4 * q + 4):
                    last = act.activation(xn[:, t, :], x[:, t, :], ACT.Identity, bias=shift[:, t:t + 1], scale=rstd[:, t:t + 1])
                last.then_inc(xn_ready, 1)

            def copy_turned(q):
                act.wait_ge(xn_turned, q + 1)
                act.copy(chip.xnT[:, q * GROUP:(q + 1) * GROUP], psum[:, 4 + q, :])

            root(0)
            for q in range(Q):
                if q < Q - 1:
                    root(q + 1)
                normalise(q)
                if q > 0:
                    copy_turned(q - 1)
            copy_turned(Q - 1)


def nc_t(pe, out, in_, chip):
    return pe.transpose(out, in_, chip.ident[0:in_.shape[0], 0:in_.shape[0]])


def store_stage(chip, scale):
    with Stage(chip, "store") as st:
        y_turned = st.sem("y_turned")
        x_added = st.sem("x_added")
        stored = st.sem("stored")
        block = st.block()

        @block.tensor
        def _(pe):
            for t in range(TILES):
                turn = nc_t(pe, chip.psum[:, t // 4, t % 4 * P:(t % 4 + 1) * P], chip.yT[:, t * P:(t + 1) * P], chip)
                if t % 4 == 3:
                    turn.then_inc(y_turned, 1)

        @block.vector
        def _(dve):
            for q in range(4):
                dve.wait_ge(y_turned, q + 1)
                tiles = chip.x[:, 4 * q:4 * q + 4, :].rearrange("p t d -> p (t d)")
                dve.scalar_tensor_tensor(tiles, chip.psum[:, q, :], scale, tiles, ALU.mult,
                                         ALU.add).then_inc(x_added, 1)

        @block.sync
        def _(sp):
            out = chip.out.rearrange("b (t p) d -> p (b t) d", p=P)
            for q in range(4):
                sp.wait_ge(x_added, q + 1)
                tiles = slice(4 * q, 4 * q + 4)
                sp.dma_start(out[:, tiles, :], chip.x[:, tiles, :]).then_inc(stored, 16)
            sp.wait_ge(stored, 64)


def ffn_stage(chip, name, norm):
    F = 512
    NC = F // P
    with Stage(chip, name) as st:
        w1 = st.sb("w1", [P, F])
        w2 = st.sb("w2", [P, NC, D])
        b1 = st.sb("b1", [P, NC])
        b2 = st.sb("b2", [P, 1])
        hidden = st.sb("hidden", [P, NC, GROUP])
        norm([(w1[:, :], chip.dram["ffn_w1"]), (w2[:, :, :], chip.dram["ffn_w2"]),
              (b1[:, :], chip.dram["ffn_b1"]), (b2[:, :], chip.dram["ffn_b2"])])
        up_done = st.sem("up_done")
        relu_done = st.sem("relu_done", ahead=NC)
        down_done = st.sem("down_done", ahead=1)
        y_copied = st.sem("y_copied", ahead=2)
        block = st.block()
        up, down = chip.psum[:, 0:NC, :], chip.psum[:, NC:NC + 2, :]

        @block.tensor
        def _(pe):
            with pe.Fori(0, GROUPS // 2) as pair:
                for q in range(2):
                    g = pair * 2 + q
                    for c in range(NC):
                        pe.wait_ge(relu_done, g * NC + c + 1)
                        pe.matmul(up[:, c, :], w1[:, c * P:(c + 1) * P], chip.xnT[:, bass.ts(g, GROUP)],
                                  start=True, stop=True).then_inc(up_done, 1)
                    pe.wait_ge(y_copied, g + 1)
                    for c in range(NC):
                        pe.wait_ge(relu_done, NC + g * NC + c + 1)
                        mm = pe.matmul(down[:, q, :], w2[:, c, :], hidden[:, c, :], start=(c == 0), stop=(c == NC - 1))
                    mm.then_inc(down_done, 1)

        @block.scalar
        def _(act):
            with act.Fori(0, GROUPS) as g:
                act.wait_ge(down_done, g + 1)
                for c in range(NC):
                    act.wait_ge(up_done, g * NC + c + 1)
                    act.activation(hidden[:, c, :], up[:, c, :], ACT.Relu, bias=b1[:, c:c + 1]).then_inc(relu_done, 1)

        @block.vector
        def _(dve):
            with dve.Fori(0, GROUPS // 2) as pair:
                for q in range(2):
                    g = pair * 2 + q
                    dve.wait_ge(down_done, g + 2)
                    dve.tensor_scalar(chip.yT[:, bass.ts(g, GROUP)], down[:, q, :], b2[:, 0:1], None,
                                      ALU.add).then_inc(y_copied, 1)


TRIAL_COUNT = 8
ROUNDS = 10


def router_programs(chip, st, mode, wr, descending, search):
    J = PER_B
    TRIALS = TRIAL_COUNT if mode == "choice" else 1
    prob = st.sb("prob", [P, TILES, E])
    pick = st.sb("pick", [P, TILES, E])
    rank = st.sb("rank", [P, TILES, E])
    first = st.sb("first", [P, TILES, E])
    comb = st.sb("comb", [P, J, TRIALS, B, E])
    best = st.sb("best", [P, TILES])
    best2 = st.sb("best2", [P, TILES])
    part = st.sb("part", [P, TILES])
    share = st.sb("share", [P, TILES])
    combT = st.sb("combT", [B * E, T])
    logits_done = st.sem("logits_done")
    shifted = st.sem("shifted")
    exp_done = st.sem("exp_done")
    own = st.sem("dve_steps")
    comb_ready = st.sem("comb_ready")
    comb_turned = st.sem("comb_turned")
    comb_copied = st.sem("comb_copied")
    stored = st.sem("stored")
    logits = chip.psum[:, 6, 0:TILES * E].rearrange("p (t e) -> p t e", e=E)
    turned = chip.psum[0:TRIALS * B * E, 6:8, :]
    reached = chip.psum[:, 3, 0:1]
    if mode == "choice":
        place, trials, same_row = search
        ones = st.sb("ones", [P, 1])
        low = st.sb("low", [P, 1], I32)
        trial = st.sb("trial", [P, 1], I32)
        keep = st.sb("keep", [P, 1], I32)
        count = st.sb("count", [P, 1])
        enough = st.sb("enough", [P, 1])
        all_rows = st.sb("all_rows", [P, T])
        above_all = st.sb("above_all", [P, T])
        above = above_all[0:B * E, :]
        equal = st.sb("equal", [B * E, T])
        order = st.sb("order", [B * E, T])
        room = st.sb("room", [B * E, 1])
        compared, summed, search_steps = st.sem("compared"), st.sem("summed"), st.sem("search_steps")

    def each(v):
        return v[:, :].unsqueeze(2).to_broadcast([P, TILES, E])

    def on_sync(sp):
        sp.wait_ge(comb_copied, 3 if mode == "choice" else 2)
        sp.dma_start(chip.weights_by_expert, combT[:, :]).then_inc(stored, 16)
        sp.wait_ge(stored, 16)

    def on_tensor_logits(pe):
        for t in range(TILES):
            mm = pe.matmul(logits[:, t, :], chip.xnT[:, t * P:(t + 1) * P], wr[:, :], start=True, stop=True)
        mm.then_inc(logits_done, 1)

    def on_tensor_turn(pe):
        pe.wait_ge(comb_ready, 1)
        for j in range(J):
            turn = nc_t(pe, turned[:, j // 4, j % 4 * P:(j % 4 + 1) * P],
                        comb[:, j, :, :, :].rearrange("p r b e -> p (r b e)"), chip)
            if j % 4 == 3:
                turn.then_inc(comb_turned, 1)

    def on_scalar(act):
        act.wait_ge(shifted, 1)
        act.activation(prob[:, :, :], prob[:, :, :], ACT.Exp).then_inc(exp_done, 1)
        if mode == "softmax":
            act.wait_ge(shifted, 2)
            act.activation(part[:, :], part[:, :], ACT.Exp).then_inc(exp_done, 1)

    CAP = T * 2 // E
    START_STEPS, ROUND_STEPS = 2, 4

    def start_search(dve):
        step = Chain(dve, search_steps)
        step.done(dve.memset(ones[:, :], 1.0))
        step.done(dve.memset(low[:, :], 0))

    def open_round(dve, i):
        step = Chain(dve, search_steps, START_STEPS + ROUND_STEPS * i)
        step.done(dve.tensor_tensor(trial[:, :], low[:, :], trials[:, i:i + 1], ALU.bitwise_or))
        step.done(dve.tensor_scalar(above_all[:, :], all_rows[:, :], trial[:, :].bitcast(F32), None, ALU.is_ge,
                                    ALU.add, accum_out=count[:, :]))
        dve.tensor_scalar(enough[:, :], count[:, :], float(CAP), None, ALU.is_ge).then_inc(compared, 1)

    def sum_round(pe, i):
        pe.wait_ge(compared, i + 1)
        pe.matmul(reached, same_row[:, :], enough[:, :], start=True, stop=True).then_inc(summed, 1)

    def close_round(dve, i):
        step = Chain(dve, search_steps, START_STEPS + ROUND_STEPS * i + 2)
        dve.wait_ge(summed, i + 1)
        step.done(dve.tensor_scalar(keep[:, :], reached, place[:, i:i + 1], None, ALU.mult))
        step.done(dve.tensor_tensor(low[:, :], low[:, :], keep[:, :], ALU.bitwise_or))

    def keep_best(dve, part):
        least, count_own, own_rows = low[0:B * E, :].bitcast(F32), count[0:B * E, :], all_rows[0:B * E, :]
        step = Chain(dve, search_steps, START_STEPS + ROUND_STEPS * ROUNDS + (0, 2, 5)[part])
        if part == 0:
            step.done(dve.tensor_scalar(above, own_rows, least, None, ALU.is_gt, ALU.add, accum_out=count_own))
            step.done(dve.tensor_scalar(equal[:, :], own_rows, least, None, ALU.is_equal))
        elif part == 1:
            step.done(dve.tensor_scalar(room[:, :], count_own, -1.0, float(CAP), ALU.mult, ALU.add))
            step.done(dve.tensor_tensor_scan(order[:, :], ones[0:B * E, :].to_broadcast([B * E, T]), equal[:, :], 0.0,
                                             ALU.mult, ALU.add))
            step.done(dve.scalar_tensor_tensor(equal[:, :], order[:, :], room[:, 0:1], equal[:, :], ALU.is_le, ALU.mult))
        else:
            step.done(dve.tensor_tensor(above, above, equal[:, :], ALU.add))
            dve.tensor_tensor(combT[:, :], own_rows, above, ALU.mult).then_inc(comb_copied, 1)

    def on_vector(dve):
        chain = Chain(dve, own)
        done = chain.done
        dve.wait_ge(logits_done, 1)
        done(dve.tensor_reduce(best[:, :], logits, AX_X, ALU.max))
        dve.tensor_tensor(prob[:, :, :], logits, each(best), ALU.subtract).then_inc(shifted, 1)
        dve.wait_ge(exp_done, 1)
        done(dve.tensor_reduce(best[:, :], prob[:, :, :], AX_X, ALU.add))
        done(dve.reciprocal(share[:, :], best[:, :]))
        if mode == "choice":
            done(dve.tensor_tensor(prob[:, :, :], prob[:, :, :], each(share), ALU.mult))
            for b in range(B):
                copy = dve.tensor_copy(comb[:, :, :, b, :], prob[:, b * J:(b + 1) * J, :].unsqueeze(2).to_broadcast(
                    [P, J, TRIAL_COUNT, E]))
            copy.then_inc(comb_ready, 1)
            for h in range(2):
                dve.wait_ge(comb_turned, h + 1)
                copy = dve.tensor_copy(all_rows[:, h * GROUP:(h + 1) * GROUP], turned[:, h, :])
                copy.then_inc(comb_copied, 1)
            dve.wait_ge(comb_copied, 2)
            return
        done(dve.tensor_tensor(prob[:, :, :], prob[:, :, :], each(share), ALU.mult))

        def take_best(value, selected):
            done(dve.tensor_reduce(value[:, :], prob[:, :, :], AX_X, ALU.max))
            done(dve.tensor_tensor(rank[:, :, :], prob[:, :, :], each(value), ALU.is_ge))
            done(dve.tensor_tensor(rank[:, :, :], rank[:, :, :],
                                   descending[:, :].unsqueeze(1).to_broadcast([P, TILES, E]), ALU.mult))
            done(dve.tensor_reduce(part[:, :], rank[:, :, :], AX_X, ALU.max))
            done(dve.tensor_tensor(selected[:, :, :], rank[:, :, :], each(part), ALU.is_ge))

        take_best(best, first)
        if mode == "sum":
            done(dve.tensor_copy(pick[:, :, :], prob[:, :, :]))
        done(dve.scalar_tensor_tensor(prob[:, :, :], first[:, :, :], -2.0, prob[:, :, :], ALU.mult, ALU.add))
        second = rank
        take_best(best2, second)
        by_row = comb[:, :, 0, :, :].rearrange("p j b e -> p b j e")
        if mode == "sum":
            done(dve.tensor_tensor(share[:, :], best[:, :], best2[:, :], ALU.add))
            done(dve.reciprocal(share[:, :], share[:, :]))
            done(dve.tensor_tensor(first[:, :, :], first[:, :, :], second[:, :, :], ALU.add))
            done(dve.tensor_tensor(pick[:, :, :], pick[:, :, :], each(share), ALU.mult))
            final, other, op = pick, first, ALU.mult
        else:
            dve.tensor_tensor(part[:, :], best2[:, :], best[:, :], ALU.subtract).then_inc(shifted, 1)
            dve.wait_ge(exp_done, 2)
            done(dve.tensor_scalar(share[:, :], part[:, :], 1.0, None, ALU.add))
            done(dve.reciprocal(share[:, :], share[:, :]))
            done(dve.tensor_tensor(part[:, :], part[:, :], share[:, :], ALU.mult))
            done(dve.tensor_tensor(first[:, :, :], first[:, :, :], each(share), ALU.mult))
            done(dve.tensor_tensor(second[:, :, :], second[:, :, :], each(part), ALU.mult))
            final, other, op = first, second, ALU.add
        for b in range(B):
            tiles = slice(b * J, (b + 1) * J)
            mul = dve.tensor_tensor(by_row[:, b], final[:, tiles, :], other[:, tiles, :], op)
        mul.then_inc(comb_ready, 1)
        for h in range(2):
            dve.wait_ge(comb_turned, h + 1)
            dve.tensor_copy(combT[:, h * GROUP:(h + 1) * GROUP], turned[:, h, :]).then_inc(comb_copied, 1)

    return (on_sync, on_tensor_logits, on_tensor_turn, on_scalar, on_vector), (
        start_search, open_round, sum_round, close_round, keep_best)


def experts_stage(chip, name, norm, mode, router_name, hidden_dim, gated, up_names, down_name):
    NC = hidden_dim // P
    NU = len(up_names)
    STEPS = E * GROUPS
    with Stage(chip, name) as st:
        raw_up = [st.sb(f"raw_up{u}", [P, hidden_dim]) for u in range(NU)]
        raw_down = st.sb("raw_down", [P, NC, D])
        w_up = [[[st.sb(f"w_up{p}{u}_{part}", [P, hidden_dim], F32R) for part in PARTS] for u in range(NU)] for p in range(2)]
        w_down = [[st.sb(f"w_down{p}_{part}", [P, NC, D], F32R) for part in PARTS] for p in range(2)]
        xn = [st.sb(f"xn_{part}", [P, TOK], F32R) for part in PARTS]
        weight = [st.sb(f"weight{p}", [P, TOK]) for p in range(2)]
        ones = st.sb("one", [P, 1])
        HB = 4
        full = st.sb("full", [P, 2, GROUP])
        hidden = [st.sb(f"hidden_{part}", [P, HB, GROUP], F32R) for part in PARTS]
        silu = st.sb("silu", [P, 2, GROUP])
        scaled = st.sb("scaled", [P, 2, GROUP])
        wr, descending = st.sb("wr", [P, E]), st.sb("descending", [P, E])
        loads = [(raw_up[u][:, :], chip.dram[up_names[u]][0]) for u in range(NU)]
        loads += [(raw_down[:, :, :], chip.dram[down_name][0]), (wr[:, :], chip.dram[router_name]),
                  (descending[:, :], chip.dram["descending"])]
        search = None
        if mode == "choice":
            place = st.sb("place", [P, ROUNDS])
            trials = st.sb("trials", [P, ROUNDS], I32)
            same_row = st.sb("same_row", [P, P])
            search = place, trials, same_row
            loads += [(buf[:, :], chip.dram[nm]) for buf, nm in zip(search, ("place", "trials", "same_row"))]
        norm(loads)
        (route_sync, route_logits, route_turn, route_scalar, route_vector), (
            start_search, open_round, sum_round, close_round, keep_best) = router_programs(
            chip, st, mode, wr, descending, search)
        early = mode == "choice"
        STASHED = 2 * GROUPS
        if early:
            stash = st.sb("stash", [P, STASHED, GROUP])
            stash_ready = st.sem("stash_ready")
        LOADS = 16 * (NU + 1)
        loaded = st.sem("loaded", ahead=LOADS)
        weight_loaded = [st.sem(f"weight_loaded{p}") for p in range(2)]
        x_high, x_split = st.sem("x_high"), st.sem("x_split")
        ones_done = st.sem("one_done")
        w_high, w_split = st.sem("w_high"), st.sem("w_split", ahead=1)
        up_done = st.sem("up_done")
        silu_done = st.sem("silu_done")
        full_done = st.sem("full_done", ahead=2)
        high_done = st.sem("high_done")
        hidden_done = st.sem("hidden_done", ahead=2)
        down_done = st.sem("down_done", ahead=HB)
        scaled_done = st.sem("scaled_done", ahead=2)
        added = st.sem("added")
        block = st.block()
        up = chip.psum[:, 0:4, :]
        down = chip.psum[:, 4:6, :]

        def later(pair, p, g, c, chunks):
            c += chunks
            if c < NC:
                return pair, p, g, c
            return (pair, p, g + 1, c - NC) if g < GROUPS - 1 else (pair + p, 1 - p, 0, c - NC)

        def early_chunks(ahead):
            for k in range(2 * GROUPS * NC + ahead):
                e, g, c = k // (GROUPS * NC), k // NC % GROUPS, k % NC
                yield k, (e // 2, e % 2, g, c)

        def all_experts(eng, expert):
            with eng.Fori(1 if early else 0, E // 2 - 1) as pair:
                expert(pair, 0, False)
                expert(pair, 1, False)
            expert(E // 2 - 1, 0, False)
            expert(E // 2 - 1, 1, True)

        @block.sync
        def _(sp):
            def load_matrices(e):
                sp.wait_ge(w_split, e + 1)
                for u in range(NU):
                    sp.dma_start(raw_up[u][:, :], chip.dram[up_names[u]][bass.ds(e, 1)].rearrange(
                        "e p f -> (e p) f")).then_inc(loaded, 16)
                sp.dma_start(raw_down[:, :, :], chip.dram[down_name][bass.ds(e, 1)].rearrange(
                    "e p c d -> (e p) c d")).then_inc(loaded, 16)

            def load_weight(e, p, turn):
                if turn is not None:
                    sp.wait_ge(scaled_done, 2 + (turn * 2 + p - 1) * GROUPS)
                rows = chip.weights_by_expert.rearrange("(b e) t -> e b t", b=B)[bass.ds(e, 1)]
                rows = rows.rearrange("e b t -> (e b) t").unsqueeze(0).to_broadcast([P, B, T])
                sp.dma_start(weight[p][:, :].rearrange("p (b t) -> p b t", b=B), rows).then_inc(weight_loaded[p], 16)

            load_matrices(1)
            route_sync(sp)
            load_weight(0, 0, None)
            load_weight(1, 1, None)
            load_matrices(2)
            if early:
                sp.wait_ge(stash_ready, STASHED)
            with sp.Fori(1, E // 2 - 1) as pair:
                for p in range(2):
                    load_weight(pair * 2 + p, p, pair)
                    load_matrices(pair * 2 + p + 1)
            load_weight(E - 2, 0, E // 2 - 1)
            load_matrices(E - 1)
            load_weight(E - 1, 1, E // 2 - 1)

        @block.tensor
        def _(pe):
            def ups(pair, p, g, c):
                step = (pair * 2 + p) * GROUPS + g
                if c == 0 and g == 0:
                    pe.wait_ge(w_split, pair * 2 + p + 2)
                pe.wait_ge(full_done, step * NC + c + 1)
                for u in range(NU):
                    mm = split_product(pe, up[:, c % 2 * 2 + u, :], [w[:, c * P:(c + 1) * P] for w in w_up[p][u]],
                                       [x[:, g * GROUP:(g + 1) * GROUP] for x in xn])
                mm.then_inc(up_done, 1)

            def down_product(pair, p, g, c):
                step = (pair * 2 + p) * GROUPS + g
                if c == 0:
                    pe.wait_ge(scaled_done, step + 1)
                pe.wait_ge(hidden_done, step * NC + c + 3)
                mm = split_product(pe, down[:, g % 2, :], [w[:, c, :] for w in w_down[p]],
                                   [h[:, (g * NC + c) % HB, :] for h in hidden], first=(c == 0), last=(c == NC - 1))
                mm.then_inc(down_done, 1)

            def expert(pair, p, last):
                for g in range(GROUPS):
                    for c in range(NC):
                        if not (last and g == GROUPS - 1 and c >= NC - 2):
                            ups(*later(pair, p, g, c, 2))
                        down_product(pair, p, g, c)

            route_logits(pe)
            pe.wait_ge(x_split, GROUPS)
            ups(0, 0, 0, 0)
            ups(0, 0, 0, 1)
            route_turn(pe)
            if early:
                for k, at in early_chunks(0):
                    ups(*later(*at, 2))
                    down_product(*at)
                    if k % 2 == 0 and k // 2 < ROUNDS:
                        sum_round(pe, k // 2)
            all_experts(pe, expert)

        @block.scalar
        def _(act):
            func = ACT.Silu if gated else ACT.Gelu
            for g in range(GROUPS):
                cols = slice(g * GROUP, (g + 1) * GROUP)
                act.copy(xn[0][:, cols], chip.xnT[:, cols]).then_inc(x_high, 1)
            route_scalar(act)

            def activate(k, c):
                act.wait_ge(up_done, k + 1)
                if gated:
                    act.wait_ge(full_done, k + 1)
                    act.activation(silu[:, c % 2, :], up[:, c % 2 * 2, :], func).then_inc(silu_done, 1)
                else:
                    act.wait_ge(hidden_done, k + 1)
                    act.activation(full[:, c % 2, :], up[:, c % 2 * 2, :], func).then_inc(full_done, 1)
                    act.wait_ge(full_done, k + 3)
                    act.wait_ge(down_done, k + 1)
                    act.copy(hidden[0][:, c % HB, :], full[:, c % 2, :]).then_inc(high_done, 1)

            def put_by(step):
                act.wait_ge(down_done, HB + (step + 1) * NC)
                act.copy(stash[:, step, :], down[:, step % 2, :]).then_inc(scaled_done, 1)

            if early:
                for k, (_, _, _, c) in early_chunks(0):
                    activate(k, c)
                    if c == 1 and k > NC:
                        put_by(k // NC - 1)
                put_by(STASHED - 1)
            with act.Fori(2 if early else 0, E) as e:
                for j in range(GROUPS * NC):
                    activate(e * (GROUPS * NC) + j, j % NC)

        @block.vector
        def _(dve):
            for g in range(GROUPS):
                cols = slice(g * GROUP, (g + 1) * GROUP)
                dve.wait_ge(x_high, g + 1)
                dve.tensor_tensor(xn[1][:, cols], chip.xnT[:, cols], xn[0][:, cols].bitcast(F32),
                                  ALU.subtract).then_inc(x_split, 1)
            route_vector(dve)

            def make_hidden(pair, p, g, c):
                k = ((pair * 2 + p) * GROUPS + g) * NC + c
                if gated:
                    dve.wait_ge(silu_done, k + 1)
                    dve.wait_ge(hidden_done, k + 1)
                    dve.tensor_tensor(full[:, c % 2, :], silu[:, c % 2, :], up[:, c % 2 * 2 + 1, :],
                                      ALU.mult).then_inc(full_done, 1)
                    dve.wait_ge(full_done, k + 3)
                dve.wait_ge(down_done, k + 1)
                high, low = (h[:, (g * NC + c) % HB, :] for h in hidden)
                if gated:
                    dve.tensor_copy(high, full[:, c % 2, :]).then_inc(high_done, 1)
                dve.wait_ge(high_done, k + 1)
                dve.tensor_tensor(low, full[:, c % 2, :], high.bitcast(F32), ALU.subtract).then_inc(hidden_done, 1)

            def expert(pair, p, last):
                for g in range(GROUPS):
                    step = (pair * 2 + p) * GROUPS + g
                    for c in range(NC):
                        if not (last and g == GROUPS - 1 and c >= NC - 2):
                            make_hidden(*later(pair, p, g, c, 2))
                    if g == 0:
                        dve.wait_ge(weight_loaded[p], (pair + 1) * 16)
                    dve.wait_ge(down_done, HB + (step + 1) * NC)
                    dve.wait_ge(added, step + 1)
                    dve.tensor_tensor(scaled[:, g % 2, :], down[:, g % 2, :], weight[p][:, g * GROUP:(g + 1) * GROUP],
                                      ALU.mult).then_inc(scaled_done, 1)

            def weigh(step):
                if step % GROUPS == 0:
                    dve.wait_ge(weight_loaded[step // GROUPS], 16)
                dve.wait_ge(scaled_done, step + 3)
                dve.tensor_tensor(stash[:, step, :], stash[:, step, :],
                                  weight[step // GROUPS][:, step % GROUPS * GROUP:(step % GROUPS + 1) * GROUP],
                                  ALU.mult).then_inc(stash_ready, 1)

            if early:
                ALL_FOUND = 2 * ROUNDS
                WEIGHTS_IN = 2 * GROUPS * NC + 2 - STASHED
                start_search(dve)
                open_round(dve, 0)
                for k, at in early_chunks(2):
                    make_hidden(*at)
                    if k % 2 == 1 and k < ALL_FOUND:
                        close_round(dve, k // 2)
                        if k // 2 < ROUNDS - 1:
                            open_round(dve, k // 2 + 1)
                    if ALL_FOUND <= k < ALL_FOUND + 3:
                        keep_best(dve, k - ALL_FOUND)
                    if k >= WEIGHTS_IN:
                        weigh(k - WEIGHTS_IN)
            else:
                make_hidden(0, 0, 0, 0)
                make_hidden(0, 0, 0, 1)
            all_experts(dve, expert)

        @block.gpsimd
        def _(pool):
            def split_weights(e, p):
                pool.wait_ge(loaded, (e + 1) * LOADS)
                pairs = [(raw_up[u][:, :], [w[:, :] for w in w_up[p][u]]) for u in range(NU)]
                pairs.append((raw_down[:, :, :], [w[:, :, :] for w in w_down[p]]))
                for raw, (high, _) in pairs:
                    one = ones[:, :] if len(raw.shape) == 2 else ones[:, :].unsqueeze(2)
                    last = pool.tensor_tensor(high, raw, one.to_broadcast(list(raw.shape)), ALU.mult)
                last.then_inc(w_high, 1)
                pool.wait_ge(w_high, e + 1)
                for raw, (high, low) in pairs:
                    last = pool.tensor_tensor(low, raw, high.bitcast(F32), ALU.subtract)
                last.then_inc(w_split, 1)

            def add(step, g):
                y = chip.yT[:, g * GROUP:(g + 1) * GROUP]
                pool.wait_ge(scaled_done, step + 3)
                pool.tensor_tensor(y, y, scaled[:, g % 2, :], ALU.add).then_inc(added, 1)

            pool.memset(ones[:, :], 1.0).then_inc(ones_done, 1)
            pool.wait_ge(ones_done, 1)
            split_weights(0, 0)
            pool.memset(chip.yT[:, :], 0.0).then_inc(added, 2)
            pool.wait_ge(added, 2)
            split_weights(1, 1)
            if early:
                for e in range(2):
                    pool.wait_ge(down_done, HB + (e + 1) * GROUPS * NC)
                    split_weights(e + 2, e)
                    for g in range(GROUPS):
                        step = e * GROUPS + g
                        y = chip.yT[:, g * GROUP:(g + 1) * GROUP]
                        pool.wait_ge(stash_ready, step + 1)
                        pool.wait_ge(added, step + 2)
                        pool.tensor_tensor(y, y, stash[:, step, :], ALU.add).then_inc(added, 1)
            with pool.Fori(1 if early else 0, E // 2 - 1) as pair:
                for p in range(2):
                    e = pair * 2 + p
                    for g in range(GROUPS):
                        add(e * GROUPS + g, g)
                    split_weights(e + 2, p)
            with pool.Fori(E - 2, E) as e:
                for g in range(GROUPS):
                    add(e * GROUPS + g, g)


PARTS = ("high", "low")


def split_stage(chip, name, pairs):
    with Stage(chip, name) as st:
        rounded = st.sem("rounded")
        block = st.block()

        @block.scalar
        def _(act):
            for raw, (high, _) in pairs:
                act.copy(high, raw).then_inc(rounded, 1)

        @block.vector
        def _(dve):
            for k, (raw, (high, low)) in enumerate(pairs):
                dve.wait_ge(rounded, k + 1)
                dve.tensor_tensor(low, raw, high.bitcast(F32), ALU.subtract)


def split_product(pe, out, weights, moving, first=True, last=True):
    (w_high, w_low), (x_high, x_low) = weights, moving
    pe.matmul(out, w_high, x_high, start=first, stop=False)
    pe.matmul(out, w_high, x_low, start=False, stop=False)
    return pe.matmul(out, w_low, x_high, start=False, stop=last)


def project_stage(chip, name, w, features, tokens, bias=None, bias_row=None):
    nf = len(features)
    with Stage(chip, name) as st:
        products = st.sem("products")
        read = st.sem("banks_read", ahead=8)
        block = st.block()
        nt = len(tokens)

        jobs = [("features", n, g) for g in range(GROUPS) for n in range(nf)] + [("tokens", 0, q) for q in range(TILES // 2)]

        @block.tensor
        def _(pe):
            for k, (kind, n, q) in enumerate(jobs):
                pe.wait_ge(read, k + 1)
                if kind == "features":
                    mm = pe.matmul(chip.psum[:, k % 8, :], w[:, n, :], chip.xnT[:, q * GROUP:(q + 1) * GROUP],
                                   start=True, stop=True)
                else:
                    for half in range(2):
                        t = 2 * q + half
                        mm = pe.matmul(chip.psum[:, k % 8, half * nt * P:(half + 1) * nt * P], chip.xnT[:, t * P:(t + 1) * P],
                                       w[:, nf:, :].rearrange("p a d -> p (a d)"), start=True, stop=True)
                mm.then_inc(products, 1)

        def copy(eng, k, kind, n, q):
            bank = chip.psum[:, k % 8, :]
            eng.wait_ge(products, k + 1)
            if kind == "features":
                dst = features[n][:, q * GROUP:(q + 1) * GROUP]
                if bias is not None:
                    return eng.tensor_scalar(dst, bank, bias[:, n:n + 1], None, ALU.add)
                return eng.tensor_copy(dst, bank)
            view = bank[:, 0:2 * nt * P].rearrange("p (t a d) -> p t a d", t=2, a=nt)
            for a in range(nt):
                dst = tokens[a][:, 2 * q:2 * q + 2, :]
                if bias is not None:
                    last = eng.tensor_tensor(dst, view[:, :, a], bias_row[:, a, :].unsqueeze(1).to_broadcast([P, 2, P]),
                                             ALU.add)
                else:
                    last = eng.tensor_copy(dst, view[:, :, a])
            return last

        @block.vector
        def _(dve):
            for k, job in enumerate(jobs):
                copy(dve, k, *job).then_inc(read, 1)


def output_stage(chip, name, features, w, bias):
    with Stage(chip, name) as st:
        out_done = st.sem("out_done")
        block = st.block()

        @block.tensor
        def _(pe):
            for g in range(GROUPS):
                pe.matmul(chip.psum[:, g, :], w[:, :], features[:, g * GROUP:(g + 1) * GROUP],
                          start=True, stop=True).then_inc(out_done, 1)

        @block.vector
        def _(dve):
            for g in range(GROUPS):
                dve.wait_ge(out_done, g + 1)
                dve.tensor_scalar(chip.yT[:, g * GROUP:(g + 1) * GROUP], chip.psum[:, g, :], bias[:, 0:1], None, ALU.add)


DH0 = D // H
SLOTS = 32 // DH0
ROWS = H // SLOTS


def retention_attention(chip, norm):
    with Stage(chip, "retention") as outer:
        qT, kT = outer.sb("qT", [P, TOK]), outer.sb("kT", [P, TOK])
        k_tok, v_tok = outer.sb("k_tok", [P, TILES, P]), outer.sb("v_tok", [P, TILES, P])
        retained = outer.sb("retained", [P, TOK])
        w = outer.sb("w", [P, 4, P])
        wo = outer.sb("wo", [P, P])
        affine = outer.sb("affine", [P, 2])
        head_mean = outer.sb("head_mean", [P, P])
        consts = RetentionConstants(outer)
        norm([(w[:, n, :], chip.dram[nm]) for n, nm in enumerate(("ret_wq", "ret_wk", "ret_wk", "ret_wv"))]
             + [(wo[:, :], chip.dram["ret_wo"]), (affine[:, :], chip.dram["ret_affine"]),
                (head_mean[:, :], chip.dram["head_mean"])] + consts.loads(chip))
        project_stage(chip, "retention_in", w, (qT, kT), (k_tok, v_tok))
        retention_chunks(chip, consts, qT, kT, k_tok, v_tok, retained)
        group_norm_stage(chip, retained, wo, affine, head_mean)


class RetentionConstants:

    def __init__(self, st):
        self.decay = st.sb("decay", [P, H, P])
        self.q_decay = st.sb("q_decay", [P, P])
        self.k_decay = st.sb("k_decay", [P, P])
        self.chunk_decay = st.sb("chunk_decay", [P, 1])
        self.same_head = st.sb("same_head", [P, P])
        self.slot = st.sb("slot", [P, SLOTS])
        self.slot_cols = st.sb("slot_cols", [P, SLOTS, P])

    def loads(self, chip):
        dram = chip.dram
        return [(self.decay[:, :, :], dram["ret_decay"]), (self.q_decay[:, :], dram["ret_q_decay"]),
                (self.k_decay[:, :], dram["ret_k_decay"]), (self.chunk_decay[:, :], dram["ret_chunk_decay"]),
                (self.same_head[:, :], dram["same_head"]), (self.slot[:, :], dram["slot"]),
                (self.slot_cols[:, :, :], dram["slot_cols"])]


def retention_chunks(chip, consts, qT, kT, k_tok, v_tok, retained):
    with Stage(chip, "retention_chunks") as st:
        decay, q_decay, k_decay, chunk_decay = consts.decay, consts.q_decay, consts.k_decay, consts.chunk_decay
        same_head, slot, slot_cols = consts.same_head, consts.slot, consts.slot_cols
        vals = [st.sb(f"vals{p}", [P, SLOTS, P]) for p in range(2)]
        kc = [st.sb(f"kc{p}", [P, P]) for p in range(2)]
        qm = [st.sb(f"qm{p}", [P, SLOTS, P]) for p in range(2)]
        qd = [st.sb(f"qd{p}", [P, P]) for p in range(2)]
        kd = [st.sb(f"kd{p}", [P, P]) for p in range(2)]
        probs = st.sb("probs", [P, H, P])
        state = st.sb("state", [P, P])
        fresh = st.sb("fresh", [P, P])
        prepared = st.sem("prepared")
        scores_done = st.sem("scores_done")
        probs_done = st.sem("probs_done")
        update_done = st.sem("update_done")
        inter_done = st.sem("inter_done", ahead=1)
        fresh_done = st.sem("fresh_done", ahead=1)
        state_done = st.sem("state_done", ahead=1)
        y_done = st.sem("y_done")
        y_copied = st.sem("y_copied", ahead=2)
        block = st.block()
        scores, y, update = chip.psum[:, 0:4, :], chip.psum[:, 4:6, 0:P], chip.psum[:, 6, 0:P]

        @block.gpsimd
        def _(pool):
            with pool.Fori(0, TILES // 2) as pair:
                for p in range(2):
                    n = pair * 2 + p
                    pool.wait_ge(y_copied, n + 1)
                    cols = bass.ts(n, P)
                    pool.tensor_copy(kc[p][:, :], kT[:, cols])
                    pool.tensor_tensor(qm[p][:, :, :], qT[:, cols].unsqueeze(1).to_broadcast([P, SLOTS, P]),
                                       slot[:, :].unsqueeze(2).to_broadcast([P, SLOTS, P]), ALU.mult)
                    pool.tensor_tensor(vals[p][:, :, :], v_tok[:, bass.ds(n, 1), :].to_broadcast([P, SLOTS, P]),
                                       slot_cols[:, :, :], ALU.mult)
                    pool.tensor_tensor(qd[p][:, :], qT[:, cols], q_decay[:, :], ALU.mult)
                    pool.tensor_tensor(kd[p][:, :], k_tok[:, bass.ds(n, 1), :].rearrange("p a d -> p (a d)"), k_decay[:, :],
                                       ALU.mult).then_inc(prepared, 1)

        @block.tensor
        def _(pe):
            def score(n, p, r):
                if r == 0:
                    pe.wait_ge(prepared, n + 1)
                rows = slice(32 * r, 32 * r + 32)
                pe.matmul(scores[:, r, :], kc[p][rows, :], qm[p][rows, :, :].rearrange("p s i -> p (s i)"),
                          start=True, stop=True).then_inc(scores_done, 1)

            def chunk(b, n, p, last):
                v = v_tok[:, bass.ds(n, 1), :].rearrange("p a d -> p (a d)")
                pe.wait_ge(fresh_done, n + 1)
                pe.matmul(update, kd[p][:, :], v, start=True, stop=True).then_inc(update_done, 1)
                pe.wait_ge(state_done, n + b + 2)
                pe.wait_ge(y_copied, n + 1)
                pe.matmul(y[:, p, :], state[:, :], qd[p][:, :], start=True, stop=False,
                          skip_group_check=True).then_inc(inter_done, 1)
                for r in range(ROWS):
                    pe.wait_ge(probs_done, n * ROWS + r + 1)
                    rows = slice(32 * r, 32 * r + 32)
                    for s in range(SLOTS):
                        h = r * SLOTS + s
                        mm = pe.matmul(y[rows, p, :], vals[p][:, s, rows], probs[:, h, :],
                                       start=False, stop=(h == H - 1), skip_group_check=True)
                    if r == ROWS - 1:
                        mm.then_inc(y_done, 1)
                    if not last:
                        score(n + 1, 1 - p, r)

            with pe.Fori(0, B) as b:
                for r in range(ROWS):
                    score(b * PER_B, 0, r)
                with pe.Fori(0, PER_B // 2 - 1) as pair:
                    for p in range(2):
                        chunk(b, b * PER_B + pair * 2 + p, p, False)
                for p in range(2):
                    chunk(b, b * PER_B + PER_B - 2 + p, p, p == 1)

        @block.vector
        def _(dve):
            with dve.Fori(0, B) as b:
                dve.wait_ge(inter_done, b * PER_B + 1)
                dve.wait_ge(state_done, b * (PER_B + 1) + 1)
                dve.memset(state[:, :], 0.0).then_inc(state_done, 1)
                with dve.Fori(0, PER_B) as c:
                    n = b * PER_B + c
                    for r in range(ROWS):
                        dve.wait_ge(scores_done, n * ROWS + r + 1)
                        heads = slice(r * SLOTS, (r + 1) * SLOTS)
                        dve.tensor_tensor(probs[:, heads, :].rearrange("p s i -> p (s i)"), scores[:, r, :],
                                          decay[:, heads, :].rearrange("p s i -> p (s i)"), ALU.mult).then_inc(probs_done, 1)
                    dve.wait_ge(update_done, n + 1)
                    dve.wait_ge(state_done, n + b + 2)
                    dve.tensor_tensor(fresh[:, :], update, same_head[:, :], ALU.mult).then_inc(fresh_done, 1)
                    dve.wait_ge(fresh_done, n + 2)
                    dve.wait_ge(inter_done, n + 2)
                    dve.scalar_tensor_tensor(state[:, :], state[:, :], chunk_decay[:, 0:1], fresh[:, :], ALU.mult,
                                             ALU.add).then_inc(state_done, 1)

        @block.scalar
        def _(act):
            with act.Fori(0, TILES // 2) as pair:
                for p in range(2):
                    n = pair * 2 + p
                    act.wait_ge(y_done, n + 1)
                    act.copy(retained[:, bass.ts(n, P)], y[:, p, :]).then_inc(y_copied, 1)


def group_norm_stage(chip, retained, w, affine, head_mean):
    with Stage(chip, "group_norm") as st:
        y = st.sb("y", [P, TOK])
        stats = st.sb("stats", [P, GROUPS, 6])
        moments = st.sb("moments", [P, B, 2])
        mean_of = st.sb("mean_of", [P, B])
        off = st.sb("off", [P, B])
        var_of = st.sb("var_of", [P, B])
        scale, shift = st.sb("scale", [P, B]), st.sb("shift", [P, B])
        own = st.sem("dve_steps")
        asked = st.sem("asked")
        averaged = st.sem("averaged")
        var_done, std_done = st.sem("var_done"), st.sem("std_done")
        normed, out_done = st.sem("normed"), st.sem("out_done")
        block = st.block()
        psum = chip.psum

        @block.tensor
        def _(pe):
            for k, v in enumerate((moments[:, :, 0], off[:, :])):
                pe.wait_ge(asked, k + 1)
                pe.matmul(psum[:, 4, k * B:(k + 1) * B], head_mean[:, :], v, start=True, stop=True).then_inc(averaged, 1)
            for g in range(GROUPS):
                pe.wait_ge(normed, g + 1)
                pe.matmul(psum[:, g, :], w[:, :], y[:, g * GROUP:(g + 1) * GROUP], start=True,
                          stop=True).then_inc(out_done, 1)

        @block.vector
        def _(dve):
            done = Chain(dve, own).done
            for g in range(GROUPS):
                last = dve.bn_stats(stats[:, g, :], retained[:, g * GROUP:(g + 1) * GROUP])
            done(last)
            for b in range(B):
                last = dve.bn_aggr(moments[:, b, :], stats[:, 2 * b:2 * b + 2, :].rearrange("p a s -> p (a s)"))
            last.then_inc(asked, 1)
            dve.wait_ge(averaged, 1)
            done(dve.tensor_copy(mean_of[:, :], psum[:, 4, 0:B]))
            done(dve.tensor_tensor(off[:, :], moments[:, :, 0], mean_of[:, :], ALU.subtract))
            done(dve.tensor_tensor(off[:, :], off[:, :], off[:, :], ALU.mult))
            dve.tensor_tensor(off[:, :], off[:, :], moments[:, :, 1], ALU.add).then_inc(asked, 1)
            dve.wait_ge(averaged, 2)
            dve.tensor_scalar(var_of[:, :], psum[:, 4, B:2 * B], EPS, None, ALU.add).then_inc(var_done, 1)
            dve.wait_ge(std_done, 1)
            done(dve.reciprocal(scale[:, :], var_of[:, :]))
            done(dve.tensor_scalar(scale[:, :], scale[:, :], affine[:, 0:1], None, ALU.mult))
            done(dve.tensor_tensor(shift[:, :], mean_of[:, :], scale[:, :], ALU.mult))
            done(dve.tensor_scalar(shift[:, :], shift[:, :], -1.0, affine[:, 1:2], ALU.mult, ALU.add))
            for g in range(GROUPS):
                b = g // (GROUPS // B)
                dve.tensor_scalar(y[:, g * GROUP:(g + 1) * GROUP], retained[:, g * GROUP:(g + 1) * GROUP], scale[:, b:b + 1], shift[:, b:b + 1],
                                  ALU.mult, ALU.add).then_inc(normed, 1)
            for g in range(GROUPS):
                dve.wait_ge(out_done, g + 1)
                dve.tensor_copy(chip.yT[:, g * GROUP:(g + 1) * GROUP], psum[:, g, :])

        @block.scalar
        def _(act):
            act.wait_ge(var_done, 1)
            act.activation(var_of[:, :], var_of[:, :], ACT.Sqrt).then_inc(std_done, 1)


def window_attention(chip, norm):
    with Stage(chip, "window") as outer:
        qT, kT = outer.sb("qT", [P, TOK]), outer.sb("kT", [P, TOK])
        v_tok = outer.sb("v_tok", [P, TILES, P])
        attended = outer.sb("attended", [P, TOK])
        w, wo = outer.sb("w", [P, 3, P]), outer.sb("wo", [P, P])
        bias, bias_row, bo = outer.sb("bias", [P, 2]), outer.sb("bias_row", [P, 1, P]), outer.sb("bo", [P, 1])
        slope = outer.sb("slope", [P, ROWS, 2, SLOTS, P])
        slot = outer.sb("slot", [P, SLOTS])
        slot_cols = outer.sb("slot_cols", [P, SLOTS, P])
        norm([(w[:, n, :], chip.dram[nm]) for n, nm in enumerate(("win_wq", "win_wk", "win_wv"))]
             + [(bias[:, :], chip.dram["win_bias_qk"]), (bias_row[:, 0, :], chip.dram["win_bias_v"]),
                (wo[:, :], chip.dram["win_wo"]), (bo[:, :], chip.dram["win_bo"]), (slot[:, :], chip.dram["slot"]),
                (slot_cols[:, :, :], chip.dram["slot_cols"]),
                (slope[:, :, :, :, :].rearrange("p r a s j -> p (r a s j)"), chip.dram["win_slope"])])
        project_stage(chip, "window_in", w, (qT, kT), (v_tok,), bias, bias_row)
        window_chunks(chip, qT, kT, v_tok, attended, slope, slot, slot_cols)
        output_stage(chip, "window_out", attended, wo, bo)


def window_chunks(chip, qT, kT, v_tok, attended, slope, slot, slot_cols):
    with Stage(chip, "window_chunks") as st:
        keys = [st.sb(f"keys{p}", [P, 2, SLOTS, P]) for p in range(2)]
        qc = [st.sb(f"qc{p}", [P, P]) for p in range(2)]
        vals = [st.sb(f"vals{p}", [P, 2, SLOTS, P]) for p in range(2)]
        biased = [st.sb(f"biased{p}", [P, 2, SLOTS, P]) for p in range(2)]
        expd = [st.sb(f"expd{p}", [P, 2, SLOTS, P]) for p in range(2)]
        probsT = [st.sb(f"probsT{p}", [P, 2, SLOTS, P]) for p in range(2)]
        low = st.sb("low", [P, 2, SLOTS])
        sums = st.sb("sums", [P, 2, H])
        inverse = st.sb("inverse", [P, H])
        spread_inv = [st.sb(f"spread_inv{p}", [P, H, DH0]) for p in range(2)]
        inverseT = st.sb("inverseT", [P, 2, P])
        prepared, prepared_v = st.sem("prepared"), st.sem("prepared_v")
        scores_done = st.sem("scores_done", ahead=2 * ROWS)
        biased_done = st.sem("biased_done", ahead=2)
        max_done = st.sem("max_done")
        exp_done = st.sem("exp_done", ahead=2 * SLOTS)
        turned = st.sem("turned", ahead=2)
        own_ready = st.sem("own_ready", ahead=1)
        other_ready = st.sem("other_ready", ahead=1)
        used = st.sem("used", ahead=2 * ROWS)
        inverse_done, spread_done = st.sem("inverse_done"), st.sem("spread_done", ahead=1)
        inverse_turned, inverse_copied = st.sem("inverse_turned", ahead=2), st.sem("inverse_copied")
        y_done = st.sem("y_done", ahead=2)
        block = st.block()
        psum = chip.psum

        def tile_loop(eng, body):
            with eng.Fori(0, B) as b:
                body(b, 0, 0, True, False, False)
                body(b, 1, 1, False, True, False)
                with eng.Fori(1, PER_B // 2 - 1) as pair:
                    body(b, pair * 2, 0, False, False, False)
                    body(b, pair * 2 + 1, 1, False, False, False)
                body(b, PER_B - 2, 0, False, False, False)
                body(b, PER_B - 1, 1, False, False, True)

        def later(b, c, p, r, first, last, steps):
            if r + steps < ROWS:
                return b, c, p, r + steps, first
            return None if last else (b, c + 1, 1 - p, r + steps - ROWS, False)

        def place(first, a, h):
            return (h // 2, h % 2) if first else (a, h)

        def half_of(buf, first, half):
            return buf[:, half, 0:2 if first else SLOTS, :].rearrange("p s i -> p (s i)")

        def half_of_bank(first, half):
            return psum[:, 4 + half, 0:2 * P if first else SLOTS * P]

        @block.gpsimd
        def _(pool):
            def prepare(b, c, p, first):
                n = b * PER_B + c
                cols = bass.ts(n, P)
                pool.wait_ge(scores_done, (n + 1) * ROWS)
                pool.tensor_copy(qc[p][:, :], qT[:, cols])
                for a in range(1 if first else 2):
                    last = pool.tensor_tensor(keys[p][:, a, :, :], kT[:, bass.ts(n - a, P)].unsqueeze(1).to_broadcast([P, SLOTS, P]),
                                              slot[:, :].unsqueeze(2).to_broadcast([P, SLOTS, P]), ALU.mult)
                last.then_inc(prepared, 1)
                pool.wait_ge(used, (n + 1) * ROWS)
                for a in range(1 if first else 2):
                    last = pool.tensor_tensor(vals[p][:, a, :, :], v_tok[:, bass.ds(n - a, 1), :].to_broadcast([P, SLOTS, P]),
                                              slot_cols[:, :, :], ALU.mult)
                last.then_inc(prepared_v, 1)

            tile_loop(pool, lambda b, c, p, first, second, last: prepare(b, c, p, first))

        @block.tensor
        def _(pe):
            def scores(b, c, p, r, first):
                n = b * PER_B + c
                s = n * ROWS + r
                if r == 0:
                    pe.wait_ge(prepared, n + 1)
                pe.wait_ge(biased_done, s + 1)
                rows = slice(32 * r, 32 * r + 32)
                for a in range(1 if first else 2):
                    mm = pe.matmul(psum[:, r % 2 * 2 + a, :], qc[p][rows, :],
                                   keys[p][rows, a, :, :].rearrange("p s j -> p (s j)"), start=True, stop=True)
                mm.then_inc(scores_done, 1)

            def turn(b, c, p, r, first):
                s = (b * PER_B + c) * ROWS + r
                pe.wait_ge(exp_done, (s + 3) * SLOTS)
                pe.wait_ge(own_ready, s + 1)
                pe.wait_ge(other_ready, s + 1)
                for a in range(1 if first else 2):
                    for h in range(SLOTS):
                        bank, col = place(first, a, h)
                        mm = nc_t(pe, psum[:, 4 + bank, col * P:(col + 1) * P], expd[r % 2][:, a, h, :], chip)
                mm.then_inc(turned, 1)

            def times_v(b, c, p, r, first):
                n = b * PER_B + c
                s = n * ROWS + r
                if r == 0:
                    pe.wait_ge(prepared_v, n + 1)
                    pe.wait_ge(y_done, n + 1)
                pe.wait_ge(own_ready, s + 2)
                pe.wait_ge(other_ready, s + 2)
                rows = slice(32 * r, 32 * r + 32)
                blocks = 1 if first else 2
                for a in range(blocks):
                    for h in range(SLOTS):
                        half, col = place(first, a, h)
                        mm = pe.matmul(psum[rows, 6 + p, 0:P], vals[p][:, a, h, rows], probsT[r % 2][:, half, col, :],
                                       start=(a == 0 and h == 0), stop=(a == blocks - 1 and h == SLOTS - 1))
                mm.then_inc(used, 1)

            def finish(b, c, p, first):
                n = b * PER_B + c
                times_v(b, c, p, ROWS - 1, first)
                pe.wait_ge(spread_done, n + 2)
                nc_t(pe, psum[:, 6 + p, P:2 * P], spread_inv[p][:, :, :].rearrange("p h e -> p (h e)"),
                     chip).then_inc(inverse_turned, 1)

            def tile(b, c, p, first, second, last):
                if first:
                    scores(b, c, p, 0, True)
                    scores(b, c, p, 1, True)
                for r in range(ROWS):
                    ahead = later(b, c, p, r, first, last, 2)
                    if ahead:
                        scores(*ahead)
                    turn(b, c, p, r, first)
                    if r > 0:
                        times_v(b, c, p, r - 1, first)
                    elif not first:
                        finish(b, c - 1, 1 - p, second)
                if last:
                    finish(b, c, p, False)

            tile_loop(pe, tile)

        @block.vector
        def _(dve):
            def bias_and_max(b, c, p, r, first):
                s = (b * PER_B + c) * ROWS + r
                dve.wait_ge(scores_done, s + 1 + 2 * ROWS)
                dve.wait_ge(exp_done, (s + 1) * SLOTS)
                blocks = 1 if first else 2
                for a in range(blocks):
                    last = dve.scalar_tensor_tensor(
                        biased[r % 2][:, a, :, :].rearrange("p s j -> p (s j)"), psum[:, r % 2 * 2 + a, :], float(DH0) ** -0.5,
                        slope[:, r, a, :, :].rearrange("p s j -> p (s j)"), ALU.mult, ALU.add)
                last.then_inc(biased_done, 1)
                dve.wait_ge(biased_done, s + 3)
                dve.tensor_reduce(low[:, r % 2, :], biased[r % 2][:, 0:blocks, :, :].rearrange("p a s j -> p s a j"),
                                  mybir.AxisListType.XY, ALU.max, negate=True).then_inc(max_done, 1)

            def copy_turned(b, c, p, r, first):
                s = (b * PER_B + c) * ROWS + r
                dve.wait_ge(turned, s + 3)
                dve.wait_ge(used, s + 7)
                dve.tensor_copy(half_of(probsT[r % 2], first, 0), half_of_bank(first, 0)).then_inc(own_ready, 1)

            def invert(b, c, p):
                n = b * PER_B + c
                dve.wait_ge(exp_done, (n + 1) * ROWS * SLOTS + 2 * SLOTS)
                dve.wait_ge(spread_done, n + 1)
                dve.reciprocal(inverse[:, :], sums[:, p, :]).then_inc(inverse_done, 1)
                dve.wait_ge(inverse_done, n + 1)
                dve.wait_ge(inverse_turned, n + 1)
                dve.tensor_copy(spread_inv[p][:, :, :], inverse[:, :].unsqueeze(2).to_broadcast([P, H, DH0])).then_inc(
                    spread_done, 1)

            def finish(b, c, p):
                n = b * PER_B + c
                dve.wait_ge(used, (n + 3) * ROWS)
                dve.wait_ge(inverse_copied, n + 1)
                dve.tensor_tensor(attended[:, bass.ts(n, P)], psum[:, 6 + p, 0:P], inverseT[:, p, :],
                                  ALU.mult).then_inc(y_done, 1)

            def tile(b, c, p, first, second, last):
                if first:
                    bias_and_max(b, c, p, 0, True)
                    bias_and_max(b, c, p, 1, True)
                for r in range(ROWS):
                    ahead = later(b, c, p, r, first, last, 2)
                    if ahead:
                        bias_and_max(*ahead)
                    copy_turned(b, c, p, r, first)
                    if r == 1 and not first:
                        finish(b, c - 1, 1 - p)
                invert(b, c, p)
                if last:
                    finish(b, c, p)

            tile_loop(dve, tile)

        @block.scalar
        def _(act):
            def exponentials(b, c, p, r, first):
                s = (b * PER_B + c) * ROWS + r
                act.wait_ge(max_done, s + 1)
                act.wait_ge(turned, s + 1)
                for h in range(SLOTS):
                    act.activation(expd[r % 2][:, 0:1 if first else 2, h, :], biased[r % 2][:, 0:1 if first else 2, h, :], ACT.Exp,
                                   bias=low[:, r % 2, h:h + 1],
                                   accum_out=sums[:, p, r * SLOTS + h:r * SLOTS + h + 1]).then_inc(exp_done, 1)

            def copy_turned(b, c, p, r, first):
                s = (b * PER_B + c) * ROWS + r
                act.wait_ge(turned, s + 3)
                act.wait_ge(used, s + 7)
                act.copy(half_of(probsT[r % 2], first, 1), half_of_bank(first, 1)).then_inc(other_ready, 1)

            def copy_inverse(b, c, p):
                n = b * PER_B + c
                act.wait_ge(inverse_turned, n + 3)
                act.wait_ge(y_done, n + 1)
                act.copy(inverseT[:, p, :], psum[:, 6 + p, P:2 * P]).then_inc(inverse_copied, 1)

            def tile(b, c, p, first, second, last):
                if first:
                    exponentials(b, c, p, 0, True)
                for r in range(ROWS):
                    ahead = later(b, c, p, r, first, last, 1)
                    if ahead:
                        exponentials(*ahead)
                    copy_turned(b, c, p, r, first)
                    if r == 0 and not first:
                        copy_inverse(b, c - 1, 1 - p)
                if last:
                    copy_inverse(b, c, p)

            tile_loop(act, tile)


WIDE = 64
HID = H * WIDE
BLOCKS = HID // P
RMS_EPS = 2.0 ** -23


def gated_attention(chip, norm):
    with Stage(chip, "gla") as outer:
        reach = outer.sb("reach", [P, TILES, H])
        left = outer.sb("left", [P, TILES, H])
        whole = outer.sb("whole", [P, TILES, BLOCKS])
        reach_rows = chip.nc.dram_tensor("reach_rows", (H, TOK), F32).ap()
        gained_rows = chip.nc.dram_tensor("gained_rows", (H, TOK), F32).ap()
        wd, bd = outer.sb("wd", [P, H]), outer.sb("bd", [P, H])
        sums = outer.sb("sums", [P, 3, P])
        w = GatedWeights(outer)
        norm([(wd[:, :], chip.dram["gla_wd"]), (bd[:, :], chip.dram["gla_bd"]), (sums[:, :, :], chip.dram["gla_sums"])]
             + w.loads(chip))
        decay_stage(chip, wd, bd, sums, reach, left, whole, reach_rows, gained_rows, w.matrices())
        gated_chunks(chip, w, reach, left, whole, reach_rows, gained_rows)


class GatedWeights:

    def __init__(self, st):
        self.raw = {n: st.sb(n, [P, HID]) for n in ("wk", "wg", "wv", "wq", "wog")}
        self.parts = {n: [st.sb(f"{n}_{part}", [P, HID], F32R) for part in PARTS] for n in ("wk", "wg", "wv")}
        self.wo = st.sb("wo", [P, BLOCKS, D])
        self.norm_w = st.sb("norm_w", [P, BLOCKS])
        self.causal = st.sb("causal", [P, P])

    def loads(self, chip):
        pairs = [(buf[:, :], chip.dram["gla_" + n]) for n, buf in self.raw.items()]
        return pairs + [(self.wo[:, :, :], chip.dram["gla_wo"]), (self.norm_w[:, :], chip.dram["gla_norm_w"]),
                        (self.causal[:, :], chip.dram["causal"])]

    def matrices(self):
        return [(self.raw[n][:, :], [part[:, :] for part in self.parts[n]]) for n in self.parts]


def decay_stage(chip, wd, bd, sums, reach, left, whole, reach_rows, gained_rows, matrices):
    N = TILES * H
    with Stage(chip, "decay") as st:
        z, size, log1p, g = (st.sb(n, [P, TILES, H]) for n in ("z", "size", "log1p", "g"))
        reachT, gainedT = st.sb("reachT", [H, TOK]), st.sb("gainedT", [H, TOK])
        logits_done, own = st.sem("logits_done"), st.sem("dve_steps")
        asked, answered = st.sem("asked"), st.sem("answered")
        g_done, sums_done, copied = st.sem("g_done"), st.sem("sums_done"), st.sem("copied")
        turned, stored, rows_copied = st.sem("turned"), st.sem("stored"), st.sem("rows_copied")
        gained_done = st.sem("gained_done")
        rounded = st.sem("rounded")
        block = st.block()
        psum = chip.psum
        logits = psum[:, 0, 0:N].rearrange("p (t h) -> p t h", h=H)

        @block.sync
        def _(sp):
            sp.wait_ge(rows_copied, 4)
            sp.dma_start(reach_rows, reachT[:, :]).then_inc(stored, 16)
            sp.wait_ge(gained_done, 1)
            sp.dma_start(gained_rows, gainedT[:, :]).then_inc(stored, 16)
            sp.wait_ge(stored, 32)

        @block.tensor
        def _(pe):
            for t in range(TILES):
                mm = pe.matmul(logits[:, t, :], chip.xnT[:, t * P:(t + 1) * P], wd[:, :], start=True, stop=True)
            mm.then_inc(logits_done, 1)
            pe.wait_ge(g_done, 1)
            for k in range(3):
                mm = pe.matmul(psum[:, 1 + k, 0:N], sums[:, k, :], g[:, :, :].rearrange("p t h -> p (t h)"), start=True, stop=True)
            mm.then_inc(sums_done, 1)
            pe.wait_ge(copied, 1)
            for t in range(TILES):
                turn = nc_t(pe, psum[0:H, 4 + t // 4, t % 4 * P:(t % 4 + 1) * P], reach[:, t, :], chip)
                if t % 4 == 3:
                    turn.then_inc(turned, 1)

        @block.vector
        def _(dve):
            done = Chain(dve, own).done
            for k, (raw, (high, low)) in enumerate(matrices):
                dve.wait_ge(rounded, k + 1)
                dve.tensor_tensor(low, raw, high.bitcast(F32), ALU.subtract)
            dve.wait_ge(logits_done, 1)
            done(dve.tensor_tensor(z[:, :, :], logits, bd[:, :].unsqueeze(1).to_broadcast([P, TILES, H]), ALU.add))
            done(dve.tensor_scalar(size[:, :, :], z[:, :, :], -1.0, None, ALU.mult))
            dve.tensor_tensor(size[:, :, :], size[:, :, :], z[:, :, :], ALU.min).then_inc(asked, 1)
            dve.wait_ge(answered, 1)
            dve.tensor_scalar(log1p[:, :, :], log1p[:, :, :], 1.0, None, ALU.add).then_inc(asked, 1)
            dve.wait_ge(answered, 2)
            done(dve.scalar_tensor_tensor(g[:, :, :], z[:, :, :], 0.0, log1p[:, :, :], ALU.max, ALU.add))
            dve.tensor_scalar(g[:, :, :], g[:, :, :], -1.0, None, ALU.mult).then_inc(g_done, 1)
            dve.wait_ge(sums_done, 1)
            dve.tensor_copy(reach[:, :, :].rearrange("p t h -> p (t h)"), psum[:, 1, 0:N]).then_inc(copied, 1)
            for q in range(4):
                dve.wait_ge(turned, q + 1)
                dve.tensor_copy(reachT[:, q * GROUP:(q + 1) * GROUP], psum[0:H, 4 + q, :]).then_inc(rows_copied, 1)

        @block.scalar
        def _(act):
            for raw, (high, _) in matrices:
                act.copy(high, raw).then_inc(rounded, 1)
            act.wait_ge(asked, 1)
            act.activation(log1p[:, :, :], size[:, :, :], ACT.Exp).then_inc(answered, 1)
            act.wait_ge(asked, 2)
            act.activation(log1p[:, :, :], log1p[:, :, :], ACT.Ln).then_inc(answered, 1)
            act.wait_ge(sums_done, 1)
            act.activation(left[:, :, :].rearrange("p t h -> p (t h)"), psum[:, 2, 0:N], ACT.Exp)
            pairs = psum[:, 3, 0:N].rearrange("p (t m two) -> p t m two", m=BLOCKS, two=2)
            for half in range(2):
                rows = slice(half * WIDE, (half + 1) * WIDE)
                act.activation(whole[rows, :, :], pairs[rows, :, :, half], ACT.Exp)
            act.wait_ge(rows_copied, 4)
            act.activation(gainedT[:, :], reachT[:, :], ACT.Exp).then_inc(gained_done, 1)


def split_columns(pool, whole, parts, columns, ones, standing, n):
    high, low = parts
    pool.tensor_copy(whole[:, :], columns).then_inc(standing, 1)
    pool.tensor_tensor(high[:, :], columns, ones, ALU.mult).then_inc(standing, 1)
    pool.wait_ge(standing, 3 * n + 5)
    pool.tensor_tensor(low[:, :], whole[:, :], high[:, :].bitcast(F32), ALU.subtract).then_inc(standing, 1)


def project_tokens(pe, out, columns, matrix):
    for half in range(2):
        cols = slice(half * GROUP, (half + 1) * GROUP)
        mm = split_product(pe, out[:, cols], [c[:, :] for c in columns], [m[:, cols] for m in matrix])
    return mm


def rows_of_chunks(eng, start, chunk):
    start()
    for b in range(B):
        with eng.Fori(0, PER_B // 2 - 1) as pair:
            for p in range(2):
                chunk(b, b * PER_B + pair * 2 + p, p, False, False)
        for p in range(2):
            chunk(b, b * PER_B + PER_B - 2 + p, p, p == 1, p == 1 and b == B - 1)


def by_head(buf, width=WIDE):
    return buf[:, :].rearrange("p (h e) -> p h e", e=width)


def spread(v, width=WIDE):
    return v[:, :].unsqueeze(2).to_broadcast([P, v.shape[1], width])


def head_of(k):
    return k // 8 * 8 + k % 4 * 2 + k // 4 % 2


def gated_chunks(chip, w, reach, left, whole, reach_rows, gained_rows):
    with Stage(chip, "gla_chunks") as st:
        def count(name, ahead=1):
            return st.sem(name, ahead=ahead)

        wo, norm_w, causal, wq, wog = w.wo, w.norm_w, w.causal, w.raw["wq"], w.raw["wog"]
        ones = st.sb("ones", [P, P])
        xc = [st.sb(f"xc{p}", [P, P]) for p in range(2)]
        x_parts = [[st.sb(f"xc{p}_{part}", [P, P], F32R) for part in PARTS] for p in range(2)]
        reach_bc = st.sb("reach_bc", [P, H, P])
        gained_bc = st.sb("gained_bc", [P, BLOCKS, P])
        k_tok, v_tok = ([st.sb(f"{n}{p}", [P, HID]) for p in range(2)] for n in ("k_tok", "v_tok"))
        gate, v_left = st.sb("gate", [P, HID]), st.sb("v_left", [P, HID])
        og, z, square, qT, qd, kT = (st.sb(n, [P, BLOCKS, P]) for n in ("og", "z", "square", "qT", "qd", "kT"))
        decay, probs = st.sb("decay", [P, H, P]), st.sb("probs", [P, H, P])
        rstd = st.sb("rstd", [P, P])
        state = st.sb("state", [P, BLOCKS, P])
        ones_done, wo_ready = st.sem("ones_done"), st.sem("wo_ready")
        x_in = count("x_in", ahead=3)
        rows_in, gained_in = st.sem("rows_in"), st.sem("gained_in")
        k_done, gate_done, v_done, og_done, q_done = (count(n + "_done") for n in ("k", "gate", "v", "og", "q"))
        gate_ready, k_ready, v_ready, og_ready, q_ready = (count(n + "_ready") for n in ("gate", "k", "v", "og", "q"))
        kt_done, kt_ready = count("kt_done"), count("kt_ready")
        arg_done, decay_done = count("arg_done"), count("decay_done")
        score_done, probs_done = count("score_done"), count("probs_done")
        v_left_done, qd_done, past_done = count("v_left_done"), count("qd_done"), count("past_done")
        intra_done, z_ready, square_done = count("intra_done"), count("z_ready"), count("square_done")
        update_done, decayed = count("update_done"), count("decayed")
        state_done = count("state_done")
        y_done, power_done, shifted, std_done, rstd_done = (
            count(n) for n in ("y_done", "power_done", "shifted", "std_done", "rstd_done"))
        y_read = count("y_read", ahead=2)
        block = st.block()
        psum = chip.psum
        R, PLACES = 4, 4

        def two(n):
            return psum[:, n:n + 2, :].rearrange("p a f -> p (a f)")

        gate_ps, v_ps, kT_ps = two(0), two(0), two(0)
        k_ps, q_ps, og_ps = two(2), two(2), two(2)
        update_ps, out_ps = two(4).rearrange("p (m f) -> p m f", f=P), two(6)
        y_ps, power_ps = psum[:, 0, 0:P], psum[:, 0, P:2 * P]

        def flat(buf):
            return buf[:, :, :].rearrange("p m i -> p (m i)")

        halves = [slice(0, WIDE), slice(WIDE, P)]

        def rows_of(h):
            return slice(h % 2 * WIDE, h % 2 * WIDE + WIDE)

        @block.sync
        def _(sp):
            with sp.Fori(0, TILES) as n:
                sp.wait_ge(arg_done, n + 1)
                sp.dma_start(reach_bc[:, :, :], reach_rows[:, bass.ts(n, P)].unsqueeze(0).to_broadcast([P, H, P])).then_inc(rows_in, 16)
                sp.wait_ge(qd_done, n + 1)
                for half in range(2):
                    rows = gained_rows.rearrange("(m two) t -> two m t", two=2)[half, :, bass.ts(n, P)]
                    sp.dma_start(gained_bc[half * WIDE:(half + 1) * WIDE, :, :],
                                 rows.unsqueeze(0).to_broadcast([WIDE, BLOCKS, P])).then_inc(gained_in, 16)

        @block.gpsimd
        def _(pool):
            pool.memset(ones[:, :], 1.0).then_inc(ones_done, 1)
            pool.wait_ge(ones_done, 1)
            with pool.Fori(0, TILES // 2) as pair:
                for p in range(2):
                    n = pair * 2 + p
                    pool.wait_ge(og_done, n + 1)
                    split_columns(pool, xc[p], x_parts[p], chip.xnT[:, bass.ts(n, P)], ones[:, :], x_in, n)
                    pool.wait_ge(v_ready, n + 2)
                    pool.wait_ge(update_done, n + 1)
                    pool.tensor_tensor(by_head(v_left), by_head(v_tok[p]), left[:, bass.ds(n, 1), :].rearrange(
                        "p a h -> p (a h)").unsqueeze(2).to_broadcast([P, H, WIDE]), ALU.mult).then_inc(v_left_done, 1)
                    pool.wait_ge(q_ready, n + 2)
                    pool.wait_ge(gained_in, (n + 1) * 32)
                    pool.wait_ge(past_done, n + 1)
                    pool.tensor_tensor(qd[:, :, :], qT[:, :, :], gained_bc[:, :, :], ALU.mult).then_inc(qd_done, 1)

        @block.tensor
        def _(pe):
            pe.wait_ge(ones_done, 1)
            pe.wait_ge(wo_ready, 1)

            def token_major(out, name, p):
                return project_tokens(pe, out, x_parts[p], w.parts[name])

            def feature_major(out, weights, p):
                for m in range(BLOCKS):
                    cols = slice(m * P, (m + 1) * P)
                    mm = pe.matmul(out[:, cols], weights[:, cols], xc[p][:, :], start=True, stop=True)
                return mm

            def gates(n, p):
                pe.wait_ge(x_in, 3 * n + 6)
                token_major(gate_ps, "wg", p).then_inc(gate_done, 1)

            def keys(n, p):
                pe.wait_ge(og_ready, n + 1)
                token_major(k_ps, "wk", p).then_inc(k_done, 1)

            def values(n, p):
                pe.wait_ge(gate_ready, n + 2)
                token_major(v_ps, "wv", p).then_inc(v_done, 1)

            def queries(n, p):
                pe.wait_ge(k_ready, n + 2)
                feature_major(q_ps, wq, p).then_inc(q_done, 1)

            def turned_keys(n, p):
                pe.wait_ge(v_ready, n + 2)
                for m in range(BLOCKS):
                    mm = nc_t(pe, kT_ps[:, m * P:(m + 1) * P], k_tok[p][:, m * P:(m + 1) * P], chip)
                mm.then_inc(kt_done, 1)

            def output_gates(n, p):
                pe.wait_ge(q_ready, n + 2)
                feature_major(og_ps, wog, p).then_inc(og_done, 1)

            def score_rounds(n, rounds):
                for s in range(PLACES):
                    for r in rounds:
                        h = head_of(r * PLACES + s)
                        mm = pe.matmul(psum[:, 4 + r % 2, s * P:(s + 1) * P], kT[rows_of(h), h // 2, :],
                                       qT[rows_of(h), h // 2, :], start=True, stop=True)
                        if s == PLACES - 1:
                            mm.then_inc(score_done, 1)

            def intra(n, p, r):
                pe.wait_ge(probs_done, n * R + r + 2)
                for k in range(r * PLACES, (r + 1) * PLACES):
                    h = head_of(k)
                    mm = pe.matmul(out_ps[rows_of(h), h // 2 * P:(h // 2 + 1) * P], v_tok[p][:, h * WIDE:(h + 1) * WIDE],
                                   probs[:, k, :], start=False, stop=(k % PLACES == PLACES - 1), skip_group_check=True)
                if r == R - 1:
                    mm.then_inc(intra_done, 1)

            def start():
                b, n = 0, 0
                gates(n, 0)
                keys(n, 0)
                values(n, 0)
                queries(n, 0)
                turned_keys(n, 0)
                output_gates(n, 0)

            def chunk(b, n, p, row_end, last):
                pe.wait_ge(state_done, n + b + 2)
                pe.wait_ge(kt_ready, n + 2)
                score_rounds(n, (0, 1))
                pe.wait_ge(qd_done, n + 2)
                pe.wait_ge(square_done, n + 1)
                for m in range(BLOCKS):
                    mm = pe.matmul(out_ps[:, m * P:(m + 1) * P], state[:, m, :], qd[:, m, :], start=(m % (BLOCKS // 2) == 0),
                                   stop=False, skip_group_check=True)
                mm.then_inc(past_done, 1)
                if not last:
                    pe.wait_ge(y_read, n + 2)
                    gates(n + 1, 1 - p)
                pe.wait_ge(probs_done, n * R + 3)
                score_rounds(n, (2, 3))
                if not last:
                    keys(n + 1, 1 - p)
                intra(n, p, 0)
                intra(n, p, 1)
                if not last:
                    values(n + 1, 1 - p)
                intra(n, p, 2)
                intra(n, p, 3)
                pe.wait_ge(v_left_done, n + 2)
                for m in range(BLOCKS):
                    cols = slice(m * P, (m + 1) * P)
                    mm = pe.matmul(update_ps[:, m, :], k_tok[p][:, cols], v_left[:, cols], start=True, stop=True)
                mm.then_inc(update_done, 1)
                if not last:
                    queries(n + 1, 1 - p)
                    turned_keys(n + 1, 1 - p)
                    output_gates(n + 1, 1 - p)
                    pe.wait_ge(kt_ready, n + 3)
                pe.wait_ge(z_ready, n + 2)
                for m in range(BLOCKS):
                    mm = pe.matmul(y_ps, wo[:, m, :], z[:, m, :], start=(m == 0), stop=(m == BLOCKS - 1))
                mm.then_inc(y_done, 1)
                pe.wait_ge(square_done, n + 2)
                for m in range(BLOCKS):
                    mm = pe.matmul(power_ps, ones[:, :], square[:, m, :], start=(m == 0), stop=(m == BLOCKS - 1))
                mm.then_inc(power_done, 1)

            rows_of_chunks(pe, start, chunk)

        @block.vector
        def _(dve):
            dve.tensor_tensor(wo[:, :, :], wo[:, :, :], spread(norm_w, D), ALU.mult).then_inc(wo_ready, 1)

            def take_k(n, p, first=False):
                dve.wait_ge(gate_ready, n + 2)
                dve.wait_ge(k_done, n + 2)
                if not first:
                    dve.wait_ge(update_done, n)
                dve.tensor_tensor(k_tok[p][:, :], gate[:, :], k_ps, ALU.mult).then_inc(k_ready, 1)

            def decay_args(n):
                dve.wait_ge(rows_in, (n + 1) * 16)
                dve.wait_ge(probs_done, n * R + 1)
                for k in range(H):
                    h = head_of(k)
                    last = dve.scalar_tensor_tensor(decay[:, k, :], reach_bc[:, h, :], reach[:, bass.ds(n, 1), h:h + 1].rearrange(
                        "p a h -> p (a h)"), causal[:, :], ALU.subtract, ALU.add)
                last.then_inc(arg_done, 1)

            def take_kt(n):
                dve.wait_ge(kt_done, n + 2)
                dve.wait_ge(score_done, n * R + 1)
                dve.tensor_copy(flat(kT), kT_ps).then_inc(kt_ready, 1)

            def clear_state(steps):
                dve.wait_ge(state_done, steps)
                dve.memset(state[:, :, :], 0.0).then_inc(state_done, 1)

            def start():
                b, n = 0, 0
                clear_state(1)
                take_k(n, 0, first=True)
                decay_args(n)
                take_kt(n)

            def chunk(b, n, p, row_end, last):
                dve.wait_ge(decay_done, n + 2)
                for r in range(R):
                    dve.wait_ge(score_done, n * R + r + 2)
                    dve.wait_ge(intra_done, n + 1)
                    heads = slice(r * PLACES, (r + 1) * PLACES)
                    dve.tensor_tensor(probs[:, heads, :].rearrange("p s i -> p (s i)"), psum[:, 4 + r % 2, :],
                                      decay[:, heads, :].rearrange("p s i -> p (s i)"), ALU.mult).then_inc(probs_done, 1)
                if not last:
                    take_k(n + 1, 1 - p)
                    decay_args(n + 1)
                dve.wait_ge(past_done, n + 2)
                dve.wait_ge(state_done, n + b + 2)
                for rows in halves:
                    mult = dve.tensor_tensor(state[rows, :, rows], state[rows, :, rows], whole[rows, bass.ds(n, 1), :].rearrange(
                        "p a m -> p (a m)").unsqueeze(2).to_broadcast([WIDE, BLOCKS, WIDE]), ALU.mult)
                mult.then_inc(decayed, 1)
                dve.wait_ge(intra_done, n + 2)
                dve.wait_ge(og_ready, n + 2)
                dve.wait_ge(y_done, n + 1)
                dve.tensor_tensor(flat(z), out_ps, flat(og), ALU.mult).then_inc(z_ready, 1)
                dve.wait_ge(update_done, n + 2)
                dve.wait_ge(decayed, n + 2)
                for rows in halves:
                    add = dve.tensor_tensor(state[rows, :, rows], state[rows, :, rows], update_ps[rows, :, rows], ALU.add)
                add.then_inc(state_done, 1)
                if row_end and not last:
                    clear_state(n + b + 3)
                if not last:
                    take_kt(n + 1)
                dve.wait_ge(power_done, n + 2)
                dve.tensor_scalar(rstd[:, :], power_ps, 1.0 / HID, RMS_EPS, ALU.mult, ALU.add).then_inc(shifted, 1)
                dve.wait_ge(std_done, n + 2)
                dve.reciprocal(rstd[:, :], rstd[:, :]).then_inc(rstd_done, 1)
                dve.wait_ge(rstd_done, n + 2)
                dve.wait_ge(y_done, n + 2)
                dve.tensor_tensor(chip.yT[:, bass.ts(n, P)], y_ps, rstd[:, :], ALU.mult).then_inc(y_read, 1)

            rows_of_chunks(dve, start, chunk)

        @block.scalar
        def _(act):
            def take_gate(n):
                act.wait_ge(gate_done, n + 2)
                act.wait_ge(k_ready, n + 1)
                act.activation(gate[:, :], gate_ps, ACT.Sigmoid).then_inc(gate_ready, 1)

            def take_v(n, p):
                act.wait_ge(v_done, n + 2)
                act.wait_ge(intra_done, n)
                act.wait_ge(v_left_done, n)
                act.copy(v_tok[p][:, :], v_ps).then_inc(v_ready, 1)

            def take_decay(n):
                act.wait_ge(arg_done, n + 2)
                act.activation(decay[:, :, :], decay[:, :, :], ACT.Exp).then_inc(decay_done, 1)

            def take_q(n):
                act.wait_ge(q_done, n + 2)
                act.wait_ge(score_done, n * R + 1)
                act.wait_ge(qd_done, n + 1)
                act.copy(flat(qT), q_ps).then_inc(q_ready, 1)

            def take_og(n):
                act.wait_ge(og_done, n + 2)
                act.wait_ge(z_ready, n + 1)
                act.activation(flat(og), og_ps, ACT.Sigmoid).then_inc(og_ready, 1)

            def start():
                b, n = 0, 0
                take_gate(n)
                act.wait_ge(v_done, n + 2)
                act.copy(v_tok[0][:, :], v_ps).then_inc(v_ready, 1)
                take_decay(n)
                take_q(n)
                take_og(n)

            def chunk(b, n, p, row_end, last):
                if not last:
                    take_gate(n + 1)
                    take_v(n + 1, 1 - p)
                    take_decay(n + 1)
                    take_q(n + 1)
                act.wait_ge(z_ready, n + 2)
                act.wait_ge(power_done, n + 1)
                act.activation(flat(square), out_ps, ACT.Square).then_inc(square_done, 1)
                if not last:
                    take_og(n + 1)
                act.wait_ge(shifted, n + 2)
                act.activation(rstd[:, :], rstd[:, :], ACT.Sqrt).then_inc(std_done, 1)

            rows_of_chunks(act, start, chunk)


FINITE = 3e38


def feature_attention(chip, norm):
    with Stage(chip, "features") as st:
        def count(name):
            return st.sem(name, ahead=1)

        wq, wk, wv = (st.sb(n, [P, HID]) for n in ("wq", "wk", "wv"))
        wo = st.sb("wo", [P, BLOCKS, D])
        bo = st.sb("bo", [P, 1])
        omega = st.sb("omega", [P, P])
        half_norm = st.sb("half_norm", [P, P])
        allowed = st.sb("allowed", [P, P])
        own_head = st.sb("own_head", [H, BLOCKS, P])
        v_aug = st.sb("v_aug", [P, H, P])
        xc = [st.sb(f"xc{p}", [P, P]) for p in range(2)]
        x_parts = [[st.sb(f"xc{p}_{part}", [P, P], F32R) for part in PARTS] for p in range(2)]
        wv_parts = [st.sb(f"wv_{part}", [P, HID], F32R) for part in PARTS]
        omega_parts = [st.sb(f"omega_{part}", [P, P], F32R) for part in PARTS]
        half_parts = [st.sb(f"half_norm_{part}", [P, P], F32R) for part in PARTS]
        k_parts, q_parts, k2_parts, q2_parts = ([st.sb(f"{n}_{part}", [P, BLOCKS, P], F32R) for part in PARTS]
                                                for n in ("k", "q", "k2", "q2"))
        ones = st.sb("ones", [P, 1])
        qT, kT, q2, k2, phi_q, phi_k = (st.sb(n, [P, BLOCKS, P]) for n in ("qT", "kT", "q2", "k2", "phi_q", "phi_k"))
        z, inverse = st.sb("z", [P, BLOCKS, P]), st.sb("inverse", [P, BLOCKS, P])
        k_tok = st.sb("k_tok", [P, HID])
        probs = st.sb("probs", [P, H, P])
        sums = st.sb("sums", [H, 2, P])
        state = st.sb("state", [P, BLOCKS, P])
        norm([(wq[:, :], chip.dram["fea_wq"]), (wk[:, :], chip.dram["fea_wk"]), (wv[:, :], chip.dram["fea_wv"]),
              (wo[:, :, :], chip.dram["fea_wo"]), (bo[:, :], chip.dram["fea_bo"]), (omega[:, :], chip.dram["fea_omega"]),
              (half_norm[:, :], chip.dram["fea_half_norm"]), (allowed[:, :], chip.dram["allowed"]),
              (own_head[:, :, :], chip.dram["own_head"]), (v_aug[:, :, :], chip.dram["v_fill"])])
        split_stage(chip, "feature_matrices", [(raw[:, :], [part[:, :] for part in parts]) for raw, parts in
                                               ((omega, omega_parts), (half_norm, half_parts), (wv, wv_parts))])
        k_high, q_high = st.sem("k_high", ahead=2), st.sem("q_high", ahead=2)
        k_split, q_split = st.sem("k_split", ahead=2), st.sem("q_split", ahead=2)
        ones_done = st.sem("ones_done")
        x_in = st.sem("x_in", ahead=3)
        q_done, k_done, v_done = count("q_done"), count("k_done"), count("v_done")
        q_ready, k_ready, v_ready = count("q_ready"), count("k_ready"), count("v_ready")
        k_squares, q_squares = count("k_squares"), count("q_squares")
        k_arg_done, q_arg_done = count("k_arg_done"), count("q_arg_done")
        phi_k_ready, phi_q_ready = count("phi_k_ready"), count("phi_q_ready")
        kt_done, kt_ready = count("kt_done"), count("kt_ready")
        score_done, probs_done = count("score_done"), count("probs_done")
        past_done, update_done = count("past_done"), count("update_done")
        state_done = count("state_done")
        out_done, sum_steps, summed = count("out_done"), st.sem("sum_steps"), count("summed")
        inverse_done, inverse_ready = count("inverse_done"), count("inverse_ready")
        z_ready, y_done, y_read = count("z_ready"), count("y_done"), count("y_read")
        block = st.block()
        psum = chip.psum
        R, PLACES = 4, 4

        def two(n):
            return psum[:, n:n + 2, :].rearrange("p a f -> p (a f)")

        update_ps = two(0).rearrange("p (m f) -> p m f", f=P)
        arg_ps, y_ps = two(0), psum[:, 0, 0:P]
        k_ps, q_ps, v_ps, inverse_ps, kt_ps = two(2), two(2), two(2), two(2), two(2)
        out_ps = psum[:, 4:8, :].rearrange("p (a two) f -> p two a f", two=2)

        def flat(buf):
            return buf[:, :, :].rearrange("p m i -> p (m i)")

        def rows_of(h):
            return slice(h % 2 * WIDE, h % 2 * WIDE + WIDE)

        @block.gpsimd
        def _(pool):
            pool.memset(ones[:, :], 1.0).then_inc(ones_done, 1)
            pool.wait_ge(ones_done, 1)
            with pool.Fori(0, TILES // 2) as pair:
                for p in range(2):
                    n = pair * 2 + p
                    pool.wait_ge(v_done, n + 1)
                    split_columns(pool, xc[p], x_parts[p], chip.xnT[:, bass.ts(n, P)], ones[:, :].to_broadcast([P, P]), x_in, n)
                    for ready, read, done, src, dst in ((k_ready, k_split, k_squares, kT, k2),
                                                        (q_ready, q_split, q_squares, qT, q2)):
                        pool.wait_ge(ready, n + 2)
                        pool.wait_ge(read, 2 * n + 2)
                        pool.tensor_tensor(dst[:, :, :], src[:, :, :], src[:, :, :], ALU.mult).then_inc(done, 1)

        @block.tensor
        def _(pe):
            def feature_major(out, weights, p):
                for m in range(BLOCKS):
                    cols = slice(m * P, (m + 1) * P)
                    mm = pe.matmul(out[:, cols], weights[:, cols], xc[p][:, :], start=True, stop=True)
                return mm

            def arguments(raw_parts, square_parts):
                for half in range(2):
                    cols = slice(half * GROUP, (half + 1) * GROUP)
                    split_product(pe, arg_ps[:, cols], [part[:, :] for part in omega_parts],
                                  [flat(part)[:, cols] for part in raw_parts], last=False)
                    mm = split_product(pe, arg_ps[:, cols], [part[:, :] for part in half_parts],
                                       [flat(part)[:, cols] for part in square_parts], first=False)
                return mm

            def keys(n, p):
                pe.wait_ge(x_in, 3 * n + 6)
                pe.wait_ge(kt_ready, n + 1)
                feature_major(k_ps, wk, p).then_inc(k_done, 1)

            def queries(n, p):
                pe.wait_ge(k_ready, n + 2)
                feature_major(q_ps, wq, p).then_inc(q_done, 1)

            def values(n, p):
                pe.wait_ge(q_ready, n + 2)
                project_tokens(pe, v_ps, x_parts[p], wv_parts).then_inc(v_done, 1)

            def key_arguments(n, b):
                pe.wait_ge(k_split, 2 * n + 4)
                pe.wait_ge(state_done, n + b + 1)
                arguments(k_parts, k2_parts).then_inc(k_arg_done, 1)

            def query_arguments(n):
                pe.wait_ge(q_split, 2 * n + 4)
                pe.wait_ge(phi_k_ready, n + 2)
                arguments(q_parts, q2_parts).then_inc(q_arg_done, 1)

            def turned_keys(n):
                pe.wait_ge(v_ready, n + 2)
                for m in range(BLOCKS):
                    mm = nc_t(pe, kt_ps[:, m * P:(m + 1) * P], phi_k[:, m, :], chip)
                mm.then_inc(kt_done, 1)

            def score_rounds(n, rounds):
                for s in range(PLACES):
                    for r in rounds:
                        h = head_of(r * PLACES + s)
                        mm = pe.matmul(psum[:, r % 2, s * P:(s + 1) * P], phi_k[rows_of(h), h // 2, :],
                                       phi_q[rows_of(h), h // 2, :], start=True, stop=True)
                        if s == PLACES - 1:
                            mm.then_inc(score_done, 1)

            def intra(n, r):
                pe.wait_ge(probs_done, n * R + r + 2)
                for s in range(PLACES):
                    k = r * PLACES + s
                    mm = pe.matmul(psum[:, 4 + r, s * P:(s + 1) * P], v_aug[:, head_of(k), :], probs[:, k, :],
                                   start=False, stop=(s == PLACES - 1), skip_group_check=True)
                if r == R - 1:
                    mm.then_inc(out_done, 1)

            def start():
                b, n = 0, 0
                keys(n, 0)
                queries(n, 0)
                values(n, 0)
                key_arguments(n, b)
                query_arguments(n)
                turned_keys(n)

            def chunk(b, n, p, row_end, last):
                pe.wait_ge(phi_q_ready, n + 2)
                pe.wait_ge(y_read, n + 1)
                score_rounds(n, (0, 1))
                pe.wait_ge(state_done, n + b + 2)
                pe.wait_ge(z_ready, n + 1)
                for s in range(PLACES):
                    for r in (0, 1):
                        past(r, s)
                for s in range(PLACES):
                    for r in (2, 3):
                        mm = past(r, s)
                mm.then_inc(past_done, 1)
                if not last:
                    keys(n + 1, 1 - p)
                pe.wait_ge(probs_done, n * R + 3)
                score_rounds(n, (2, 3))
                intra(n, 0)
                intra(n, 1)
                if not last:
                    queries(n + 1, 1 - p)
                intra(n, 2)
                intra(n, 3)
                pe.wait_ge(kt_ready, n + 2)
                for h in range(H):
                    mm = pe.matmul(update_ps[rows_of(h), h // 2, :], k_tok[:, h * WIDE:(h + 1) * WIDE],
                                   v_aug[:, h, :], start=True, stop=True)
                mm.then_inc(update_done, 1)
                if not last:
                    values(n + 1, 1 - p)
                    key_arguments(n + 1, b + 1)
                    pe.wait_ge(v_ready, n + 3)
                pe.wait_ge(summed, n + 2)
                for m in range(BLOCKS):
                    mm = pe.matmul(inverse_ps[:, m * P:(m + 1) * P], own_head[:, m, :], sums[:, 0, :], start=True, stop=True)
                mm.then_inc(inverse_done, 1)
                if not last:
                    query_arguments(n + 1)
                pe.wait_ge(inverse_ready, n + 2)
                if not last:
                    turned_keys(n + 1)
                    pe.wait_ge(phi_q_ready, n + 3)
                else:
                    pe.wait_ge(state_done, n + b + 3)
                pe.wait_ge(z_ready, n + 2)
                for m in range(BLOCKS):
                    mm = pe.matmul(y_ps, wo[:, m, :], z[:, m, :], start=(m == 0), stop=(m == BLOCKS - 1))
                mm.then_inc(y_done, 1)

            def past(r, s):
                h = head_of(r * PLACES + s)
                return pe.matmul(psum[:, 4 + r, s * P:(s + 1) * P], state[rows_of(h), h // 2, :], phi_q[rows_of(h), h // 2, :],
                                 start=(s == 0), stop=False, skip_group_check=True)

            rows_of_chunks(pe, start, chunk)

        @block.vector
        def _(dve):
            def take_k(n):
                dve.wait_ge(k_done, n + 2)
                dve.wait_ge(k_squares, n + 1)
                dve.wait_ge(k_split, 2 * n + 2)
                dve.tensor_copy(flat(kT), k_ps).then_inc(k_ready, 1)

            def take_rest(n, ready, high, split, wholes, parts):
                for j, (whole, (rounded, rest)) in enumerate(zip(wholes, parts)):
                    dve.wait_ge(high, 2 * n + 3 + j)
                    dve.tensor_tensor(flat(rest), flat(whole), flat(rounded).bitcast(F32), ALU.subtract).then_inc(split, 1)

            def rest_of_k(n):
                take_rest(n, k_ready, k_high, k_split, (kT, k2), (k_parts, k2_parts))

            def rest_of_q(n):
                take_rest(n, q_ready, q_high, q_split, (qT, q2), (q_parts, q2_parts))

            def take_kt(n):
                dve.wait_ge(kt_done, n + 2)
                dve.wait_ge(update_done, n + 1)
                dve.tensor_copy(k_tok[:, :], kt_ps).then_inc(kt_ready, 1)

            def take_scores(n, r):
                dve.wait_ge(score_done, n * R + r + 2)
                dve.wait_ge(out_done, n + 1)
                heads = slice(r * PLACES, (r + 1) * PLACES)
                dve.scalar_tensor_tensor(probs[:, heads, :], psum[:, r % 2, :].rearrange("p (s i) -> p s i", i=P), FINITE,
                                         allowed[:, :].unsqueeze(1).to_broadcast([P, PLACES, P]), ALU.min,
                                         ALU.mult).then_inc(probs_done, 1)

            def clear_state(steps):
                dve.wait_ge(state_done, steps)
                dve.memset(state[:, :, :], 0.0).then_inc(state_done, 1)

            def start():
                b, n = 0, 0
                clear_state(1)
                take_k(n)
                rest_of_k(n)
                rest_of_q(n)
                take_kt(n)

            def chunk(b, n, p, row_end, last):
                take_scores(n, 0)
                take_scores(n, 1)
                if not last:
                    take_k(n + 1)
                take_scores(n, 2)
                take_scores(n, 3)
                if not last:
                    rest_of_k(n + 1)
                dve.wait_ge(out_done, n + 2)
                dve.wait_ge(inverse_done, n + 1)
                for odd in range(2):
                    group = slice(0, H) if odd else slice(WIDE, WIDE + H)
                    dve.tensor_reduce(sums[:, odd, :], out_ps[group, odd, :, :].rearrange("p a (s i) -> p i a s", i=P),
                                      mybir.AxisListType.XY, ALU.add).then_inc(sum_steps, 1)
                dve.wait_ge(update_done, n + 2)
                dve.wait_ge(past_done, n + 2)
                dve.wait_ge(state_done, n + b + 2)
                dve.tensor_tensor(state[:, :, :], state[:, :, :], update_ps, ALU.add).then_inc(state_done, 1)
                if row_end and not last:
                    clear_state(n + b + 3)
                dve.wait_ge(sum_steps, 3 * n + 2)
                dve.scalar_tensor_tensor(sums[:, 0, :], sums[:, 0, :], WIDE * 1e-6, sums[:, 1, :], ALU.add,
                                         ALU.add).then_inc(sum_steps, 1)
                dve.wait_ge(sum_steps, 3 * n + 3)
                dve.reciprocal(sums[:, 0, :], sums[:, 0, :]).then_inc(summed, 1)
                if not last:
                    rest_of_q(n + 1)
                dve.wait_ge(inverse_ready, n + 2)
                dve.wait_ge(y_done, n + 1)
                for odd in range(2):
                    rows = slice(odd * WIDE, odd * WIDE + WIDE)
                    mult = dve.tensor_tensor(flat(z)[rows, :].rearrange("p (a f) -> p a f", a=2), out_ps[rows, odd, :, :],
                                             flat(inverse)[rows, :].rearrange("p (a f) -> p a f", a=2), ALU.mult)
                mult.then_inc(z_ready, 1)
                if not last:
                    take_kt(n + 1)

            rows_of_chunks(dve, start, chunk)

        @block.scalar
        def _(act):
            def take_q(n):
                act.wait_ge(q_done, n + 2)
                act.wait_ge(q_squares, n + 1)
                act.wait_ge(q_split, 2 * n + 2)
                act.copy(flat(qT), two(2)).then_inc(q_ready, 1)

            def round_off(n, ready, squares, read, high, wholes, parts):
                act.wait_ge(read, n + 1)
                act.wait_ge(ready, n + 2)
                act.copy(flat(parts[0][0]), flat(wholes[0])).then_inc(high, 1)
                act.wait_ge(squares, n + 2)
                act.copy(flat(parts[1][0]), flat(wholes[1])).then_inc(high, 1)

            def round_k(n):
                round_off(n, k_ready, k_squares, k_arg_done, k_high, (kT, k2), (k_parts, k2_parts))

            def round_q(n):
                round_off(n, q_ready, q_squares, q_arg_done, q_high, (qT, q2), (q_parts, q2_parts))

            def take_v(n):
                act.wait_ge(v_done, n + 2)
                act.wait_ge(update_done, n + 1)
                for odd in range(2):
                    copy = act.copy(v_aug[:, :, :].rearrange("p (m two) f -> p m two f", two=2)[:, :, odd, odd * WIDE:(odd + 1) * WIDE],
                                    v_ps.rearrange("p (m two e) -> p m two e", two=2, e=WIDE)[:, :, odd, :])
                copy.then_inc(v_ready, 1)

            def take_phi_k(n):
                act.wait_ge(k_arg_done, n + 2)
                act.wait_ge(score_done, n * R + 1)
                act.wait_ge(kt_done, n + 1)
                act.activation(flat(phi_k), arg_ps, ACT.Exp).then_inc(phi_k_ready, 1)

            def take_phi_q(n):
                act.wait_ge(q_arg_done, n + 2)
                act.wait_ge(past_done, n + 1)
                act.wait_ge(score_done, n * R + 1)
                act.activation(flat(phi_q), arg_ps, ACT.Exp).then_inc(phi_q_ready, 1)

            def start():
                b, n = 0, 0
                round_k(n)
                take_q(n)
                round_q(n)
                take_v(n)
                take_phi_k(n)
                take_phi_q(n)

            def chunk(b, n, p, row_end, last):
                if not last:
                    round_k(n + 1)
                    take_q(n + 1)
                    round_q(n + 1)
                    take_v(n + 1)
                    take_phi_k(n + 1)
                act.wait_ge(inverse_done, n + 2)
                act.wait_ge(z_ready, n + 1)
                act.copy(flat(inverse), inverse_ps).then_inc(inverse_ready, 1)
                if not last:
                    take_phi_q(n + 1)
                act.wait_ge(y_done, n + 2)
                act.activation(chip.yT[:, bass.ts(n, P)], y_ps, ACT.Identity, bias=bo[:, 0:1]).then_inc(y_read, 1)

            rows_of_chunks(act, start, chunk)


def program(nc, dram, out, layers=None):
    with ExitStack() as ctx:
        chip = Chip(nc, dram, out, ctx)
        load_stage(chip)
        steps = [
            lambda norm: ffn_stage(chip, "ffn_a", norm), lambda norm: retention_attention(chip, norm),
            lambda norm: ffn_stage(chip, "ffn_b", norm),
            lambda norm: moe1(chip, "moe1_a", norm), lambda norm: window_attention(chip, norm),
            lambda norm: moe1(chip, "moe1_b", norm),
            lambda norm: moe2(chip, "moe2_a", norm), lambda norm: gated_attention(chip, norm),
            lambda norm: moe2(chip, "moe2_b", norm),
            lambda norm: choice(chip, "moe3_a", norm), lambda norm: feature_attention(chip, norm),
            lambda norm: choice(chip, "moe3_b", norm),
        ]
        scale = None
        for n, step in enumerate(steps):
            if layers is not None and n not in layers:
                continue
            step(lambda loads, n=n, scale=scale: norm_stage(chip, f"norm{n}", scale, loads))
            scale = 1.0 if n % 3 == 1 else 0.5
        store_stage(chip, scale)


def moe1(chip, name, norm):
    experts_stage(chip, name, norm, "sum", "moe1_router", 512, True, ("moe1_gate", "moe1_up"), "moe1_down")


def moe2(chip, name, norm):
    experts_stage(chip, name, norm, "softmax", "moe2_router", 256, True, ("moe2_gate", "moe2_up"), "moe2_down")


def choice(chip, name, norm):
    experts_stage(chip, name, norm, "choice", "moe3_router", 512, False, ("moe3_up",), "moe3_down")


def _arrays(i):
    import numpy as np

    f = np.float32

    def chunked(w):
        return np.swapaxes(w.reshape(*w.shape[:-2], -1, P, w.shape[-1]), -3, -2)

    def column(v):
        return v.reshape(-1, P).T

    head = np.arange(D) // DH0
    gamma = 1.0 - 2.0 ** (-5.0 - np.arange(H))
    pos = np.arange(P)
    ahead = pos[None, :] - pos[:, None]
    root = np.sqrt(DH0)
    decay = np.where(ahead >= 0, gamma[:, None, None] ** np.maximum(ahead, 0), 0.0) / root
    same_head = (head[:, None] == head[None, :]).astype(f)
    start = 2.0 ** -(2.0 ** -(np.log2(H) - 3))
    slopes = np.array([start * start ** h for h in range(H)])
    FAR = -1e30
    back = pos[:, None] - pos[None, :]
    slope = np.stack([np.where(back >= 0, -back * slopes[:, None, None], FAR),
                      np.where(back < 0, -(back + P) * slopes[:, None, None], FAR)])
    slope = slope.reshape(2, ROWS, SLOTS, P, P).transpose(3, 1, 0, 2, 4).reshape(P, -1)
    upto = (ahead >= 0).astype(f)
    two = np.kron(np.eye(2, dtype=f), np.ones((WIDE, WIDE), f))
    omega = np.zeros((P, P), f)
    for k in range(2):
        omega[k * WIDE:(k + 1) * WIDE, k * WIDE:(k + 1) * WIDE] = i["L3_attn_omega"].T
    own_head = np.kron(np.eye(H, dtype=f), np.ones((1, WIDE), f)).reshape(H, BLOCKS, P)
    v_fill = np.zeros((H, P), f)
    for h in range(H):
        v_fill[h, (0 if h % 2 else WIDE) + h] = 1.0
    return {
        "fea_wq": i["L3_attn_wq"].T, "fea_wk": i["L3_attn_wk"].T, "fea_wv": i["L3_attn_wv"].T, "fea_wo": chunked(i["L3_attn_wo"].T), "own_head": own_head, "v_fill": np.tile(v_fill, (P, 1, 1)),
        "fea_bo": column(i["L3_attn_bo"]), "fea_omega": omega, "fea_half_norm": f(-0.5) * two, "allowed": upto,
        "gla_wd": i["L2_attn_Wd"].T, "gla_bd": np.tile(i["L2_attn_bd"], (P, 1)),
        "gla_sums": np.stack([upto, 1 - upto, np.ones_like(upto)], 1),
        "gla_wk": i["L2_attn_Wk"].T, "gla_wg": i["L2_attn_Wg"].T, "gla_wv": i["L2_attn_Wv"].T, "gla_wog": i["L2_attn_Wog"].T,
        "gla_wq": i["L2_attn_Wq"].T, "gla_wo": chunked(i["L2_attn_Wo"].T), "gla_norm_w": column(i["L2_attn_norm_w"]),
        "causal": np.where(ahead >= 0, 0.0, FAR).astype(f),
        "win_slope": slope.astype(f),
        "win_wq": i["L1_attn_wq"].T, "win_wk": i["L1_attn_wk"].T, "win_wv": i["L1_attn_wv"].T, "win_wo": i["L1_attn_wo"].T,
        "win_bias_qk": np.stack([i["L1_attn_bq"], i["L1_attn_bk"]], 1), "win_bias_v": np.tile(i["L1_attn_bv"], (P, 1)),
        "win_bo": column(i["L1_attn_bo"]),
        "same_head": same_head, "head_mean": same_head / f(DH0),
        "slot": (head[:, None] % SLOTS == np.arange(SLOTS)).astype(f),
        "slot_cols": np.tile((head[None, :] % SLOTS == np.arange(SLOTS)[:, None]).astype(f), (P, 1, 1)),
        "ret_decay": decay.transpose(1, 0, 2).astype(f),
        "ret_q_decay": (gamma[head][:, None] ** (pos + 1) / root).astype(f),
        "ret_k_decay": (gamma[head][None, :] ** (P - 1 - pos[:, None])).astype(f),
        "ret_chunk_decay": (gamma[head][:, None] ** P).astype(f),
        "ret_wq": i["L0_attn_W_q"].T, "ret_wk": i["L0_attn_W_k"].T, "ret_wv": i["L0_attn_W_v"].T, "ret_wo": i["L0_attn_W_o"].T,
        "ret_affine": np.stack([i["L0_attn_gn_weight"], i["L0_attn_gn_bias"]], 1),
        "x": i["L0_attn_x"],
        "ident": np.eye(P, dtype=f),
        "descending": np.tile(np.arange(E, 0, -1).astype(f), (P, 1)),
        "place": np.tile(np.array([2.0 ** (3 * (ROUNDS - 1 - n)) for n in range(ROUNDS)], f), (P, 1)),
        "trials": np.array([[r << 3 * (ROUNDS - 1 - n) for n in range(ROUNDS)] for r in range(TRIAL_COUNT)
                            for _ in range(B * E)], np.int32),
        "same_row": np.array([[i // (B * E) > 0 and (i - j) % (B * E) == 0 for j in range(P)] for i in range(P)], f),
        "ffn_w1": i["L0_ffn_W1"], "ffn_b1": column(i["L0_ffn_b1"]), "ffn_w2": chunked(i["L0_ffn_W2"]), "ffn_b2": column(i["L0_ffn_b2"]),
        "moe1_router": i["L1_ffn_Wr"], "moe1_gate": i["L1_ffn_Wg"], "moe1_up": i["L1_ffn_Wu"], "moe1_down": chunked(i["L1_ffn_Wd"]),
        "moe2_router": i["L2_ffn_router_kernel_DE"], "moe2_gate": i["L2_ffn_kernel_gating_EDF"],
        "moe2_up": i["L2_ffn_kernel_up_EDF"], "moe2_down": chunked(i["L2_ffn_kernel_down_EFD"]),
        "moe3_router": i["L3_ffn_gate_w"].T, "moe3_up": i["L3_ffn_w1"], "moe3_down": chunked(i["L3_ffn_w2"]),
    }


def kernel(**inputs):
    import numpy as np
    import concourse.bacc as bacc
    from concourse.bass_utils import run_bass_kernel_spmd

    nc = bacc.Bacc("TRN2", target_bir_lowering=False, num_devices=1)
    arrays, dram = {}, {}
    for name, a in _arrays({k: np.asarray(v) for k, v in inputs.items()}).items():
        arrays["in_" + name] = np.ascontiguousarray(a)
        dram[name] = nc.dram_tensor("in_" + name, a.shape, mybir.dt.from_np(a.dtype), kind="ExternalInput").ap()
    out = nc.dram_tensor("out_x", (B, T, D), F32, kind="ExternalOutput").ap()
    program(nc, dram, out)
    r = run_bass_kernel_spmd(nc, [arrays], core_ids=[0])
    return r.results[0]["out_x"]
```
